# Optimizing a Trainium2 kernel written in Bass

```python
import numpy as np
import jax
import jax.numpy as jnp

def _softmax(x, axis=-1):
    return jax.nn.softmax(x, axis=axis)

def _gelu(x):
    return jax.nn.gelu(x, approximate=True)

def _silu(x):
    return jax.nn.silu(x)

def _sigmoid(x):
    return jax.nn.sigmoid(x)

def _layernorm(x, axis=-1, eps=1e-05):
    m = jnp.mean(x, axis=axis, keepdims=True)
    v = jnp.var(x, axis=axis, keepdims=True)
    return (x - m) / jnp.sqrt(v + eps)

def _scatter_add(tgt, idx, src, axis=0):
    return tgt.at[idx].add(src)

def _segment_sum(src, seg, n):
    return jax.ops.segment_sum(src, seg, n)
kernel_name = 'mk_recurrent_d2_jaxref_r8_a1a90c'

def setup_inputs(seed: int=0):
    np.random.seed(seed)
    _w = jnp.asarray

    def _L0_attn_setup():
        import jax, jax.numpy as jnp
        import numpy as np
        B, L, D, H, W = (2, 512, 128, 16, 128)
        E = D // H

        def _ln(x, g, b):
            m = jnp.mean(x, axis=-1, keepdims=True)
            v = jnp.mean((x - m) ** 2, axis=-1, keepdims=True)
            return (x - m) / jnp.sqrt(v + 1e-05) * g + b

        def _swa(xn, Wqkv, bqkv, Wp, bp):
            b_, l_, d_ = xn.shape
            nb = l_ // W
            qkv = xn @ Wqkv + bqkv
            q, k, v = jnp.split(qkv, 3, axis=-1)

            def heads(t):
                return t.reshape(b_, l_, H, E).transpose(0, 2, 1, 3)
            q, k, v = (heads(q), heads(k), heads(v))

            def blk(t):
                return t.reshape(b_, H, nb, W, E)
            qb, kb, vb = (blk(q), blk(k), blk(v))
            kprev = jnp.pad(kb, ((0, 0), (0, 0), (1, 0), (0, 0), (0, 0)))[:, :, :nb]
            vprev = jnp.pad(vb, ((0, 0), (0, 0), (1, 0), (0, 0), (0, 0)))[:, :, :nb]
            kc = jnp.concatenate([kprev, kb], axis=3)
            vc = jnp.concatenate([vprev, vb], axis=3)
            scores = jnp.einsum('bhnre,bhnse->bhnrs', qb, kc) / np.float32(np.sqrt(E))
            r = jnp.arange(W)[:, None]
            s = jnp.arange(2 * W)[None, :]
            band = (s >= r + 1) & (s <= r + W)
            first = band & (s >= W)
            mask = jnp.concatenate([first[None], jnp.broadcast_to(band, (nb - 1, W, 2 * W))], axis=0)
            scores = jnp.where(mask[None, None], scores, jnp.float32(-1e+30))
            attn = jax.nn.softmax(scores, axis=-1)
            out = jnp.einsum('bhnrs,bhnse->bhnre', attn, vc)
            out = out.reshape(b_, H, l_, E).transpose(0, 2, 1, 3).reshape(b_, l_, d_)
            return out @ Wp + bp

        def _linattn(xn, Wqkv, bqkv, Wo, bo):
            b_, l_, d_ = xn.shape
            C = 128
            nc = l_ // C
            qkv = xn @ Wqkv + bqkv
            q, k, v = jnp.split(qkv, 3, axis=-1)
            q = q.reshape(b_, l_, H, E)
            k = k.reshape(b_, l_, H, E)
            v = v.reshape(b_, l_, H, E)
            q = jax.nn.elu(q * np.float32(E ** (-0.5))) + np.float32(1.0001)
            k = jax.nn.elu(k) + np.float32(1.0001)

            def chunks(t):
                return t.reshape(b_, nc, C, H, E).transpose(1, 0, 3, 2, 4)
            qc, kc, vc = (chunks(q), chunks(k), chunks(v))
            tril = jnp.tril(jnp.ones((C, C), jnp.float32))

            def step(carry, inp):
                S, z = carry
                qi, ki, vi = inp
                A = jnp.einsum('bhce,bhde->bhcd', qi, ki) * tril
                num = jnp.einsum('bhce,bhef->bhcf', qi, S) + jnp.einsum('bhcd,bhdf->bhcf', A, vi)
                den = jnp.einsum('bhce,bhe->bhc', qi, z) + A.sum(-1)
                o = num / (den[..., None] + 1e-06)
                S = S + jnp.einsum('bhce,bhcf->bhef', ki, vi)
                z = z + ki.sum(2)
                return ((S, z), o)
            S0 = jnp.zeros((b_, H, E, E), jnp.float32)
            z0 = jnp.zeros((b_, H, E), jnp.float32)
            _, out = jax.lax.scan(step, (S0, z0), (qc, kc, vc))
            out = out.transpose(1, 0, 3, 2, 4).reshape(b_, l_, d_)
            return out @ Wo + bo
        key = jax.random.key(seed)
        ks = jax.random.split(key, 9)

        def w(k, shape, s=0.02):
            return jax.random.normal(k, shape, jnp.float32) * s
        return {'x': jax.random.normal(ks[0], (B, L, D), jnp.float32), 'g1': jnp.ones((D,), jnp.float32), 'b1': jnp.zeros((D,), jnp.float32), 'Wqkv_a': w(ks[1], (D, 3 * D)), 'bqkv_a': jnp.zeros((3 * D,), jnp.float32), 'Wp_a': w(ks[2], (D, D)), 'bp_a': jnp.zeros((D,), jnp.float32), 'Wqkv_s': w(ks[3], (D, 3 * D)), 'bqkv_s': jnp.zeros((3 * D,), jnp.float32), 'Wo_s': w(ks[4], (D, D)), 'bo_s': jnp.zeros((D,), jnp.float32), 'Wo': w(ks[5], (D, D)), 'bo': jnp.zeros((D,), jnp.float32), 'gm': jnp.ones((D,), jnp.float32), 'bm': jnp.zeros((D,), jnp.float32), 'W1': w(ks[6], (D, 4 * D)), 'b1m': jnp.zeros((4 * D,), jnp.float32), 'W2': w(ks[7], (4 * D, D)), 'b2m': jnp.zeros((D,), jnp.float32)}
    _L0_attn_in = _L0_attn_setup()

    def _L0_ffn_setup():
        import jax, jax.numpy as jnp
        import numpy as np
        EPS = 1e-06
        LN_EPS = 1e-05

        def _absmean_core(W):
            gamma = jnp.mean(jnp.abs(W)) + EPS
            Ws = W / gamma
            Wq = jnp.sign(Ws) * jnp.minimum(jnp.round(jnp.abs(Ws)), 1.0)
            return (Wq, gamma)

        @jax.custom_vjp
        def absmean(W):
            return _absmean_core(W)[0]

        def _absmean_fwd(W):
            Wq, gamma = _absmean_core(W)
            return (Wq, gamma)

        def _absmean_bwd(gamma, g):
            return (g / gamma,)
        absmean.defvjp(_absmean_fwd, _absmean_bwd)

        def layernorm(x, w, b, eps=LN_EPS):
            mu = jnp.mean(x, axis=-1, keepdims=True)
            var = jnp.mean((x - mu) ** 2, axis=-1, keepdims=True)
            return (x - mu) * jax.lax.rsqrt(var + eps) * w + b
        key = jax.random.key(seed)
        k1, k2, k3 = jax.random.split(key, 3)
        d, h = (128, 512)
        B, T = (8, 256)
        return {'x': jax.random.normal(k1, (B, T, d), jnp.float32), 'W_fc': jax.random.normal(k2, (h, d), jnp.float32), 'ln_w': jnp.ones((h,), jnp.float32), 'ln_b': jnp.zeros((h,), jnp.float32), 'W_proj': jax.random.normal(k3, (d, h), jnp.float32)}
    _L0_ffn_in = _L0_ffn_setup()

    def _L1_attn_setup():
        import jax, jax.numpy as jnp
        import numpy as np
        N_HEADS = 16
        HEAD_DIM = 64
        HIDDEN = 128
        key = jax.random.key(seed)
        kx, kq, kk, kv, ko = jax.random.split(key, 5)
        B, S = (1, 512)
        lim = float(np.sqrt(6.0 / (HIDDEN + N_HEADS * HEAD_DIM)))
        x = jax.random.normal(kx, (B, S, HIDDEN), dtype=jnp.float32)
        wq = jax.random.uniform(kq, (N_HEADS * HEAD_DIM, HIDDEN), jnp.float32, -lim, lim)
        wk = jax.random.uniform(kk, (N_HEADS * HEAD_DIM, HIDDEN), jnp.float32, -lim, lim)
        wv = jax.random.uniform(kv, (N_HEADS * HEAD_DIM, HIDDEN), jnp.float32, -lim, lim)
        wo = jax.random.uniform(ko, (HIDDEN, N_HEADS * HEAD_DIM), jnp.float32, -lim, lim)
        return {'x': x, 'wq': wq, 'wk': wk, 'wv': wv, 'wo': wo}
    _L1_attn_in = _L1_attn_setup()

    def _L1_ffn_setup():
        import jax, jax.numpy as jnp
        import numpy as np
        BLOCK = 16
        _GRID = jnp.array([0.0, 0.5, 1.0, 1.5, 2.0, 3.0, 4.0, 6.0], dtype=jnp.float32)
        _MID = jnp.array([0.25, 0.75, 1.25, 1.75, 2.5, 3.5, 5.0], dtype=jnp.float32)

        def fp4_quant_dequant(x):
            shape = x.shape
            xb = x.reshape(shape[:-1] + (shape[-1] // BLOCK, BLOCK))
            scale = jnp.max(jnp.abs(xb), axis=-1, keepdims=True) / 6.0
            scale = jnp.maximum(scale, jnp.float32(1e-12))
            xn = xb / scale
            idx = jnp.searchsorted(_MID, jnp.abs(xn))
            q = _GRID[idx] * jnp.sign(xn) * scale
            return q.reshape(shape)

        def fp4_linear(x, w):
            xq = fp4_quant_dequant(x)
            wq = fp4_quant_dequant(w)
            return jnp.einsum('bsk,nk->bsn', xq, wq)
        key = jax.random.key(seed)
        k1, k2, k3, k4 = jax.random.split(key, 4)
        H, I = (128, 352)
        x = jax.random.normal(k1, (4, 512, H), dtype=jnp.float32)
        w_gate = jax.random.normal(k2, (I, H), dtype=jnp.float32) * 0.02
        w_up = jax.random.normal(k3, (I, H), dtype=jnp.float32) * 0.02
        w_down = jax.random.normal(k4, (H, I), dtype=jnp.float32) * 0.02
        return {'x': x, 'w_gate': w_gate, 'w_up': w_up, 'w_down': w_down}
    _L1_ffn_in = _L1_ffn_setup()
    _d = {'L0_attn_x': _L0_attn_in['x'], 'L0_attn_g1': _L0_attn_in['g1'], 'L0_attn_b1': _L0_attn_in['b1'], 'L0_attn_Wqkv_a': _L0_attn_in['Wqkv_a'], 'L0_attn_bqkv_a': _L0_attn_in['bqkv_a'], 'L0_attn_Wp_a': _L0_attn_in['Wp_a'], 'L0_attn_bp_a': _L0_attn_in['bp_a'], 'L0_attn_Wqkv_s': _L0_attn_in['Wqkv_s'], 'L0_attn_bqkv_s': _L0_attn_in['bqkv_s'], 'L0_attn_Wo_s': _L0_attn_in['Wo_s'], 'L0_attn_bo_s': _L0_attn_in['bo_s'], 'L0_attn_Wo': _L0_attn_in['Wo'], 'L0_attn_bo': _L0_attn_in['bo'], 'L0_attn_gm': _L0_attn_in['gm'], 'L0_attn_bm': _L0_attn_in['bm'], 'L0_attn_W1': _L0_attn_in['W1'], 'L0_attn_b1m': _L0_attn_in['b1m'], 'L0_attn_W2': _L0_attn_in['W2'], 'L0_attn_b2m': _L0_attn_in['b2m'], 'L0_ffn_W_fc': _L0_ffn_in['W_fc'], 'L0_ffn_ln_w': _L0_ffn_in['ln_w'], 'L0_ffn_ln_b': _L0_ffn_in['ln_b'], 'L0_ffn_W_proj': _L0_ffn_in['W_proj'], 'L1_attn_wq': _L1_attn_in['wq'], 'L1_attn_wk': _L1_attn_in['wk'], 'L1_attn_wv': _L1_attn_in['wv'], 'L1_attn_wo': _L1_attn_in['wo'], 'L1_ffn_w_gate': _L1_ffn_in['w_gate'], 'L1_ffn_w_up': _L1_ffn_in['w_up'], 'L1_ffn_w_down': _L1_ffn_in['w_down']}
    _x0 = _d['L0_attn_x']
    _d['L0_attn_x'] = jax.random.normal(jax.random.fold_in(jax.random.key(seed), 1), (4, 1024, 128), dtype=_x0.dtype)
    del _x0
    return _d

def reference(L0_attn_x, L0_attn_g1, L0_attn_b1, L0_attn_Wqkv_a, L0_attn_bqkv_a, L0_attn_Wp_a, L0_attn_bp_a, L0_attn_Wqkv_s, L0_attn_bqkv_s, L0_attn_Wo_s, L0_attn_bo_s, L0_attn_Wo, L0_attn_bo, L0_attn_gm, L0_attn_bm, L0_attn_W1, L0_attn_b1m, L0_attn_W2, L0_attn_b2m, L0_ffn_W_fc, L0_ffn_ln_w, L0_ffn_ln_b, L0_ffn_W_proj, L1_attn_wq, L1_attn_wk, L1_attn_wv, L1_attn_wo, L1_ffn_w_gate, L1_ffn_w_up, L1_ffn_w_down):

    def _L0_attn_ref(x, g1, b1, Wqkv_a, bqkv_a, Wp_a, bp_a, Wqkv_s, bqkv_s, Wo_s, bo_s, Wo, bo, gm, bm, W1, b1m, W2, b2m):
        import jax, jax.numpy as jnp
        import numpy as np
        B, L, D, H, W = (2, 512, 128, 16, 128)
        E = D // H

        def _ln(x, g, b):
            m = jnp.mean(x, axis=-1, keepdims=True)
            v = jnp.mean((x - m) ** 2, axis=-1, keepdims=True)
            return (x - m) / jnp.sqrt(v + 1e-05) * g + b

        def _swa(xn, Wqkv, bqkv, Wp, bp):
            b_, l_, d_ = xn.shape
            nb = l_ // W
            qkv = xn @ Wqkv + bqkv
            q, k, v = jnp.split(qkv, 3, axis=-1)

            def heads(t):
                return t.reshape(b_, l_, H, E).transpose(0, 2, 1, 3)
            q, k, v = (heads(q), heads(k), heads(v))

            def blk(t):
                return t.reshape(b_, H, nb, W, E)
            qb, kb, vb = (blk(q), blk(k), blk(v))
            kprev = jnp.pad(kb, ((0, 0), (0, 0), (1, 0), (0, 0), (0, 0)))[:, :, :nb]
            vprev = jnp.pad(vb, ((0, 0), (0, 0), (1, 0), (0, 0), (0, 0)))[:, :, :nb]
            kc = jnp.concatenate([kprev, kb], axis=3)
            vc = jnp.concatenate([vprev, vb], axis=3)
            scores = jnp.einsum('bhnre,bhnse->bhnrs', qb, kc) / np.float32(np.sqrt(E))
            r = jnp.arange(W)[:, None]
            s = jnp.arange(2 * W)[None, :]
            band = (s >= r + 1) & (s <= r + W)
            first = band & (s >= W)
            mask = jnp.concatenate([first[None], jnp.broadcast_to(band, (nb - 1, W, 2 * W))], axis=0)
            scores = jnp.where(mask[None, None], scores, jnp.float32(-1e+30))
            attn = jax.nn.softmax(scores, axis=-1)
            out = jnp.einsum('bhnrs,bhnse->bhnre', attn, vc)
            out = out.reshape(b_, H, l_, E).transpose(0, 2, 1, 3).reshape(b_, l_, d_)
            return out @ Wp + bp

        def _linattn(xn, Wqkv, bqkv, Wo, bo):
            b_, l_, d_ = xn.shape
            C = 128
            nc = l_ // C
            qkv = xn @ Wqkv + bqkv
            q, k, v = jnp.split(qkv, 3, axis=-1)
            q = q.reshape(b_, l_, H, E)
            k = k.reshape(b_, l_, H, E)
            v = v.reshape(b_, l_, H, E)
            q = jax.nn.elu(q * np.float32(E ** (-0.5))) + np.float32(1.0001)
            k = jax.nn.elu(k) + np.float32(1.0001)

            def chunks(t):
                return t.reshape(b_, nc, C, H, E).transpose(1, 0, 3, 2, 4)
            qc, kc, vc = (chunks(q), chunks(k), chunks(v))
            tril = jnp.tril(jnp.ones((C, C), jnp.float32))

            def step(carry, inp):
                S, z = carry
                qi, ki, vi = inp
                A = jnp.einsum('bhce,bhde->bhcd', qi, ki) * tril
                num = jnp.einsum('bhce,bhef->bhcf', qi, S) + jnp.einsum('bhcd,bhdf->bhcf', A, vi)
                den = jnp.einsum('bhce,bhe->bhc', qi, z) + A.sum(-1)
                o = num / (den[..., None] + 1e-06)
                S = S + jnp.einsum('bhce,bhcf->bhef', ki, vi)
                z = z + ki.sum(2)
                return ((S, z), o)
            S0 = jnp.zeros((b_, H, E, E), jnp.float32)
            z0 = jnp.zeros((b_, H, E), jnp.float32)
            _, out = jax.lax.scan(step, (S0, z0), (qc, kc, vc))
            out = out.transpose(1, 0, 3, 2, 4).reshape(b_, l_, d_)
            return out @ Wo + bo
        xn = _ln(x, g1, b1)
        attn_out = _swa(xn, Wqkv_a, bqkv_a, Wp_a, bp_a)
        ssm_out = _linattn(xn, Wqkv_s, bqkv_s, Wo_s, bo_s)
        mixed = (attn_out + ssm_out) @ Wo + bo
        x1 = x + mixed
        h = _ln(x1, gm, bm)
        mlp = jax.nn.gelu(h @ W1 + b1m, approximate=False) @ W2 + b2m
        return x1 + mlp

    def _L0_ffn_ref(x, W_fc, ln_w, ln_b, W_proj):
        import jax, jax.numpy as jnp
        import numpy as np
        EPS = 1e-06
        LN_EPS = 1e-05

        def _absmean_core(W):
            gamma = jnp.mean(jnp.abs(W)) + EPS
            Ws = W / gamma
            Wq = jnp.sign(Ws) * jnp.minimum(jnp.round(jnp.abs(Ws)), 1.0)
            return (Wq, gamma)

        @jax.custom_vjp
        def absmean(W):
            return _absmean_core(W)[0]

        def _absmean_fwd(W):
            Wq, gamma = _absmean_core(W)
            return (Wq, gamma)

        def _absmean_bwd(gamma, g):
            return (g / gamma,)
        absmean.defvjp(_absmean_fwd, _absmean_bwd)

        def layernorm(x, w, b, eps=LN_EPS):
            mu = jnp.mean(x, axis=-1, keepdims=True)
            var = jnp.mean((x - mu) ** 2, axis=-1, keepdims=True)
            return (x - mu) * jax.lax.rsqrt(var + eps) * w + b
        h = jnp.einsum('btd,hd->bth', x, absmean(W_fc))
        h = jax.nn.gelu(h, approximate=False)
        h = layernorm(h, ln_w, ln_b)
        return jnp.einsum('bth,dh->btd', h, absmean(W_proj))

    def _L1_attn_ref(x, wq, wk, wv, wo):
        import jax, jax.numpy as jnp
        import numpy as np
        N_HEADS = 16
        HEAD_DIM = 64
        HIDDEN = 128
        B, S, _ = x.shape
        scale = HEAD_DIM ** (-0.5)

        def proj(w):
            return jnp.einsum('bsh,eh->bse', x, w).reshape(B, S, N_HEADS, HEAD_DIM).transpose(0, 2, 1, 3)
        q, k, v = (proj(wq), proj(wk), proj(wv))
        scores = jnp.einsum('bhqd,bhkd->bhqk', q, k) * scale
        causal = jnp.tril(jnp.ones((S, S), dtype=bool))
        scores = jnp.where(causal, scores, -jnp.inf)
        probs = jax.nn.softmax(scores, axis=-1)
        out = jnp.einsum('bhqk,bhkd->bhqd', probs, v)
        out = out.transpose(0, 2, 1, 3).reshape(B, S, N_HEADS * HEAD_DIM)
        return jnp.einsum('bse,he->bsh', out, wo)

    def _L1_ffn_ref(x, w_gate, w_up, w_down):
        import jax, jax.numpy as jnp
        import numpy as np
        BLOCK = 16
        _GRID = jnp.array([0.0, 0.5, 1.0, 1.5, 2.0, 3.0, 4.0, 6.0], dtype=jnp.float32)
        _MID = jnp.array([0.25, 0.75, 1.25, 1.75, 2.5, 3.5, 5.0], dtype=jnp.float32)

        def fp4_quant_dequant(x):
            shape = x.shape
            xb = x.reshape(shape[:-1] + (shape[-1] // BLOCK, BLOCK))
            scale = jnp.max(jnp.abs(xb), axis=-1, keepdims=True) / 6.0
            scale = jnp.maximum(scale, jnp.float32(1e-12))
            xn = xb / scale
            idx = jnp.searchsorted(_MID, jnp.abs(xn))
            q = _GRID[idx] * jnp.sign(xn) * scale
            return q.reshape(shape)

        def fp4_linear(x, w):
            xq = fp4_quant_dequant(x)
            wq = fp4_quant_dequant(w)
            return jnp.einsum('bsk,nk->bsn', xq, wq)
        gate = fp4_linear(x, w_gate)
        y = fp4_linear(x, w_up)
        h = jax.nn.silu(gate) * y
        return fp4_linear(h, w_down)
    x = L0_attn_x
    xn = _layernorm(x, axis=-1)
    s = _L0_attn_ref(xn, L0_attn_g1, L0_attn_b1, L0_attn_Wqkv_a, L0_attn_bqkv_a, L0_attn_Wp_a, L0_attn_bp_a, L0_attn_Wqkv_s, L0_attn_bqkv_s, L0_attn_Wo_s, L0_attn_bo_s, L0_attn_Wo, L0_attn_bo, L0_attn_gm, L0_attn_bm, L0_attn_W1, L0_attn_b1m, L0_attn_W2, L0_attn_b2m)
    g = _silu(_L0_ffn_ref(xn, L0_ffn_W_fc, L0_ffn_ln_w, L0_ffn_ln_b, L0_ffn_W_proj))
    x = x + s * g
    xn = _layernorm(x, axis=-1)
    s = _L1_attn_ref(xn, L1_attn_wq, L1_attn_wk, L1_attn_wv, L1_attn_wo)
    g = _silu(_L1_ffn_ref(xn, L1_ffn_w_gate, L1_ffn_w_up, L1_ffn_w_down))
    x = x + s * g
    return x

_drawn_inputs = setup_inputs


def setup_inputs(seed=0):
    import zlib

    import numpy as np

    out = dict(_drawn_inputs(seed))
    spreads = {'L0_attn_g1': (1.0, 0.6),
     'L0_attn_b1': (0.0, 0.8),
     'L0_attn_bqkv_a': (0.0, 0.8),
     'L0_attn_bp_a': (0.0, 0.374),
     'L0_attn_bqkv_s': (0.0, 0.8),
     'L0_attn_bo_s': (0.0, 0.353),
     'L0_attn_bo': (0.0, 0.1),
     'L0_attn_gm': (1.0, 0.6),
     'L0_attn_bm': (0.0, 0.8),
     'L0_attn_b1m': (0.0, 0.364),
     'L0_attn_b2m': (0.0, 0.1),
     'L0_ffn_ln_w': (1.0, 0.2),
     'L0_ffn_ln_b': (0.0, 0.1)}
    factors = {'L0_attn_Wqkv_a': 8.0,
     'L0_attn_Wp_a': 8.0,
     'L0_attn_Wqkv_s': 8.0,
     'L0_attn_Wo_s': 8.0,
     'L1_attn_wq': 8.0,
     'L1_attn_wk': 8.0,
     'L1_attn_wv': 8.0,
     'L1_attn_wo': 8.0,
     'L1_ffn_w_gate': 8.0,
     'L1_ffn_w_up': 8.0,
     'L1_ffn_w_down': 8.0}
    for name, (base, spread) in spreads.items():
        noise = np.random.default_rng([zlib.crc32(name.encode()), seed]).standard_normal(out[name].shape)
        drawn = base * np.exp(spread * noise) if base else spread * noise
        out[name] = jnp.asarray(drawn.astype(out[name].dtype))
    for name, factor in factors.items():
        out[name] = (out[name] * factor).astype(out[name].dtype)
    return out
```

```python
from contextlib import ExitStack

import numpy as np

import concourse.bass as bass
from concourse import mybir

F32 = mybir.dt.float32
BF16 = mybir.dt.bfloat16
I32 = mybir.dt.int32
ALU = mybir.AluOpType
ACT = mybir.ActivationFunctionType
X = mybir.AxisListType.X

NB, L, C = 4, 1024, 128
P = 128
T = L // P
H0, E0 = 16, 8
GR, GH = 4, 4
H1, E1 = 16, 64
FF, FB = 512, 4
FI = 352
QB = 16
WIN_SCALE = float(np.float32(1) / np.sqrt(np.float32(E0)))
L1_SCALE = float(E1) ** -0.5
NEG = -1e30
LN_EPS = 1e-5

C_ID, C_KLE, C_KGT, C_JGT, C_BLK, C_CAUS, C_HM, C_HMS = 0, 128, 256, 384, 512, 640, 768, 772
C_N = 776
W_QKVA, W_QKVS, W_PA, W_OS, W_O, W_1, W_2, W_FC, W_PROJ = 0, 384, 768, 896, 1024, 1152, 1664, 2176, 2688
W_N = 3200
V_G1, V_B1, V_BQA, V_BKA, V_BQS, V_BKS, V_BPA, V_BOS, V_GM, V_BM, V_B1M, V_LNW, V_LNB = (
    0, 1, 2, 3, 4, 5, 6, 7, 8, 9, 10, 14, 18)
V_N = 22
R_BV, R_BO, R_B2 = 0, 256, 384
R_N = 512

JOBS = (
    [("xnT", "v"), ("xaT", "a"), ("qa", "a"), ("ka", "v"), ("qs", "v"), ("ks", "v"), ("v0", "v"), ("v1", "v"),
     ("ktok", "a"), ("den", "v"), ("kv", "v"), ("inter", "a"),
     ("sumT", "a"), ("mixed", "v"), ("hT", "a")]
    + [(f"w1_{f}", "a") for f in range(FB)] + [("mlp", "v")]
    + [(f"fc_{k}", "a") for k in range(FB)] + [(f"fT_{f}", "a") for f in range(FB)] + [("ffn", "a")]
    + [("x1T", "v"), ("xqT", "v")] + [(f"gu_{t}", "v") for t in range(T)]
    + [(f"hqT_{k}", "a") for k in range(3)] + [("down", "a")]
)
JOB = {name: k for k, (name, _) in enumerate(JOBS)}


def drained_count(k):
    return sum(1 for _, e in JOBS[:k + 1] if e == JOBS[k][1])


class Signal:

    def __init__(self, sem, per_seq, before=0):
        self.sem, self.per_seq, self.before = sem, per_seq, before

    def __call__(self, b, count):
        return self.sem, b * self.per_seq + (self.before + count)


def groups_of(i):
    return [range(0, min(4, i + 1))] + ([range(4, i + 1)] if i >= 4 else [])


T_IDX, PV_IDX = {}, {}
for _i in range(T - 1, -1, -1):
    if _i == 2:
        T_IDX["G"] = len(T_IDX)
        T_IDX["B"] = len(T_IDX)
    for _g in range(len(groups_of(_i))):
        PV_IDX[_i, _g] = len(PV_IDX)
        T_IDX[_i, _g] = len(T_IDX)
NT, NPV, NU = len(T_IDX), len(PV_IDX), 10
NPT = 4
V_STEPS = 138


def program(nc, x, head_w, wtab, vtab, rtab, ctab, w_gate, w_up, w_down, out):
    with ExitStack() as ctx:
        def sb(name, shape, dt=F32):
            return ctx.enter_context(nc.sbuf_tensor(name, shape, dt))

        def sem(name):
            return ctx.enter_context(nc.semaphore(name))

        def sig(name, per_seq, before=0):
            return Signal(sem(name), per_seq, before)

        cst = sb("cst", [P, C_N])
        wts = sb("wts", [P, W_N])
        vec = sb("vec", [P, V_N])
        row = sb("row", [P, R_N])
        ident = cst[:, C_ID:C_ID + P]
        hmask = cst[:, C_HM:C_HM + GH]
        hmask_s = cst[:, C_HMS:C_HMS + GH]
        ident_b = sb("ident_b", [P, P], BF16)
        causal_b = sb("causal_b", [P, P], BF16)
        neg = sb("neg", [P, P])
        mhalf = sb("mhalf", [P, T])
        bqa_m = sb("bqa_m", [P, GH])
        bqs_s = sb("bqs_s", [P, 1])
        bsum = sb("bsum", [P, 1])
        ones = sb("ones", [P, P])
        wfc = wts[:, W_FC:W_FC + FF]
        wproj = wts[:, W_PROJ:W_PROJ + FF].rearrange("p (f n) -> p f n", f=FB)
        rsum = sb("rsum", [P, 2])
        half = sb("half", [P, 4])
        wnat = sb("wnat", [P, 2, 3, P])
        wdn = sb("wdn", [P, FI])
        wgT = sb("wgT", [P, 2, FI])
        wdT = sb("wdT", [P, 3, P])

        xs = sb("xs", [P, T, C])
        xc = sb("xc", [P, T, C])
        xn = sb("xn", [P, T, C])
        xa = sb("xa", [P, T, C])
        tmp = sb("tmp", [P, T, C])
        st = sb("st", [P, 8, T])
        xnT = sb("xnT", [P, L])
        xaT = sb("xaT", [P, L])
        big0 = sb("big0", [P, 4 * L])
        big1 = sb("big1", [P, 4 * L])
        qam = big0[:, :].rearrange("p (n j r) -> p n j r", n=T, j=GH)
        qfm = big1[:, :].rearrange("p (n j r) -> p n j r", n=T, j=GH)
        h1T = big0[:, :].rearrange("p (f r) -> p f r", f=FB)
        hid = big0[:, :].rearrange("p (t n) -> p t n", t=T)
        hidT = big1[:, :].rearrange("p (f r) -> p f r", f=FB)
        NQ = T * FI
        work = sb("work", [P, 4 * NQ])
        kaT, qf, kf, z0, z1, z2, z3, interT, ktok_, state_ = (work[:, k * L:(k + 1) * L] for k in range(10))
        ktok, state = (w.rearrange("p (t c) -> p t c", t=T) for w in (ktok_, state_))
        qa_, qz_, qy_, qs_ = (work[:, k * NQ:(k + 1) * NQ] for k in range(4))
        val = sb("val", [P, T, 2 * C])
        rdenT = sb("rdenT", [P, L])
        winT = sb("winT", [P, L])
        linT = sb("linT", [P, L])
        sumT = sb("sumT", [P, L])
        x1 = sb("x1", [P, T, C])
        s0 = sb("s0", [P, T, C])
        gate = sb("gate", [P, T, C])
        ost = sb("ost", [P, T, C])

        probs = sb("probs", [P, 12 * 512])
        quarter = [probs[:, k * 512:(k + 1) * 512].rearrange("p (j r) -> p j r", j=GH) for k in range(12)]
        pr, ptc, ptp, am, ext = quarter[0:3], quarter[3:5], quarter[5:7], quarter[7:10], quarter[10]
        nmx = sb("nmx", [P, 3, GH])
        den = sb("den", [P, 3, GH])
        rdn = sb("rdn", [P, 3, GH])
        red = sb("red", [P, P])
        poke = sb("poke", [P, 2])
        red2 = sb("red2", [P, P])

        hw = sb("hw", [E1, 4, C])
        G = sb("G", [P, P])
        Bv = sb("Bv", [P, P])
        yT = winT
        Z = linT[:, :].rearrange("p (t c) -> p t c", t=T)
        pb = [probs[:, k * L:(k + 1) * L] for k in range(4)]
        pt = quarter[8:8 + NPT]
        nm1 = sb("nm1", [P, T])
        dn1 = sb("dn1", [P, T])
        rd1 = sb("rd1", [P, T])

        qsc = sb("qsc", [P, 2, NQ // QB])
        hh = big0[:, 0:NQ].rearrange("p (t n) -> p t n", t=T)
        hq = big1[:, 0:NQ].rearrange("p (t n) -> p t n", t=T)
        sg = sb("sg", [P, 2, FI])
        hqT = big0[:, 0:3 * L].rearrange("p (k r) -> p k r", k=3)

        pair = [ctx.enter_context(nc.psum_tensor(f"pair{i}", [P, 2, 512], F32)) for i in range(4)]

        def flat(k):
            return pair[k % 4][:, :, :].rearrange("p a n -> p (a n)")

        def tiles(k):
            return flat(k).rearrange("p (t n) -> p t n", n=P)

        def bank(n):
            return pair[n // 2][:, n % 2, :]

        loaded = sem("loaded")
        x_in = sig("x_in", 16)
        hw_in = sem("hw_in")
        stored = sig("stored", 16, 16)
        pool_const = sem("pool_const")
        filled = sig("filled", len(JOBS))
        by_v = sig("drained_by_vector", sum(e == "v" for _, e in JOBS))
        by_a = sig("drained_by_scalar", sum(e == "a" for _, e in JOBS))
        v_own = sem("v_own")
        a_own = sem("a_own")
        stat_in = sig("stat_in", 5)
        rstd_out = sig("rstd_out", 5)
        xn_ready = sig("xn_ready", 5)
        feat_neg = sig("feat_neg", 2)
        feat_exp = sig("feat_exp", 2)
        feat = sig("features", 4)
        states = sig("states", 1)
        win_scores = sig("win_scores", 32)
        win_max = sig("win_max", 32)
        win_exp = sig("win_exp", 32)
        win_rden = sig("win_rden", 32)
        win_norm = sig("win_norm", 32)
        win_tr = sig("win_tr", 32)
        win_pt = sig("win_pt", 32)
        win_pv = sig("win_pv", 32)
        win_out = sig("win_out", T)
        lin_a = sig("lin_a", 32)
        lin_am = sig("lin_am", 32)
        lin_pv = sig("lin_pv", 32)
        lin_out = sig("lin_out", T)
        hid_norm = sig("hid_norm", T)
        up_done = sig("up_silu", T)
        u_full = sem("l1_use_filled")
        u_free = sem("l1_use_drained")
        l_max = sem("l1_max")
        l_norm = sem("l1_norm")
        t_full = sem("l1_tr_filled")
        t_free = sem("l1_tr_drained")
        l_pv = sem("l1_pv")
        acc_out = sig("l1_out", 1)
        l_own = sem("l1_v_own")
        hq_ready = sig("hq_ready", 1)
        fsign = sig("fp4_sign", 2)
        set_pe = sem("setup_pe")
        set_v = sem("setup_v")
        set_a = sem("setup_a")
        ready = sem("result_ready")

        block = ctx.enter_context(nc.Block())

        def drained(eng, b, name):
            k = JOB[name]
            eng.wait_ge(*(by_v if JOBS[k][1] == "v" else by_a)(b, drained_count(k)))

        def load_filled(eng, b, name):
            eng.wait_ge(*filled(b, JOB[name] + 1))

        @block.sync
        def _(sp):
            sp.sem_inc(stored.sem, 16)
            sp.dma_start(cst[:, :], ctab).then_inc(loaded, 16)
            sp.dma_start(wts[:, :], wtab).then_inc(loaded, 16)
            sp.dma_start(vec[:, :], vtab).then_inc(loaded, 16)
            sp.dma_start(row[:, :], rtab.partition_broadcast(P)).then_inc(loaded, 16)
            sp.wait_ge(pool_const, 1)
            for k, w in enumerate((w_gate, w_up)):
                sp.dma_start(wnat[:, k, 0:2, :], w[0:2 * P, :].rearrange("(t p) c -> p t c", p=P)).then_inc(loaded, 16)
                sp.dma_start(wnat[0:FI - 2 * P, k, 2, :], w[2 * P:FI, :]).then_inc(loaded, 16)
            sp.dma_start(wdn[:, :], w_down).then_inc(loaded, 16)
            sp.dma_start(hw[:, :, :], head_w[0]).then_inc(hw_in, 16)

            def load_x(b):
                sp.dma_start(xs[:, :, :], x[b].rearrange("(t p) c -> p t c", p=P)).then_inc(x_in.sem, 16)

            def sequence(b, last):
                if not last:
                    sp.wait_ge(*xn_ready(b, 4))
                    load_x(b + 1)
                with sp.Fori(0, H1) as h:
                    sp.wait_ge(t_full, b * (H1 * NT) + h * NT + 2)
                    sp.dma_start(hw[:, :, :], head_w[h + 1]).then_inc(hw_in, 16)
                sp.wait_ge(ready, b + 1)
                sp.dma_start(out[b].rearrange("(t p) c -> p t c", p=P), ost[:, :, :]).then_inc(stored.sem, 16)

            load_x(0)
            with sp.Fori(0, NB - 1) as b:
                sequence(b, False)
            sequence(NB - 1, True)
            sp.wait_ge(*stored(NB - 1, 16))
            sp.wait_ge(hw_in, 16 * (NB * H1 + 1))

        @block.gpsimd
        def _(pool):
            pool.memset(wnat[:, :, 2, :], 0.0).then_inc(pool_const, 1)
            pool.memset(mhalf[:, :], -0.5).then_inc(pool_const, 1)
            pool.memset(ones[:, :], 1.0).then_inc(pool_const, 1)
            pool.memset(neg[:, :], NEG).then_inc(pool_const, 1)
            pool.wait_ge(pool_const, 4)

            with pool.Fori(0, NB) as b:
                def rstd(k, dst, src):
                    pool.wait_ge(*stat_in(b, k + 1))
                    pool.tensor_tensor(dst, src, mhalf[:, :], ALU.pow).then_inc(rstd_out.sem, 1)

                rstd(0, st[:, 3, :], st[:, 2, :])
                rstd(1, st[:, 5, :], st[:, 4, :])
                for s in range(4 * T):
                    pool.wait_ge(*win_rden(b, s + 1))
                    p = pr[s % 3]
                    pool.tensor_tensor(p[:, :, :], p[:, :, :],
                                       rdn[:, s % 3, :].unsqueeze(2).broadcast_to([P, GH, P]),
                                       ALU.mult).then_inc(win_norm.sem, 1)
                for k in range(2, 5):
                    rstd(k, st[:, 3, :], st[:, 2, :])

        @block.scalar
        def _(act):
            act.wait_ge(loaded, 16 * 9)
            for dst, src in ((ident_b, C_ID), (causal_b, C_CAUS)):
                act.activation(dst[:, :], cst[:, src:src + P], ACT.Copy).then_inc(set_a, 1)
            for k in range(2):
                act.activation(qs_[:, k * 3 * P:(k + 1) * 3 * P], wnat[:, k, :, :].rearrange("p t c -> p (t c)"),
                               ACT.Sign).then_inc(set_a, 1)
            act.activation(qs_[:, 6 * P:6 * P + FI], wdn[:, :], ACT.Sign).then_inc(set_a, 1)
            act.wait_ge(set_v, 10)
            act.sem_inc(u_free, 2)

            with act.Fori(0, NB) as b:
                def full(name):
                    act.wait_ge(*filled(b, JOB[name] + 1))

                full("xaT")
                act.activation(xaT[:, :], flat(JOB["xaT"]), ACT.Identity, bias=vec[:, V_B1:V_B1 + 1],
                               scale=vec[:, V_G1:V_G1 + 1]).then_inc(by_a.sem, 1)
                full("qa")
                for j in range(GH):
                    ins = act.activation(qam[:, :, j, :], tiles(JOB["qa"]), ACT.Identity, bias=bqa_m[:, j:j + 1],
                                         scale=hmask_s[:, j:j + 1])
                ins.then_inc(by_a.sem, 1)
                for k, zz in ((0, z0), (1, z2)):
                    act.wait_ge(*feat_neg(b, k + 1))
                    act.activation(zz[:, :], zz[:, :], ACT.Exp).then_inc(feat_exp.sem, 1)
                full("ktok")
                act.activation(ktok[:, :, :], tiles(JOB["ktok"]), ACT.Copy).then_inc(by_a.sem, 1)
                full("inter")
                act.activation(interT[:, P:L], flat(JOB["inter"])[:, P:L], ACT.Copy).then_inc(by_a.sem, 1)

                for s in range(4 * T):
                    act.wait_ge(*win_max(b, s + 1))
                    if s >= 3:
                        act.wait_ge(*win_tr(b, s - 2))
                    S = pair[s % 2][:, :, :].rearrange("p a n -> p (a n)").rearrange("p (j k) -> p j k", j=GH)
                    for j in range(GH):
                        ins = act.activation(pr[s % 3][:, j, :], S[:, j, P:2 * P], ACT.Exp,
                                             bias=nmx[:, s % 3, j:j + 1], accum_out=den[:, s % 3, j:j + 1])
                    ins.then_inc(win_exp.sem, 1)

                full("sumT")
                act.activation(sumT[:, :], flat(JOB["sumT"]), ACT.Identity, bias=bsum[:, 0:1]).then_inc(by_a.sem, 1)
                full("hT")
                act.activation(xaT[:, :], flat(JOB["hT"]), ACT.Identity, bias=vec[:, V_BM:V_BM + 1],
                               scale=vec[:, V_GM:V_GM + 1]).then_inc(by_a.sem, 1)
                for f in range(FB):
                    full(f"w1_{f}")
                    act.activation(h1T[:, f, :], flat(JOB[f"w1_{f}"]), ACT.Gelu,
                                   bias=vec[:, V_B1M + f:V_B1M + f + 1]).then_inc(by_a.sem, 1)
                for k in range(FB):
                    full(f"fc_{k}")
                    if k == 0:
                        drained(act, b, "mlp")
                    for t in (2 * k, 2 * k + 1):
                        ins = act.activation(hid[:, t, :], bank(2 * (JOB[f"fc_{k}"] % 4) + t % 2), ACT.Gelu,
                                             accum_out=st[:, 0, t:t + 1])
                    ins.then_inc(by_a.sem, 1)
                for f in range(FB):
                    full(f"fT_{f}")
                    act.activation(hidT[:, f, :], flat(JOB[f"fT_{f}"]), ACT.Identity,
                                   bias=vec[:, V_LNB + f:V_LNB + f + 1],
                                   scale=vec[:, V_LNW + f:V_LNW + f + 1]).then_inc(by_a.sem, 1)
                full("ffn")
                act.activation(gate[:, :, :], tiles(JOB["ffn"]), ACT.Silu).then_inc(by_a.sem, 1)

                def l1_head(i, first):
                    act.wait_ge(u_full, i * NU + 1)
                    act.activation(yT[:, :], flat(0), ACT.Copy, scale=L1_SCALE).then_inc(u_free, 1)
                    act.wait_ge(u_full, i * NU + 2)
                    if not first:
                        act.wait_ge(l_pv, i * NPV)
                    act.activation(Z[:, :, :], tiles(1), ACT.Copy).then_inc(u_free, 1)
                    for k in range(T):
                        q = T - 1 - k
                        act.wait_ge(l_max, i * T + k + 1)
                        w = (q + 1) * P
                        act.activation(pb[k % 4][:, 0:w], flat(k % 2)[:, 0:w], ACT.Exp,
                                       bias=nm1[:, q:q + 1], accum_out=dn1[:, q:q + 1]).then_inc(u_free, 1)

                l1_head(b * H1, True)
                with act.Fori(1, H1) as h:
                    l1_head(b * H1 + h, False)

                act.wait_ge(*xn_ready(b, 4))
                act.activation(qs_[:, 0:L], xn[:, :, :].rearrange("p t c -> p (t c)"), ACT.Sign)\
                   .then_inc(fsign.sem, 1)
                for t in range(T):
                    full(f"gu_{t}")
                    if t >= 2:
                        act.wait_ge(*by_v(b, drained_count(JOB[f"gu_{t - 2}"])))
                    act.activation(sg[:, t % 2, :], bank(2 * (JOB[f"gu_{t}"] % 4))[:, 0:FI], ACT.Silu)\
                       .then_inc(up_done.sem, 1)
                act.wait_ge(*by_v(b, drained_count(JOB[f"gu_{T - 1}"])))
                act.activation(qs_[:, :], hh.rearrange("p t n -> p (t n)"), ACT.Sign).then_inc(fsign.sem, 1)
                for k in range(3):
                    n = min(P, FI - k * P)
                    full(f"hqT_{k}")
                    act.activation(hqT[0:n, k, :], flat(JOB[f"hqT_{k}"])[0:n, :], ACT.Copy).then_inc(by_a.sem, 1)
                full("down")
                act.activation(gate[:, :, :], tiles(JOB["down"]), ACT.Silu).then_inc(by_a.sem, 1)

        @block.vector
        def _(dve):
            own = [0]

            def bc(ap, n):
                return ap.unsqueeze(2).broadcast_to([P, ap.shape[1], n])

            def bcm(ap, n):
                return ap.unsqueeze(1).broadcast_to([P, n, ap.shape[1]])

            def fp4(link, src, dst, sgn, nblk):
                a = qa_[:, 0:nblk * QB]
                z = qz_[:, 0:nblk * QB]
                y = qy_[:, 0:nblk * QB]
                sc, rs = qsc[:, 0, 0:nblk], qsc[:, 1, 0:nblk]
                b3 = lambda ap: ap.rearrange("p (n q) -> p n q", q=QB)
                link(dve.tensor_reduce(sc, b3(src), X, ALU.max, apply_absolute_value=True))
                link(dve.tensor_scalar(sc, sc, 1.0 / 6.0, 1e-12, ALU.mult, ALU.max))
                link(dve.reciprocal(rs, sc))
                link(dve.tensor_tensor(b3(y), b3(src), bc(rs, QB), ALU.mult))
                link(dve.scalar_tensor_tensor(a, y, -1.0, y, ALU.mult, ALU.max))
                link(dve.tensor_scalar(z, a, 5.0, 2.0, ALU.is_gt, ALU.mult))
                link(dve.scalar_tensor_tensor(y, a, 3.5, z, ALU.is_gt, ALU.add))
                link(dve.scalar_tensor_tensor(z, a, 2.5, y, ALU.is_gt, ALU.add))
                link(dve.tensor_scalar(y, z, 2.0, None, ALU.mult))
                link(dve.scalar_tensor_tensor(z, a, 1.75, y, ALU.is_gt, ALU.add))
                link(dve.scalar_tensor_tensor(y, a, 1.25, z, ALU.is_gt, ALU.add))
                link(dve.scalar_tensor_tensor(z, a, 0.75, y, ALU.is_gt, ALU.add))
                link(dve.scalar_tensor_tensor(y, a, 0.25, z, ALU.is_gt, ALU.add))
                link(dve.scalar_tensor_tensor(b3(z), b3(sgn), 0.5, bc(sc, QB), ALU.mult, ALU.mult))
                return dve.tensor_tensor(dst, y, z, ALU.mult)

            def slink(ins):
                own[0] += 1
                ins.then_inc(v_own, 1)
                dve.wait_ge(v_own, own[0])

            dve.wait_ge(loaded, 16 * 9)
            dve.wait_ge(pool_const, 4)
            for k, w in enumerate((W_FC, W_PROJ)):
                dve.tensor_reduce(rsum[:, k:k + 1], wts[:, w:w + FF], X, ALU.add, apply_absolute_value=True)\
                   .then_inc(set_v, 1)
            dve.wait_ge(set_pe, 1)
            slink(dve.tensor_scalar(half[:, 0:2], bank(0)[:, 0:2], 1.0 / (FF * C), 1e-6, ALU.mult, ALU.add))
            slink(dve.tensor_scalar(half[:, 2:4], half[:, 0:2], -0.5, None, ALU.mult))
            slink(dve.tensor_scalar(half[:, 0:2], half[:, 0:2], 0.5, None, ALU.mult))
            for k, w in enumerate((W_FC, W_PROJ)):
                m = wts[:, w:w + FF]
                slink(dve.tensor_scalar(qa_[:, 0:FF], m, half[:, 2 + k:3 + k], None, ALU.is_lt))
                slink(dve.scalar_tensor_tensor(qz_[:, 0:FF], m, half[:, k:k + 1], qa_[:, 0:FF], ALU.is_gt, ALU.subtract))
                dve.tensor_copy(m, qz_[:, 0:FF]).then_inc(set_v, 1)
                dve.wait_ge(set_v, 3 + k)
            for j in range(GH):
                dve.tensor_tensor(bqa_m[:, j:j + 1], hmask_s[:, j:j + 1], vec[:, V_BQA:V_BQA + 1], ALU.mult)\
                   .then_inc(set_v, 1)
            dve.tensor_scalar(bqs_s[:, :], vec[:, V_BQS:V_BQS + 1], WIN_SCALE, None, ALU.mult).then_inc(set_v, 1)
            dve.tensor_tensor(bsum[:, :], vec[:, V_BPA:V_BPA + 1], vec[:, V_BOS:V_BOS + 1], ALU.add).then_inc(set_v, 1)
            dve.wait_ge(set_a, 5)
            for k in range(2):
                src = wnat[:, k, :, :].rearrange("p t c -> p (t c)")
                fp4(slink, src, src, qs_[:, k * 3 * P:(k + 1) * 3 * P], 3 * P // QB).then_inc(set_v, 1)
                dve.wait_ge(set_v, 11 + k)
            fp4(slink, wdn[:, :], wdn[:, :], qs_[:, 6 * P:6 * P + FI], FI // QB).then_inc(set_v, 1)
            for k in range(3):
                dve.wait_ge(set_pe, 2 + k)
                n = min(P, FI - k * P)
                dve.tensor_copy(wgT[:, 0, k * P:k * P + n], bank(2 + k)[:, 0:n]).then_inc(set_v, 1)
                dve.tensor_copy(wgT[:, 1, k * P:k * P + n], bank(2 + k)[:, P:P + n]).then_inc(set_v, 1)
                dve.tensor_copy(wdT[0:n, k, :], bank(2 + k)[0:n, 2 * P:3 * P]).then_inc(set_v, 1)
            dve.wait_ge(t_full, 1)
            dve.tensor_copy(G[:, :], bank(4)[:, 0:P]).then_inc(t_free, 1)
            dve.wait_ge(t_full, 2)
            dve.tensor_copy(Bv[:, :], bank(5)[:, 0:P]).then_inc(t_free, 1)
            setup_steps = own[0]

            with dve.Fori(0, NB) as b:
                own[0] = 0

                def link(ins):
                    own[0] += 1
                    ins.then_inc(v_own, 1)
                    dve.wait_ge(v_own, b * V_STEPS + (setup_steps + own[0]))

                def full(name):
                    dve.wait_ge(*filled(b, JOB[name] + 1))

                def center(k, src):
                    link(dve.tensor_reduce(st[:, 0, :], src, X, ALU.add))
                    link(dve.tensor_scalar(st[:, 1, :], st[:, 0, :], -1.0 / C, None, ALU.mult))
                    link(dve.tensor_tensor(xc[:, :, :], src, bc(st[:, 1, :], C), ALU.add))
                    link(dve.tensor_tensor(tmp[:, :, :], xc[:, :, :], xc[:, :, :], ALU.mult))
                    link(dve.tensor_reduce(st[:, 6, :], tmp[:, :, :], X, ALU.add))
                    dve.tensor_scalar(st[:, 2, :], st[:, 6, :], 1.0 / C, LN_EPS, ALU.mult, ALU.add)\
                       .then_inc(stat_in.sem, 1)
                    dve.wait_ge(*rstd_out(b, k + 1))

                dve.wait_ge(*x_in(b, 16))
                center(0, xs[:, :, :])
                dve.tensor_tensor(xn[:, :, :], xc[:, :, :], bc(st[:, 3, :], C), ALU.mult).then_inc(xn_ready.sem, 1)
                link(dve.tensor_tensor(st[:, 1, :], st[:, 3, :], st[:, 3, :], ALU.mult))
                link(dve.scalar_tensor_tensor(st[:, 7, :], st[:, 6, :], 1.0 / C, st[:, 1, :], ALU.mult, ALU.mult))
                dve.tensor_scalar(st[:, 4, :], st[:, 7, :], LN_EPS, None, ALU.add).then_inc(stat_in.sem, 1)
                dve.wait_ge(*rstd_out(b, 2))
                dve.wait_ge(*xn_ready(b, 1))
                dve.tensor_tensor(xa[:, :, :], xn[:, :, :], bc(st[:, 5, :], C), ALU.mult).then_inc(xn_ready.sem, 1)

                full("xnT")
                dve.tensor_copy(xnT[:, :], flat(JOB["xnT"])).then_inc(by_v.sem, 1)
                full("ka")
                dve.tensor_scalar(kaT[:, :], flat(JOB["ka"]), vec[:, V_BKA:V_BKA + 1], None, ALU.add)\
                   .then_inc(by_v.sem, 1)

                full("qs")
                dve.tensor_scalar(z1[:, :], flat(JOB["qs"]), WIN_SCALE, bqs_s[:, 0:1], ALU.mult, ALU.add)\
                   .then_inc(by_v.sem, 1)
                full("ks")
                dve.tensor_scalar(z3[:, :], flat(JOB["ks"]), vec[:, V_BKS:V_BKS + 1], None, ALU.add)\
                   .then_inc(by_v.sem, 1)
                drained(dve, b, "ks")
                for zz, neg_part in ((z1, z0), (z3, z2)):
                    dve.tensor_scalar(neg_part[:, :], zz[:, :], 0.0, None, ALU.min).then_inc(feat_neg.sem, 1)
                for k in range(2):
                    full(f"v{k}")
                    dve.tensor_tensor(val[:, 4 * k:4 * k + 4, :],
                                      flat(JOB[f"v{k}"]).rearrange("p (t n) -> p t n", n=2 * C),
                                      bcm(row[:, R_BV:R_BV + 2 * C], 4), ALU.add).then_inc(by_v.sem, 1)
                for k, (zz, ee, ff) in enumerate(((z1, z0, qf), (z3, z2, kf))):
                    dve.wait_ge(*feat_exp(b, k + 1))
                    link(dve.scalar_tensor_tensor(zz[:, :], zz[:, :], 0.0, ee[:, :], ALU.max, ALU.add))
                    dve.tensor_scalar(ff[:, :], zz[:, :], 0.0001, None, ALU.add).then_inc(feat.sem, 1)
                dve.wait_ge(*feat(b, 2))
                link(dve.tensor_tensor_scan(z0[:, :], kf[:, :], kf[:, :], 0.0, ALU.add, ALU.bypass))
                dve.tensor_tensor(z2[:, :], z0[:, :], qf[:, :], ALU.mult).then_inc(feat.sem, 1)
                for j in range(GH):
                    ins = dve.tensor_scalar(qfm[:, :, j, :], qf[:, :].rearrange("p (n r) -> p n r", n=T),
                                            hmask[:, j:j + 1], None, ALU.mult)
                ins.then_inc(feat.sem, 1)
                full("den")
                link(dve.tensor_scalar(z1[:, :], flat(JOB["den"]), 1e-6, None, ALU.add))
                dve.reciprocal(rdenT[:, :], z1[:, :]).then_inc(by_v.sem, 1)
                full("kv")
                dve.tensor_tensor(tmp[:, 0:T - 1, :], tiles(JOB["kv"])[:, 0:T - 1, :],
                                  bcm(cst[:, C_BLK:C_BLK + P], T - 1), ALU.mult).then_inc(by_v.sem, 1)
                drained(dve, b, "kv")
                link(dve.tensor_copy(state[:, 1, :], tmp[:, 0, :]))
                for n in range(2, T):
                    ins = dve.tensor_tensor(state[:, n, :], state[:, n - 1, :], tmp[:, n - 1, :], ALU.add)
                    if n < T - 1:
                        link(ins)
                ins.then_inc(states.sem, 1)

                def scores_there(s):
                    dve.wait_ge(*win_scores(b, s + 1))

                def win_front(s):
                    n = s // 4
                    S = pair[s % 2][:, :, :].rearrange("p a n -> p (a n)").rearrange("p (j k) -> p j k", j=GH)
                    if s < 2:
                        scores_there(s)
                        own[0] += 1
                        dve.memset(poke[:, s:s + 1], 0.0).then_inc(v_own, 1)
                    before = S[:, :, 0:P] if n else bcm(neg[:, :], GH)
                    link(dve.copy_predicated(S[:, :, P:2 * P], bcm(cst[:, C_JGT:C_JGT + P].bitcast(I32), GH), before))
                    dve.tensor_reduce(nmx[:, s % 3, :], S[:, :, P:2 * P], X, ALU.max, negate=True)\
                       .then_inc(win_max.sem, 1)

                def win_recip(s):
                    dve.wait_ge(*win_exp(b, s + 1))
                    dve.reciprocal(rdn[:, s % 3, :], den[:, s % 3, :]).then_inc(win_rden.sem, 1)

                def win_evac(s):
                    dve.wait_ge(*win_tr(b, s + 1))
                    if s >= 2:
                        dve.wait_ge(*win_pv(b, s - 1))
                    t = bank(4 + s % 2).rearrange("p (j r) -> p j r", j=GH)
                    dve.tensor_tensor(ptp[s % 2][:, :, :], t, bcm(cst[:, C_KGT:C_KGT + P], GH), ALU.mult)
                    if s + 2 < 4 * T:
                        scores_there(s + 2)
                    dve.tensor_tensor(ptc[s % 2][:, :, :], t, bcm(cst[:, C_KLE:C_KLE + P], GH), ALU.mult)\
                       .then_inc(win_pt.sem, 1)

                def pick(n):
                    link(dve.tensor_tensor(ext[:, :, :], bank(6 + n % 2).rearrange("p (j r) -> p j r", j=GH),
                                           bc(hmask, P), ALU.mult))
                    return ext[:, :, :].rearrange("p j r -> p r j")

                def win_extract(n):
                    dve.wait_ge(*win_pv(b, 4 * n + 4))
                    dve.tensor_reduce(winT[:, n * P:(n + 1) * P], pick(n), X, ALU.add).then_inc(win_out.sem, 1)

                for s in range(4 * T + 4):
                    if 2 <= s < 4 * T + 2:
                        win_evac(s - 2)
                    if s < 4 * T:
                        win_front(s)
                    if 1 <= s <= 4 * T:
                        win_recip(s - 1)
                    if s >= 4 and s % 4 == 3 and s < 4 * T + 4 and s // 4 - 1 < T:
                        win_extract(s // 4 - 1)

                def lin_evac(s):
                    dve.wait_ge(*lin_a(b, s + 1))
                    if s >= 3:
                        dve.wait_ge(*lin_pv(b, s - 2))
                    dve.tensor_tensor(am[s % 3][:, :, :], bank(s % 4).rearrange("p (j r) -> p j r", j=GH),
                                      bcm(cst[:, C_KLE:C_KLE + P], GH), ALU.mult).then_inc(lin_am.sem, 1)

                def lin_extract(n):
                    at = slice(n * P, (n + 1) * P)
                    dve.wait_ge(*lin_pv(b, 4 * n + 4))
                    link(dve.tensor_reduce(red[:, :], pick(n), X, ALU.add))
                    src = red
                    if n:
                        link(dve.tensor_tensor(red2[:, :], red[:, :], interT[:, at], ALU.add))
                        src = red2
                    dve.tensor_tensor(linT[:, at], src[:, :], rdenT[:, at], ALU.mult).then_inc(lin_out.sem, 1)

                drained(dve, b, "inter")
                for s in range(4 * T + 3):
                    if s < 4 * T:
                        lin_evac(s)
                    if s >= 6 and s % 4 == 2 and s // 4 - 1 < T:
                        lin_extract(s // 4 - 1)

                full("mixed")
                dve.tensor_tensor(tmp[:, :, :], tiles(JOB["mixed"]), xn[:, :, :], ALU.add).then_inc(by_v.sem, 1)
                drained(dve, b, "mixed")
                link(dve.tensor_tensor(s0[:, :, :], tmp[:, :, :], bcm(row[:, R_BO:R_BO + C], T), ALU.add))
                center(2, s0[:, :, :])
                dve.tensor_tensor(xa[:, :, :], xc[:, :, :], bc(st[:, 3, :], C), ALU.mult).then_inc(xn_ready.sem, 1)
                link(dve.tensor_tensor(s0[:, :, :], s0[:, :, :], bcm(row[:, R_B2:R_B2 + C], T), ALU.add))
                full("mlp")
                dve.tensor_tensor(s0[:, :, :], tiles(JOB["mlp"]), s0[:, :, :], ALU.add).then_inc(by_v.sem, 1)
                drained(dve, b, "fc_3")
                link(dve.tensor_scalar(st[:, 1, :], st[:, 0, :], -1.0 / FF, None, ALU.mult))
                for t in range(T):
                    link(dve.tensor_scalar(hid[:, t, :], hid[:, t, :], st[:, 1, t:t + 1], None, ALU.add))
                for q in range(2):
                    sq = big1[:, 0:4 * FF].rearrange("p (t n) -> p t n", t=4)
                    link(dve.tensor_tensor(sq, hid[:, 4 * q:4 * q + 4, :], hid[:, 4 * q:4 * q + 4, :], ALU.mult))
                    link(dve.tensor_reduce(st[:, 6, 4 * q:4 * q + 4], sq, X, ALU.add))
                dve.tensor_scalar(st[:, 2, :], st[:, 6, :], 1.0 / FF, LN_EPS, ALU.mult, ALU.add)\
                   .then_inc(stat_in.sem, 1)
                dve.wait_ge(*rstd_out(b, 4))
                for t in range(T):
                    dve.tensor_scalar(hid[:, t, :], hid[:, t, :], st[:, 3, t:t + 1], None, ALU.mult)\
                       .then_inc(hid_norm.sem, 1)
                drained(dve, b, "ffn")
                drained(dve, b, "mlp")
                link(dve.tensor_tensor(tmp[:, :, :], s0[:, :, :], gate[:, :, :], ALU.mult))
                link(dve.tensor_tensor(x1[:, :, :], tmp[:, :, :], xs[:, :, :], ALU.add))

                center(4, x1[:, :, :])
                dve.tensor_tensor(xn[:, :, :], xc[:, :, :], bc(st[:, 3, :], C), ALU.mult).then_inc(xn_ready.sem, 1)
                dve.wait_ge(*xn_ready(b, 4))
                full("x1T")
                dve.tensor_copy(xnT[:, :], flat(JOB["x1T"])).then_inc(by_v.sem, 1)

                def l_front(i, q):
                    k, w = T - 1 - q, (q + 1) * P
                    dve.wait_ge(u_full, i * NU + 3 + k)
                    dve.tensor_reduce(nm1[:, q:q + 1], flat(k % 2)[:, 0:w], X, ALU.max, negate=True).then_inc(l_max, 1)

                def l_normalize(i, q):
                    k, w = T - 1 - q, (q + 1) * P
                    dve.wait_ge(u_free, i * NU + 2 + 3 + k)
                    llink(i, dve.reciprocal(rd1[:, q:q + 1], dn1[:, q:q + 1]))
                    dve.tensor_scalar(pb[k % 4][:, 0:w], pb[k % 4][:, 0:w], rd1[:, q:q + 1], None, ALU.mult)\
                       .then_inc(l_norm, 1)

                def llink(i, ins):
                    lown[0] += 1
                    ins.then_inc(l_own, 1)
                    dve.wait_ge(l_own, i * T + lown[0])

                def l_evac(i, q, before):
                    for g, js in enumerate(groups_of(q)):
                        ti = T_IDX[q, g] + 2
                        pi = PV_IDX[q, g]
                        base, pbase = (i - 1, i - 1) if before else (i, i)
                        dve.wait_ge(t_full, base * NT + ti + 1)
                        if pi >= NPT or before or not first_head[0]:
                            dve.wait_ge(l_pv, pbase * NPV + pi - NPT + 1)
                        dve.tensor_copy(pt[pi % NPT][:, 0:len(js), :],
                                        bank(4 + ti % 2).rearrange("p (j r) -> p j r", j=4)[:, 0:len(js), :])\
                           .then_inc(t_free, 1)

                first_head = [True]
                lown = [0]

                def l1_head(i, first):
                    first_head[0] = first
                    lown[0] = 0
                    if not first:
                        l_evac(i, 1, True)
                        l_evac(i, 0, True)
                    l_front(i, 7)
                    l_front(i, 6)
                    l_normalize(i, 7)
                    l_front(i, 5)
                    l_evac(i, 7, False)
                    l_normalize(i, 6)
                    for q in range(4, -1, -1):
                        l_front(i, q)
                        if q == 0:
                            for k, dst in ((T_IDX["G"] + 2, G), (T_IDX["B"] + 2, Bv)):
                                dve.wait_ge(t_full, i * NT + k + 1)
                                dve.tensor_copy(dst[:, :], bank(4 + k % 2)[:, 0:P]).then_inc(t_free, 1)
                        l_evac(i, q + 2, False)
                        l_normalize(i, q + 1)
                    l_normalize(i, 0)

                l1_head(b * H1, True)
                with dve.Fori(1, H1) as h:
                    l1_head(b * H1 + h, False)
                first_head[0] = False
                l_evac((b + 1) * H1, 1, True)
                l_evac((b + 1) * H1, 0, True)
                dve.wait_ge(l_pv, (b + 1) * (H1 * NPV))
                dve.tensor_copy(s0[:, :, :], tiles(3)).then_inc(acc_out.sem, 1)

                dve.wait_ge(*fsign(b, 1))
                xn_f = xn[:, :, :].rearrange("p t c -> p (t c)")
                fp4(link, xn_f, xa[:, :, :].rearrange("p t c -> p (t c)"), qs_[:, 0:L], L // QB)\
                    .then_inc(xn_ready.sem, 1)
                full("xqT")
                dve.tensor_copy(xaT[:, :], flat(JOB["xqT"])).then_inc(by_v.sem, 1)
                for t in range(T):
                    dve.wait_ge(*up_done(b, t + 1))
                    dve.tensor_tensor(hh[:, t, :], bank(2 * (JOB[f"gu_{t}"] % 4) + 1)[:, 0:FI], sg[:, t % 2, :],
                                      ALU.mult).then_inc(by_v.sem, 1)
                drained(dve, b, f"gu_{T - 1}")
                dve.wait_ge(*fsign(b, 2))
                fp4(link, hh.rearrange("p t n -> p (t n)"), hq.rearrange("p t n -> p (t n)"), qs_[:, :], NQ // QB)\
                    .then_inc(hq_ready.sem, 1)
                drained(dve, b, "down")
                dve.wait_ge(*acc_out(b, 1))
                link(dve.tensor_tensor(tmp[:, :, :], s0[:, :, :], gate[:, :, :], ALU.mult))
                dve.wait_ge(*stored(b, 0))
                dve.tensor_tensor(ost[:, :, :], tmp[:, :, :], x1[:, :, :], ALU.add).then_inc(ready, 1)
                assert own[0] == V_STEPS, own[0]

        @block.tensor
        def _(pe):
            def mm(o, lhsT, rhs, start=True, stop=True, **kw):
                return pe.matmul(o, lhsT, rhs, start=start, stop=stop, **kw)

            pe.wait_ge(loaded, 16 * 9)
            pe.wait_ge(pool_const, 4)
            pe.wait_ge(set_v, 2)
            mm(bank(0)[:, 0:2], ones[:, :], rsum[:, :]).then_inc(set_pe, 1)
            pe.wait_ge(set_v, 13)
            for k in range(3):
                n = min(P, FI - k * P)
                pe.transpose(bank(2 + k)[:, 0:P], wnat[:, 0, k, :], ident)
                pe.transpose(bank(2 + k)[:, P:2 * P], wnat[:, 1, k, :], ident)
                pe.transpose(bank(2 + k)[0:n, 2 * P:3 * P], wdn[:, k * P:k * P + n], ident).then_inc(set_pe, 1)
            pe.wait_ge(set_a, 5)

            def fold(index, i_wait):
                for k, name in enumerate(("G", "B")):
                    slot = 4 + k % 2 if index is None else 4 + (T_IDX[name] + 2) % 2
                    if index is not None:
                        pe.wait_ge(t_free, index * NT + T_IDX[name] + 2 - 1)
                    if k == 0:
                        pe.wait_ge(hw_in, i_wait)
                    mm(bank(slot)[:, 0:P], hw[:, 2 * k, :], hw[:, 2 * k + 1, :]).then_inc(t_full, 1)

            pe.wait_ge(set_v, 22)
            fold(None, 16)

            with pe.Fori(0, NB) as b:
                def begin(name):
                    k = JOB[name]
                    if k >= 4:
                        drained(pe, b, JOBS[k - 4][0])

                def end(ins):
                    ins.then_inc(filled.sem, 1)

                def transpose_tiles(name, src):
                    begin(name)
                    for t in range(T):
                        ins = pe.transpose(tiles(JOB[name])[:, t, :], src[:, t, :], ident)
                    end(ins)

                def wide(name, lhsT, rhs):
                    begin(name)
                    for a in range(2):
                        ins = mm(flat(JOB[name])[:, a * 512:(a + 1) * 512], lhsT, rhs[:, a * 512:(a + 1) * 512])
                    end(ins)

                pe.wait_ge(*xn_ready(b, 1))
                transpose_tiles("xnT", xn)
                pe.wait_ge(*xn_ready(b, 2))
                transpose_tiles("xaT", xa)
                drained(pe, b, "xaT")
                wide("qa", wts[:, W_QKVA:W_QKVA + C], xaT)
                wide("ka", wts[:, W_QKVA + C:W_QKVA + 2 * C], xaT)
                wide("qs", wts[:, W_QKVS:W_QKVS + C], xaT)
                wide("ks", wts[:, W_QKVS + C:W_QKVS + 2 * C], xaT)
                for k in range(2):
                    begin(f"v{k}")
                    for t in range(4 * k, 4 * k + 4):
                        for a, w in enumerate((W_QKVA, W_QKVS)):
                            at = (t % 4) * 2 * C + a * C
                            ins = mm(flat(JOB[f"v{k}"])[:, at:at + C], xaT[:, t * P:(t + 1) * P],
                                     wts[:, w + 2 * C:w + 3 * C])
                    end(ins)
                begin("ktok")
                pe.wait_ge(*feat(b, 2))
                for t in range(T):
                    ins = pe.transpose(tiles(JOB["ktok"])[:, t, :], kf[:, t * P:(t + 1) * P], ident)
                end(ins)
                pe.wait_ge(*feat(b, 3))
                wide("den", cst[:, C_BLK:C_BLK + P], z2)
                begin("kv")
                drained(pe, b, "ktok")
                drained(pe, b, "v1")
                for n in range(T - 1):
                    ins = mm(tiles(JOB["kv"])[:, n, :], ktok[:, n, :], val[:, n, C:2 * C])
                end(ins)
                begin("inter")
                pe.wait_ge(*states(b, 1))
                for n in range(1, T):
                    ins = mm(tiles(JOB["inter"])[:, n, :], state[:, n, :], qf[:, n * P:(n + 1) * P])
                end(ins)

                drained(pe, b, "kv")
                drained(pe, b, "inter")
                for s in range(4 * T + 3):
                    if s < 4 * T:
                        n, g = s // 4, s % 4
                        rows = slice(32 * g, 32 * g + 32)
                        if s >= 2:
                            pe.wait_ge(*win_exp(b, s - 1))
                        S = pair[s % 2][:, :, :].rearrange("p a n -> p (a n)").rearrange("p (j k) -> p j k", j=GH)
                        lo = (n - 1) * P if n else 0
                        for j in range(GH):
                            ins = mm(S[:, j, (0 if n else P):2 * P], qam[rows, n, j, :], kaT[rows, lo:(n + 1) * P])
                        ins.then_inc(win_scores.sem, 1)
                    t = s - 2
                    if 0 <= t < 4 * T:
                        pe.wait_ge(*win_norm(b, t + 1))
                        if t >= 2:
                            pe.wait_ge(*win_pt(b, t - 1))
                        for j in range(GH):
                            ins = pe.transpose(bank(4 + t % 2)[:, j * P:(j + 1) * P], pr[t % 3][:, j, :], ident)
                        ins.then_inc(win_tr.sem, 1)
                    u = s - 3
                    if 0 <= u < 4 * T:
                        n, g = u // 4, u % 4
                        pe.wait_ge(*win_pt(b, u + 1))
                        if g == 0 and n >= 2:
                            pe.wait_ge(*win_out(b, n - 1))
                        o = bank(6 + n % 2)[32 * g:32 * g + 32, :]
                        ch = slice(32 * g, 32 * g + 32)
                        ins = mm(o, val[:, n, ch], ptc[u % 2][:, :, :].rearrange("p j r -> p (j r)"), stop=(n == 0))
                        if n:
                            ins = mm(o, val[:, n - 1, ch], ptp[u % 2][:, :, :].rearrange("p j r -> p (j r)"), start=False)
                        ins.then_inc(win_pv.sem, 1)

                pe.wait_ge(*feat(b, 4))
                pe.wait_ge(*win_exp(b, 4 * T))
                for s in range(4 * T + 2):
                    if s < 4 * T:
                        n, g = s // 4, s % 4
                        rows = slice(32 * g, 32 * g + 32)
                        if s >= 4:
                            pe.wait_ge(*lin_am(b, s - 3))
                        mm(bank(s % 4), kf[rows, n * P:(n + 1) * P], qfm[rows, n, :, :].rearrange("p j r -> p (j r)"))\
                            .then_inc(lin_a.sem, 1)
                    u = s - 2
                    if 0 <= u:
                        n, g = u // 4, u % 4
                        pe.wait_ge(*lin_am(b, u + 1))
                        if g == 0:
                            pe.wait_ge(*(lin_out(b, n - 1) if n >= 2 else win_out(b, T - 1 + n)))
                        mm(bank(6 + n % 2)[32 * g:32 * g + 32, :], val[:, n, C + 32 * g:C + 32 * g + 32],
                           am[u % 3][:, :, :].rearrange("p j r -> p (j r)")).then_inc(lin_pv.sem, 1)

                pe.wait_ge(*lin_out(b, T))
                begin("sumT")
                for a in range(2):
                    at = slice(a * 512, (a + 1) * 512)
                    o = flat(JOB["sumT"])[:, at]
                    mm(o, wts[:, W_PA:W_PA + C], winT[:, at], stop=False)
                    ins = mm(o, wts[:, W_OS:W_OS + C], linT[:, at], start=False)
                end(ins)
                begin("mixed")
                drained(pe, b, "sumT")
                for t in range(T):
                    ins = mm(tiles(JOB["mixed"])[:, t, :], sumT[:, t * P:(t + 1) * P], wts[:, W_O:W_O + C])
                end(ins)
                pe.wait_ge(*xn_ready(b, 3))
                transpose_tiles("hT", xa)
                drained(pe, b, "hT")
                for f in range(FB):
                    wide(f"w1_{f}", wts[:, W_1 + f * P:W_1 + (f + 1) * P], xaT)
                begin("mlp")
                drained(pe, b, "w1_3")
                for t in range(T):
                    for f in range(FB):
                        ins = mm(tiles(JOB["mlp"])[:, t, :], h1T[:, f, t * P:(t + 1) * P],
                                 wts[:, W_2 + f * P:W_2 + (f + 1) * P], start=(f == 0), stop=(f == FB - 1))
                end(ins)
                drained(pe, b, "xnT")
                for k in range(FB):
                    begin(f"fc_{k}")
                    for t in (2 * k, 2 * k + 1):
                        ins = mm(bank(2 * (JOB[f"fc_{k}"] % 4) + t % 2), xnT[:, t * P:(t + 1) * P], wfc)
                    end(ins)
                for f in range(FB):
                    begin(f"fT_{f}")
                    pe.wait_ge(*hid_norm(b, T))
                    for t in range(T):
                        ins = pe.transpose(tiles(JOB[f"fT_{f}"])[:, t, :], hid[:, t, f * P:(f + 1) * P], ident)
                    end(ins)
                begin("ffn")
                drained(pe, b, "fT_3")
                for t in range(T):
                    for f in range(FB):
                        ins = mm(tiles(JOB["ffn"])[:, t, :], hidT[:, f, t * P:(t + 1) * P], wproj[:, f, :],
                                 start=(f == 0), stop=(f == FB - 1))
                end(ins)

                pe.wait_ge(*xn_ready(b, 4))
                transpose_tiles("x1T", xn)
                drained(pe, b, "x1T")
                drained(pe, b, "ffn")

                def use(i, u):
                    pe.wait_ge(u_free, i * NU + (2 + u - 1))

                def proj_y(i, first):
                    use(i, 0)
                    pe.wait_ge(t_free, i * NT + (2 if first else -2))
                    for a in range(2):
                        ins = mm(bank(a), G[:, :], xnT[:, a * 512:(a + 1) * 512])
                    ins.then_inc(u_full, 1)

                def proj_z(i, first):
                    use(i, 1)
                    pe.wait_ge(t_free, i * NT + (2 if first else -1))
                    for t in range(T):
                        ins = mm(tiles(1)[:, t, :], xnT[:, t * P:(t + 1) * P], Bv[:, :])
                    ins.then_inc(u_full, 1)

                def scores(i, q):
                    u = 2 + T - 1 - q
                    use(i, u)
                    if u == 2:
                        pe.wait_ge(u_free, i * NU + 3)
                    w = (q + 1) * P
                    S = flat(u % 2)
                    for at in range(0, w, 512):
                        end_ = min(w, at + 512)
                        mm(S[:, at:end_], yT[:, q * P:(q + 1) * P], xnT[:, at:end_])
                    mm(S[:, q * P:w], ident_b[:, :], causal_b[:, :], start=False, skip_group_check=True)\
                        .then_inc(u_full, 1)

                def transposes(i, q, before=False):
                    base = i - 1 if before else i
                    pe.wait_ge(l_norm, base * T + T - q)
                    for g, js in enumerate(groups_of(q)):
                        ti = T_IDX[q, g] + 2
                        pe.wait_ge(t_free, base * NT + ti - 1)
                        for n, j in enumerate(js):
                            ins = pe.transpose(bank(4 + ti % 2)[:, n * P:(n + 1) * P],
                                               pb[(T - 1 - q) % 4][:, j * P:(j + 1) * P], ident)
                        ins.then_inc(t_full, 1)

                def pv(i, q, first, before=False):
                    base = i - 1 if before else i
                    if q == T - 1:
                        pe.wait_ge(u_free, base * NU + 4)
                    for g, js in enumerate(groups_of(q)):
                        pi = PV_IDX[q, g]
                        pe.wait_ge(t_free, base * NT + T_IDX[q, g] + 2 + 1)
                        for n, j in enumerate(js):
                            ins = mm(tiles(3)[:, q, :], pt[pi % NPT][:, n, :], Z[:, j, :],
                                     start=(first and q in (3, 7) and j == 0), skip_group_check=True)
                        ins.then_inc(l_pv, 1)

                def l1_head(i, first):
                    proj_y(i, first)
                    if not first:
                        transposes(i, 1, True)
                        pv(i, 2, False, True)
                        transposes(i, 0, True)
                        pv(i, 1, False, True)
                    proj_z(i, first)
                    if not first:
                        pv(i, 0, False, True)
                    scores(i, 7)
                    scores(i, 6)
                    scores(i, 5)
                    transposes(i, 7)
                    scores(i, 4)
                    transposes(i, 6)
                    pv(i, 7, first)
                    for q in range(3, -1, -1):
                        scores(i, q)
                        if q == 0:
                            fold(i, i * 16 + 32)
                        transposes(i, q + 2)
                        pv(i, q + 3, first)

                l1_head(b * H1, True)
                with pe.Fori(1, H1) as h:
                    l1_head(b * H1 + h, False)
                end_i = (b + 1) * H1
                transposes(end_i, 1, True)
                pv(end_i, 2, False, True)
                transposes(end_i, 0, True)
                pv(end_i, 1, False, True)
                pv(end_i, 0, False, True)

                pe.wait_ge(*acc_out(b, 1))
                pe.wait_ge(t_free, end_i * NT + 2)
                pe.wait_ge(*xn_ready(b, 5))
                transpose_tiles("xqT", xa)
                drained(pe, b, "xqT")
                for t in range(T):
                    begin(f"gu_{t}")
                    for k in range(2):
                        ins = mm(bank(2 * (JOB[f"gu_{t}"] % 4) + k)[:, 0:FI], xaT[:, t * P:(t + 1) * P], wgT[:, k, :])
                    end(ins)
                pe.wait_ge(*hq_ready(b, 1))
                for k in range(3):
                    n = min(P, FI - k * P)
                    begin(f"hqT_{k}")
                    for t in range(T):
                        ins = pe.transpose(tiles(JOB[f"hqT_{k}"])[0:n, t, :], hq[:, t, k * P:k * P + n], ident)
                    end(ins)
                begin("down")
                drained(pe, b, "hqT_2")
                for t in range(T):
                    for k in range(3):
                        n = min(P, FI - k * P)
                        ins = mm(tiles(JOB["down"])[:, t, :], hqT[0:n, k, t * P:(t + 1) * P], wdT[0:n, k, :],
                                 start=(k == 0), stop=(k == 2))
                end(ins)
                drained(pe, b, "down")


def kernel(**inputs):
    import concourse.bacc as bacc
    from concourse.bass_utils import run_bass_kernel_spmd

    a = {k.removeprefix("L"): np.asarray(v) for k, v in inputs.items()}
    heads = lambda w: w.reshape(H1, E1, C)
    hw = np.stack([heads(a["1_attn_wq"]), heads(a["1_attn_wk"]), heads(a["1_attn_wv"]),
                   heads(a["1_attn_wo"].T)], axis=2)
    hw = np.concatenate([hw, hw[0:1]])
    blocks = lambda w: w.reshape(FB, P, C).transpose(1, 0, 2).reshape(P, FB * C)
    wtab = np.concatenate([
        a["0_attn_Wqkv_a"], a["0_attn_Wqkv_s"], a["0_attn_Wp_a"], a["0_attn_Wo_s"], a["0_attn_Wo"],
        a["0_attn_W1"], blocks(a["0_attn_W2"]), a["0_ffn_W_fc"].T, blocks(a["0_ffn_W_proj"].T)], axis=1)
    ba, bs = a["0_attn_bqkv_a"], a["0_attn_bqkv_s"]
    vtab = np.stack([a["0_attn_g1"], a["0_attn_b1"], ba[0:C], ba[C:2 * C], bs[0:C], bs[C:2 * C],
                     a["0_attn_bp_a"], a["0_attn_bo_s"], a["0_attn_gm"], a["0_attn_bm"],
                     *a["0_attn_b1m"].reshape(FB, P), *a["0_ffn_ln_w"].reshape(FB, P),
                     *a["0_ffn_ln_b"].reshape(FB, P)], axis=1)
    rtab = np.concatenate([ba[2 * C:], bs[2 * C:], a["0_attn_bo"], a["0_attn_b2m"]])

    p, f = np.arange(P)[:, None], np.arange(P)[None, :]
    one = np.float32(1)
    ctab = np.concatenate([
        (p == f) * one, (p <= f) * one, (p > f) * one, (f > p) * one, (p // E0 == f // E0) * one,
        (f > p) * np.float32(NEG),
        (p % 32 // E0 == f[:, 0:GH]) * one, (p % 32 // E0 == f[:, 0:GH]) * np.float32(WIN_SCALE)],
        axis=1).astype(np.float32)
    arrays = {"x": a["0_attn_x"], "head_w": hw, "wtab": wtab, "vtab": vtab, "rtab": rtab, "ctab": ctab,
              "w_gate": a["1_ffn_w_gate"], "w_up": a["1_ffn_w_up"], "w_down": a["1_ffn_w_down"]}
    arrays = {k: np.ascontiguousarray(v) for k, v in arrays.items()}
    nc = bacc.Bacc("TRN2", target_bir_lowering=False, num_devices=1)
    args = [nc.dram_tensor(k, v.shape, mybir.dt.from_np(v.dtype), kind="ExternalInput").ap()
            for k, v in arrays.items()]
    args.append(nc.dram_tensor("out", (NB, L, C), F32, kind="ExternalOutput").ap())
    program(nc, *args)
    r = run_bass_kernel_spmd(nc, [arrays], core_ids=[0])
    return r.results[0]["out"]
```

```python
from contextlib import ExitStack

import numpy as np

import concourse.bass as bass
from concourse import mybir

F32 = mybir.dt.float32
BF16 = mybir.dt.bfloat16
I32 = mybir.dt.int32
ALU = mybir.AluOpType
ACT = mybir.ActivationFunctionType
X = mybir.AxisListType.X

NB, L, C = 4, 1024, 128
P = 128
T = L // P
H0, E0 = 16, 8
GR, GH = 4, 4
H1, E1 = 16, 64
FF, FB = 512, 4
FI = 352
QB = 16
WIN_SCALE = float(np.float32(1) / np.sqrt(np.float32(E0)))
L1_SCALE = float(E1) ** -0.5
NEG = -1e30
LN_EPS = 1e-5

C_ID, C_KLE, C_KGT, C_JGT, C_BLK, C_CAUS, C_HM, C_HMS = 0, 128, 256, 384, 512, 640, 768, 772
C_N = 776
W_QKVA, W_QKVS, W_PA, W_OS, W_O, W_1, W_2, W_FC, W_PROJ = 0, 384, 768, 896, 1024, 1152, 1664, 2176, 2688
W_N = 3200
V_G1, V_B1, V_BQA, V_BKA, V_BQS, V_BKS, V_BPA, V_BOS, V_GM, V_BM, V_B1M, V_LNW, V_LNB = (
    0, 1, 2, 3, 4, 5, 6, 7, 8, 9, 10, 14, 18)
V_N = 22
R_BV, R_BO, R_B2 = 0, 256, 384
R_N = 512

JOBS = (
    [("xnT", "v", 0), ("xaT", "a", 1), ("qa", "a", 2), ("ka", "v", 3), ("qs", "v", 0), ("ks", "v", 1),
     ("v0", "v", 2), ("v1", "v", 3), ("ktok", "a", 0), ("den", "v", 1), ("kv", "v", 2), ("inter", "a", 3),
     ("sumT", "a", 0), ("fT_0", "a", 1), ("mixed", "v", 2), ("fT_1", "a", 3), ("fT_2", "a", 0), ("fT_3", "a", 1),
     ("ffn", "a", 3), ("hT", "a", 2)]
    + [(f"w1_{f}", "a", (0, 1, 3, 2)[f]) for f in range(FB)] + [("mlp", "v", 0)]
    + [("x1T", "v", 2), ("xqT", "v", 3)] + [(f"gu_{t}", "v", 2 + t % 2) for t in range(T)]
    + [(f"hqT_{k}", "a", k) for k in range(3)] + [("down", "a", 0)]
)
JOB = {name: k for k, (name, _, _) in enumerate(JOBS)}


def drained_count(k):
    return sum(1 for _, e, _ in JOBS[:k + 1] if e == JOBS[k][1])


def before_on_pair(k):
    return max((i for i in range(k) if JOBS[i][2] == JOBS[k][2]), default=None)


class Signal:

    def __init__(self, sem, per_seq, before=0):
        self.sem, self.per_seq, self.before = sem, per_seq, before

    def __call__(self, b, count):
        return self.sem, b * self.per_seq + (self.before + count)


def groups_of(i):
    return [range(0, min(4, i + 1))] + ([range(4, i + 1)] if i >= 4 else [])


ORDER = (4, 5, 1, 3, 6, 7, 0, 2)
T_LAG, PV_LAG = 3, 4
FOLD_AT = 6
T_IDX, PV_IDX = {}, {}
for _k, _q in enumerate(ORDER):
    if _k == FOLD_AT - T_LAG:
        T_IDX["G"] = len(T_IDX)
        T_IDX["B"] = len(T_IDX)
    for _g in range(len(groups_of(_q))):
        PV_IDX[_q, _g] = len(PV_IDX)
        T_IDX[_q, _g] = len(T_IDX)
NT, NPV = len(T_IDX), len(PV_IDX)
NPT = 4
USES = ("Y",) + ORDER[:2] + ("Z",) + ORDER[2:]
USE = {name: u for u, name in enumerate(USES)}
NU = len(USES)


def place_uses():
    size = [1 if name in range(4) else 2 for name in USES]
    last, first_bank = [-4, -3, -2, -1], []
    for u, n in enumerate(size):
        _, at = min((max(last[at:at + n]), at) for at in range(0, 4, n))
        first_bank.append(at)
        last[at:at + n] = [u] * n
    before = []
    last = [u - NU for u in last]
    for u, n in enumerate(size):
        at = first_bank[u]
        before.append(max(last[at:at + n]))
        last[at:at + n] = [u] * n
    return first_bank, before


USE_BANK, USE_BEFORE = place_uses()
V_STEPS = 114


def program(nc, x, head_w, wtab, vtab, rtab, ctab, w_gate, w_up, w_down, out):
    with ExitStack() as ctx:
        def sb(name, shape, dt=F32):
            return ctx.enter_context(nc.sbuf_tensor(name, shape, dt))

        def sem(name):
            return ctx.enter_context(nc.semaphore(name))

        def sig(name, per_seq, before=0):
            return Signal(sem(name), per_seq, before)

        cst = sb("cst", [P, C_N])
        wts = sb("wts", [P, W_N])
        vec = sb("vec", [P, V_N])
        row = sb("row", [P, R_N])
        ident = cst[:, C_ID:C_ID + P]
        hmask = cst[:, C_HM:C_HM + GH]
        hmask_s = cst[:, C_HMS:C_HMS + GH]
        ident_b = sb("ident_b", [P, P], BF16)
        causal_b = sb("causal_b", [P, P], BF16)
        neg = sb("neg", [P, P])
        mhalf = sb("mhalf", [P, T])
        bqa_m = sb("bqa_m", [P, GH])
        bqs_s = sb("bqs_s", [P, 1])
        bsum = sb("bsum", [P, 1])
        ones = sb("ones", [P, P])
        wfc = wts[:, W_FC:W_FC + FF]
        wproj = wts[:, W_PROJ:W_PROJ + FF].rearrange("p (f n) -> p f n", f=FB)
        rsum = sb("rsum", [P, 2])
        half = sb("half", [P, 4])
        wnat = sb("wnat", [P, 2, 3, P])
        wdn = sb("wdn", [P, FI])
        wgT = sb("wgT", [P, 2, FI])
        wdT = sb("wdT", [P, 3, P])

        xs = sb("xs", [P, T, C])
        xc = sb("xc", [P, T, C])
        xn = sb("xn", [P, T, C])
        xa = sb("xa", [P, T, C])
        tmp = sb("tmp", [P, T, C])
        st = sb("st", [P, 8, T])
        hst = sb("hst", [P, 5, T])
        xnT = sb("xnT", [P, L])
        xaT = sb("xaT", [P, L])
        big0 = sb("big0", [P, 4 * L])
        big1 = sb("big1", [P, 4 * L])
        qam = big0[:, :].rearrange("p (n j r) -> p n j r", n=T, j=GH)
        qfm = big1[:, :].rearrange("p (n j r) -> p n j r", n=T, j=GH)
        h1T = big0[:, :].rearrange("p (f r) -> p f r", f=FB)
        hid = big0[:, :].rearrange("p (t n) -> p t n", t=T)
        hidT = big1[:, :].rearrange("p (f r) -> p f r", f=FB)
        NQ = T * FI
        work = sb("work", [P, 4 * NQ])
        kaT, qf, kf, z0, z1, z2, z3, interT, ktok_, state_ = (work[:, k * L:(k + 1) * L] for k in range(10))
        ktok, state = (w.rearrange("p (t c) -> p t c", t=T) for w in (ktok_, state_))
        qa_, qz_, qy_, qs_ = (work[:, k * NQ:(k + 1) * NQ] for k in range(4))
        val = sb("val", [P, T, 2 * C])
        rdenT = sb("rdenT", [P, L])
        winT = sb("winT", [P, L])
        linT = sb("linT", [P, L])
        sumT = sb("sumT", [P, L])
        x1 = sb("x1", [P, T, C])
        s0 = sb("s0", [P, T, C])
        gate = sb("gate", [P, T, C])
        ost = sb("ost", [P, T, C])

        probs = sb("probs", [P, 12 * 512])
        quarter = [probs[:, k * 512:(k + 1) * 512].rearrange("p (j r) -> p j r", j=GH) for k in range(12)]
        pr, ptc, ptp, am, ext = quarter[0:3], quarter[3:5], quarter[5:7], quarter[7:10], quarter[10]
        h_sq = quarter[0:7] + quarter[11:12]
        nmx = sb("nmx", [P, 3, GH])
        den = sb("den", [P, 3, GH])
        rdn = sb("rdn", [P, 3, GH])
        red = sb("red", [P, P])
        poke = sb("poke", [P, 2])
        red2 = sb("red2", [P, P])

        hw = sb("hw", [E1, 4, C])
        G = sb("G", [P, P])
        Bv = sb("Bv", [P, P])
        yT = winT
        Z = linT[:, :].rearrange("p (t c) -> p t c", t=T)
        pb = [probs[:, k * L:(k + 1) * L] for k in range(4)]
        pt = quarter[8:8 + NPT]
        nm1 = sb("nm1", [P, T])
        dn1 = sb("dn1", [P, T])
        rd1 = sb("rd1", [P, T])

        qsc = sb("qsc", [P, 2, NQ // QB])
        hh = big0[:, 0:NQ].rearrange("p (t n) -> p t n", t=T)
        hq = big1[:, 0:NQ].rearrange("p (t n) -> p t n", t=T)
        sg = sb("sg", [P, 2, FI])
        hqT = big0[:, 0:3 * L].rearrange("p (k r) -> p k r", k=3)

        pair = [ctx.enter_context(nc.psum_tensor(f"pair{i}", [P, 2, 512], F32)) for i in range(4)]

        def flat(k):
            return pair[k][:, :, :].rearrange("p a n -> p (a n)")

        def tiles(k):
            return flat(k).rearrange("p (t n) -> p t n", n=P)

        def jflat(name):
            return flat(JOBS[JOB[name]][2])

        def jtiles(name):
            return tiles(JOBS[JOB[name]][2])

        def bank(n):
            return pair[n // 2][:, n % 2, :]

        def used(name):
            n = USE_BANK[USE[name]]
            return bank(n) if name in range(4) else flat(n // 2)

        loaded = sem("loaded")
        x_in = sig("x_in", 16)
        hw_in = sem("hw_in")
        stored = sig("stored", 16, 16)
        pool_const = sem("pool_const")
        filled = sig("filled", len(JOBS))
        by_v = sig("drained_by_vector", sum(e == "v" for _, e, _ in JOBS))
        by_a = sig("drained_by_scalar", sum(e == "a" for _, e, _ in JOBS))
        v_own = sem("v_own")
        stat_in = sig("stat_in", 5)
        rstd_out = sig("rstd_out", 5)
        xn_ready = sig("xn_ready", 5)
        feat_neg = sig("feat_neg", 2)
        feat_exp = sig("feat_exp", 2)
        feat = sig("features", 4)
        states = sig("states", 1)
        win_scores = sig("win_scores", 32)
        win_max = sig("win_max", 32)
        win_exp = sig("win_exp", 32)
        win_rden = sig("win_rden", 32)
        win_norm = sig("win_norm", 32)
        win_tr = sig("win_tr", 32)
        win_pt = sig("win_pt", 32)
        win_pv = sig("win_pv", 32)
        win_out = sig("win_out", T)
        lin_a = sig("lin_a", 32)
        lin_am = sig("lin_am", 32)
        lin_pv = sig("lin_pv", 32)
        lin_out = sig("lin_out", T)
        fc_full = sig("fc_filled", T)
        fc_gelu = sig("fc_gelu", T)
        hid_mean = sig("hid_mean", 1)
        hid_sq = sig("hid_squares", 1)
        hid_norm = sig("hid_norm", T)
        up_done = sig("up_silu", T)
        u_full = sem("l1_use_filled")
        u_free = sem("l1_use_drained")
        l_max = sem("l1_max")
        l_norm = sem("l1_norm")
        t_full = sem("l1_tr_filled")
        t_free = sem("l1_tr_drained")
        l_pv = sem("l1_pv")
        acc_out = sig("l1_out", 1)
        l_own = sem("l1_v_own")
        hq_ready = sig("hq_ready", 1)
        fsign = sig("fp4_sign", 2)
        fscale = sig("fp4_scale", 1)
        p_own = sig("pool_own", 15)
        set_pe = sem("setup_pe")
        set_v = sem("setup_v")
        set_a = sem("setup_a")
        ready = sem("result_ready")

        block = ctx.enter_context(nc.Block())

        def drained(eng, b, name):
            k = JOB[name]
            eng.wait_ge(*(by_v if JOBS[k][1] == "v" else by_a)(b, drained_count(k)))

        @block.sync
        def _(sp):
            sp.sem_inc(stored.sem, 16)
            sp.dma_start(cst[:, :], ctab).then_inc(loaded, 16)
            sp.dma_start(wts[:, :], wtab).then_inc(loaded, 16)
            sp.dma_start(vec[:, :], vtab).then_inc(loaded, 16)
            sp.dma_start(row[:, :], rtab.partition_broadcast(P)).then_inc(loaded, 16)
            sp.wait_ge(pool_const, 1)
            for k, w in enumerate((w_gate, w_up)):
                sp.dma_start(wnat[:, k, 0:2, :], w[0:2 * P, :].rearrange("(t p) c -> p t c", p=P)).then_inc(loaded, 16)
                sp.dma_start(wnat[0:FI - 2 * P, k, 2, :], w[2 * P:FI, :]).then_inc(loaded, 16)
            sp.dma_start(wdn[:, :], w_down).then_inc(loaded, 16)
            sp.dma_start(hw[:, :, :], head_w[0]).then_inc(hw_in, 16)

            def load_x(b):
                sp.dma_start(xs[:, :, :], x[b].rearrange("(t p) c -> p t c", p=P)).then_inc(x_in.sem, 16)

            def sequence(b, last):
                if not last:
                    sp.wait_ge(*xn_ready(b, 4))
                    load_x(b + 1)
                with sp.Fori(0, H1) as h:
                    sp.wait_ge(t_full, b * (H1 * NT) + h * NT + 2)
                    sp.dma_start(hw[:, :, :], head_w[h + 1]).then_inc(hw_in, 16)
                sp.wait_ge(ready, b + 1)
                sp.dma_start(out[b].rearrange("(t p) c -> p t c", p=P), ost[:, :, :]).then_inc(stored.sem, 16)

            load_x(0)
            with sp.Fori(0, NB - 1) as b:
                sequence(b, False)
            sequence(NB - 1, True)
            sp.wait_ge(*stored(NB - 1, 16))
            sp.wait_ge(hw_in, 16 * (NB * H1 + 1))

        @block.gpsimd
        def _(pool):
            pool.memset(wnat[:, :, 2, :], 0.0).then_inc(pool_const, 1)
            pool.memset(mhalf[:, :], -0.5).then_inc(pool_const, 1)
            pool.memset(ones[:, :], 1.0).then_inc(pool_const, 1)
            pool.memset(neg[:, :], NEG).then_inc(pool_const, 1)
            pool.wait_ge(pool_const, 4)

            with pool.Fori(0, NB) as b:
                def rstd(k, dst, src):
                    pool.wait_ge(*stat_in(b, k + 1))
                    pool.tensor_tensor(dst, src, mhalf[:, :], ALU.pow).then_inc(rstd_out.sem, 1)

                steps = [0]

                def step(ins):
                    steps[0] += 1
                    ins.then_inc(p_own.sem, 1)

                def link(ins):
                    step(ins)
                    pool.wait_ge(*p_own(b, steps[0]))

                rstd(0, st[:, 3, :], st[:, 2, :])
                rstd(1, st[:, 5, :], st[:, 4, :])
                for s in range(4 * T):
                    pool.wait_ge(*win_rden(b, s + 1))
                    p = pr[s % 3]
                    pool.tensor_tensor(p[:, :, :], p[:, :, :],
                                       rdn[:, s % 3, :].unsqueeze(2).broadcast_to([P, GH, P]),
                                       ALU.mult).then_inc(win_norm.sem, 1)
                rstd(2, hst[:, 4, :], hst[:, 3, :])
                for k in range(3, 5):
                    rstd(k, st[:, 3, :], st[:, 2, :])

                b3 = lambda ap: ap.rearrange("p (n q) -> p n q", q=QB)
                scale = lambda k: qsc[:, k, :].unsqueeze(2).broadcast_to([P, NQ // QB, QB])
                pool.wait_ge(*fsign(b, 2))
                pool.wait_ge(*fscale(b, 1))
                hq_ = hq.rearrange("p t n -> p (t n)")
                z = (qz_, hq_)
                midpoints = ((0.75, 1.0), (1.25, 1.0), (1.75, 1.0), (2.5, 2.0), (3.5, 2.0), (5.0, 4.0))

                def over(k):
                    mid, half_steps = midpoints[k]
                    step(pool.tensor_scalar(z[k % 2], qa_, mid, half_steps, ALU.is_gt, ALU.mult))

                link(pool.tensor_tensor(b3(qa_), b3(qa_), scale(1), ALU.mult))
                step(pool.tensor_tensor(b3(qs_), b3(qs_), scale(0), ALU.mult))
                step(pool.tensor_scalar(qy_, qa_, 0.25, None, ALU.is_gt))
                over(0)
                for k in range(len(midpoints)):
                    pool.wait_ge(*p_own(b, steps[0]))
                    step(pool.tensor_tensor(qy_, qy_, z[k % 2], ALU.add))
                    if k + 1 < len(midpoints):
                        over(k + 1)
                pool.wait_ge(*p_own(b, steps[0]))
                pool.tensor_tensor(hq_, qy_, qs_, ALU.mult).then_inc(hq_ready.sem, 1)
                assert steps[0] == p_own.per_seq, steps

        @block.scalar
        def _(act):
            act.wait_ge(loaded, 16 * 9)
            for dst, src in ((ident_b, C_ID), (causal_b, C_CAUS)):
                act.activation(dst[:, :], cst[:, src:src + P], ACT.Copy).then_inc(set_a, 1)
            for k in range(2):
                act.activation(qs_[:, k * 3 * P:(k + 1) * 3 * P], wnat[:, k, :, :].rearrange("p t c -> p (t c)"),
                               ACT.Sign).then_inc(set_a, 1)
            act.activation(qs_[:, 6 * P:6 * P + FI], wdn[:, :], ACT.Sign).then_inc(set_a, 1)
            act.wait_ge(set_v, 10)
            act.sem_inc(u_free, NU)

            with act.Fori(0, NB) as b:
                def full(name):
                    act.wait_ge(*filled(b, JOB[name] + 1))

                full("xaT")
                act.activation(xaT[:, :], jflat("xaT"), ACT.Identity, bias=vec[:, V_B1:V_B1 + 1],
                               scale=vec[:, V_G1:V_G1 + 1]).then_inc(by_a.sem, 1)
                full("qa")
                for j in range(GH):
                    ins = act.activation(qam[:, :, j, :], jtiles("qa"), ACT.Identity, bias=bqa_m[:, j:j + 1],
                                         scale=hmask_s[:, j:j + 1])
                ins.then_inc(by_a.sem, 1)
                for k, zz in ((0, z0), (1, z2)):
                    act.wait_ge(*feat_neg(b, k + 1))
                    act.activation(zz[:, :], zz[:, :], ACT.Exp).then_inc(feat_exp.sem, 1)
                full("ktok")
                act.activation(ktok[:, :, :], jtiles("ktok"), ACT.Copy).then_inc(by_a.sem, 1)
                full("inter")
                act.activation(interT[:, P:L], jflat("inter")[:, P:L], ACT.Copy).then_inc(by_a.sem, 1)

                for s in range(4 * T):
                    act.wait_ge(*win_max(b, s + 1))
                    if s >= 3:
                        act.wait_ge(*win_tr(b, s - 2))
                    S = pair[s % 2][:, :, :].rearrange("p a n -> p (a n)").rearrange("p (j k) -> p j k", j=GH)
                    for j in range(GH):
                        ins = act.activation(pr[s % 3][:, j, :], S[:, j, P:2 * P], ACT.Exp,
                                             bias=nmx[:, s % 3, j:j + 1], accum_out=den[:, s % 3, j:j + 1])
                    ins.then_inc(win_exp.sem, 1)

                for t in range(T):
                    act.wait_ge(*fc_full(b, t + 1))
                    act.activation(hid[:, t, :], bank(4 + t % 2), ACT.Gelu, accum_out=hst[:, 0, t:t + 1])\
                       .then_inc(fc_gelu.sem, 1)
                act.wait_ge(*hid_mean(b, 1))
                for t in range(T):
                    ins = act.activation(h_sq[t].rearrange("p j r -> p (j r)"), hid[:, t, :], ACT.Square, bias=hst[:, 1, t:t + 1],
                                         accum_out=hst[:, 2, t:t + 1])
                ins.then_inc(hid_sq.sem, 1)

                def drain_fT(f):
                    full(f"fT_{f}")
                    act.activation(hidT[:, f, :], jflat(f"fT_{f}"), ACT.Identity,
                                   bias=vec[:, V_LNB + f:V_LNB + f + 1],
                                   scale=vec[:, V_LNW + f:V_LNW + f + 1]).then_inc(by_a.sem, 1)

                full("sumT")
                act.activation(sumT[:, :], jflat("sumT"), ACT.Identity, bias=bsum[:, 0:1]).then_inc(by_a.sem, 1)
                for f in range(FB):
                    drain_fT(f)
                full("ffn")
                act.activation(gate[:, :, :], jtiles("ffn"), ACT.Silu).then_inc(by_a.sem, 1)
                full("hT")
                act.activation(xaT[:, :], jflat("hT"), ACT.Identity, bias=vec[:, V_BM:V_BM + 1],
                               scale=vec[:, V_GM:V_GM + 1]).then_inc(by_a.sem, 1)
                for f in range(FB):
                    full(f"w1_{f}")
                    act.activation(h1T[:, f, :], jflat(f"w1_{f}"), ACT.Gelu,
                                   bias=vec[:, V_B1M + f:V_B1M + f + 1]).then_inc(by_a.sem, 1)
                def gate_and_up():
                    for t in range(T):
                        full(f"gu_{t}")
                        if t >= 2:
                            act.wait_ge(*by_v(b, drained_count(JOB[f"gu_{t - 2}"])))
                        act.activation(sg[:, t % 2, :], jflat(f"gu_{t}")[:, 0:FI], ACT.Silu).then_inc(up_done.sem, 1)
                    act.wait_ge(*by_v(b, drained_count(JOB[f"gu_{T - 1}"])))
                    hidden = hh.rearrange("p t n -> p (t n)")
                    act.activation(qa_[:, :], hidden, ACT.Abs)
                    act.activation(qs_[:, :], hidden, ACT.Sign).then_inc(fsign.sem, 1)

                act.wait_ge(*xn_ready(b, 4))
                act.activation(qs_[:, 0:L], xn[:, :, :].rearrange("p t c -> p (t c)"), ACT.Sign)\
                   .then_inc(fsign.sem, 1)

                def l1_head(i, first):
                    for u, use in enumerate(USES):
                        if use == "Y":
                            act.wait_ge(u_full, i * NU + u + 1)
                            act.activation(yT[:, :], used("Y"), ACT.Copy, scale=L1_SCALE).then_inc(u_free, 1)
                        elif use == "Z":
                            if first:
                                gate_and_up()
                            act.wait_ge(u_full, i * NU + u + 1)
                            if not first:
                                act.wait_ge(l_pv, i * NPV)
                            act.activation(Z[:, :, :].rearrange("p t c -> p (t c)"), used("Z"), ACT.Copy)\
                               .then_inc(u_free, 1)
                        else:
                            k, w = ORDER.index(use), (use + 1) * P
                            act.wait_ge(l_max, i * T + k + 1)
                            act.activation(pb[k % 4][:, 0:w], used(use)[:, 0:w], ACT.Exp,
                                           bias=nm1[:, use:use + 1], accum_out=dn1[:, use:use + 1])\
                               .then_inc(u_free, 1)

                l1_head(b * H1, True)
                with act.Fori(1, H1) as h:
                    l1_head(b * H1 + h, False)

                for k in range(3):
                    n = min(P, FI - k * P)
                    full(f"hqT_{k}")
                    act.activation(hqT[0:n, k, :], jflat(f"hqT_{k}")[0:n, :], ACT.Copy).then_inc(by_a.sem, 1)
                full("down")
                act.activation(gate[:, :, :], jtiles("down"), ACT.Silu).then_inc(by_a.sem, 1)

        @block.vector
        def _(dve):
            own = [0]

            def bc(ap, n):
                return ap.unsqueeze(2).broadcast_to([P, ap.shape[1], n])

            def bcm(ap, n):
                return ap.unsqueeze(1).broadcast_to([P, n, ap.shape[1]])

            def fp4(link, src, dst, sgn, nblk):
                a = qa_[:, 0:nblk * QB]
                z = qz_[:, 0:nblk * QB]
                y = qy_[:, 0:nblk * QB]
                sc, rs = qsc[:, 0, 0:nblk], qsc[:, 1, 0:nblk]
                b3 = lambda ap: ap.rearrange("p (n q) -> p n q", q=QB)
                link(dve.tensor_reduce(sc, b3(src), X, ALU.max, apply_absolute_value=True))
                link(dve.tensor_scalar(sc, sc, 1.0 / 6.0, 1e-12, ALU.mult, ALU.max))
                link(dve.reciprocal(rs, sc))
                link(dve.tensor_tensor(b3(y), b3(src), bc(rs, QB), ALU.mult))
                link(dve.scalar_tensor_tensor(a, y, -1.0, y, ALU.mult, ALU.max))
                link(dve.tensor_scalar(z, a, 5.0, 2.0, ALU.is_gt, ALU.mult))
                link(dve.scalar_tensor_tensor(y, a, 3.5, z, ALU.is_gt, ALU.add))
                link(dve.scalar_tensor_tensor(z, a, 2.5, y, ALU.is_gt, ALU.add))
                link(dve.tensor_scalar(y, z, 2.0, None, ALU.mult))
                link(dve.scalar_tensor_tensor(z, a, 1.75, y, ALU.is_gt, ALU.add))
                link(dve.scalar_tensor_tensor(y, a, 1.25, z, ALU.is_gt, ALU.add))
                link(dve.scalar_tensor_tensor(z, a, 0.75, y, ALU.is_gt, ALU.add))
                link(dve.scalar_tensor_tensor(y, a, 0.25, z, ALU.is_gt, ALU.add))
                link(dve.scalar_tensor_tensor(b3(z), b3(sgn), 0.5, bc(sc, QB), ALU.mult, ALU.mult))
                return dve.tensor_tensor(dst, y, z, ALU.mult)

            def slink(ins):
                own[0] += 1
                ins.then_inc(v_own, 1)
                dve.wait_ge(v_own, own[0])

            dve.wait_ge(loaded, 16 * 9)
            dve.wait_ge(pool_const, 4)
            for k, w in enumerate((W_FC, W_PROJ)):
                dve.tensor_reduce(rsum[:, k:k + 1], wts[:, w:w + FF], X, ALU.add, apply_absolute_value=True)\
                   .then_inc(set_v, 1)
            dve.wait_ge(set_pe, 1)
            slink(dve.tensor_scalar(half[:, 0:2], bank(0)[:, 0:2], 1.0 / (FF * C), 1e-6, ALU.mult, ALU.add))
            slink(dve.tensor_scalar(half[:, 2:4], half[:, 0:2], -0.5, None, ALU.mult))
            slink(dve.tensor_scalar(half[:, 0:2], half[:, 0:2], 0.5, None, ALU.mult))
            for k, w in enumerate((W_FC, W_PROJ)):
                m = wts[:, w:w + FF]
                slink(dve.tensor_scalar(qa_[:, 0:FF], m, half[:, 2 + k:3 + k], None, ALU.is_lt))
                slink(dve.scalar_tensor_tensor(qz_[:, 0:FF], m, half[:, k:k + 1], qa_[:, 0:FF], ALU.is_gt, ALU.subtract))
                dve.tensor_copy(m, qz_[:, 0:FF]).then_inc(set_v, 1)
                dve.wait_ge(set_v, 3 + k)
            for j in range(GH):
                dve.tensor_tensor(bqa_m[:, j:j + 1], hmask_s[:, j:j + 1], vec[:, V_BQA:V_BQA + 1], ALU.mult)\
                   .then_inc(set_v, 1)
            dve.tensor_scalar(bqs_s[:, :], vec[:, V_BQS:V_BQS + 1], WIN_SCALE, None, ALU.mult).then_inc(set_v, 1)
            dve.tensor_tensor(bsum[:, :], vec[:, V_BPA:V_BPA + 1], vec[:, V_BOS:V_BOS + 1], ALU.add).then_inc(set_v, 1)
            dve.wait_ge(set_a, 5)
            for k in range(2):
                src = wnat[:, k, :, :].rearrange("p t c -> p (t c)")
                fp4(slink, src, src, qs_[:, k * 3 * P:(k + 1) * 3 * P], 3 * P // QB).then_inc(set_v, 1)
                dve.wait_ge(set_v, 11 + k)
            fp4(slink, wdn[:, :], wdn[:, :], qs_[:, 6 * P:6 * P + FI], FI // QB).then_inc(set_v, 1)
            for k in range(3):
                dve.wait_ge(set_pe, 2 + k)
                n = min(P, FI - k * P)
                dve.tensor_copy(wgT[:, 0, k * P:k * P + n], bank(2 + k)[:, 0:n]).then_inc(set_v, 1)
                dve.tensor_copy(wgT[:, 1, k * P:k * P + n], bank(2 + k)[:, P:P + n]).then_inc(set_v, 1)
                dve.tensor_copy(wdT[0:n, k, :], bank(2 + k)[0:n, 2 * P:3 * P]).then_inc(set_v, 1)
            dve.wait_ge(t_full, 1)
            dve.tensor_copy(G[:, :], bank(4)[:, 0:P]).then_inc(t_free, 1)
            dve.wait_ge(t_full, 2)
            dve.tensor_copy(Bv[:, :], bank(5)[:, 0:P]).then_inc(t_free, 1)
            setup_steps = own[0]

            with dve.Fori(0, NB) as b:
                own[0] = 0

                def link(ins):
                    own[0] += 1
                    ins.then_inc(v_own, 1)
                    dve.wait_ge(v_own, b * V_STEPS + (setup_steps + own[0]))

                def full(name):
                    dve.wait_ge(*filled(b, JOB[name] + 1))

                def center(k, src):
                    link(dve.tensor_reduce(st[:, 0, :], src, X, ALU.add))
                    link(dve.tensor_scalar(st[:, 1, :], st[:, 0, :], -1.0 / C, None, ALU.mult))
                    link(dve.tensor_tensor(xc[:, :, :], src, bc(st[:, 1, :], C), ALU.add))
                    link(dve.tensor_tensor(tmp[:, :, :], xc[:, :, :], xc[:, :, :], ALU.mult))
                    link(dve.tensor_reduce(st[:, 6, :], tmp[:, :, :], X, ALU.add))
                    dve.tensor_scalar(st[:, 2, :], st[:, 6, :], 1.0 / C, LN_EPS, ALU.mult, ALU.add)\
                       .then_inc(stat_in.sem, 1)
                    dve.wait_ge(*rstd_out(b, k + 1))

                dve.wait_ge(*x_in(b, 16))
                center(0, xs[:, :, :])
                dve.tensor_tensor(xn[:, :, :], xc[:, :, :], bc(st[:, 3, :], C), ALU.mult).then_inc(xn_ready.sem, 1)
                link(dve.tensor_tensor(st[:, 1, :], st[:, 3, :], st[:, 3, :], ALU.mult))
                link(dve.scalar_tensor_tensor(st[:, 7, :], st[:, 6, :], 1.0 / C, st[:, 1, :], ALU.mult, ALU.mult))
                dve.tensor_scalar(st[:, 4, :], st[:, 7, :], LN_EPS, None, ALU.add).then_inc(stat_in.sem, 1)
                dve.wait_ge(*rstd_out(b, 2))
                dve.wait_ge(*xn_ready(b, 1))
                dve.tensor_tensor(xa[:, :, :], xn[:, :, :], bc(st[:, 5, :], C), ALU.mult).then_inc(xn_ready.sem, 1)

                full("xnT")
                dve.tensor_copy(xnT[:, :], jflat("xnT")).then_inc(by_v.sem, 1)
                full("ka")
                dve.tensor_scalar(kaT[:, :], jflat("ka"), vec[:, V_BKA:V_BKA + 1], None, ALU.add)\
                   .then_inc(by_v.sem, 1)

                full("qs")
                dve.tensor_scalar(z1[:, :], jflat("qs"), WIN_SCALE, bqs_s[:, 0:1], ALU.mult, ALU.add)\
                   .then_inc(by_v.sem, 1)
                full("ks")
                dve.tensor_scalar(z3[:, :], jflat("ks"), vec[:, V_BKS:V_BKS + 1], None, ALU.add)\
                   .then_inc(by_v.sem, 1)
                drained(dve, b, "ks")
                for zz, neg_part in ((z1, z0), (z3, z2)):
                    dve.tensor_scalar(neg_part[:, :], zz[:, :], 0.0, None, ALU.min).then_inc(feat_neg.sem, 1)
                for k in range(2):
                    full(f"v{k}")
                    dve.tensor_tensor(val[:, 4 * k:4 * k + 4, :],
                                      jflat(f"v{k}").rearrange("p (t n) -> p t n", n=2 * C),
                                      bcm(row[:, R_BV:R_BV + 2 * C], 4), ALU.add).then_inc(by_v.sem, 1)
                for k, (zz, ee, ff) in enumerate(((z1, z0, qf), (z3, z2, kf))):
                    dve.wait_ge(*feat_exp(b, k + 1))
                    link(dve.scalar_tensor_tensor(zz[:, :], zz[:, :], 0.0, ee[:, :], ALU.max, ALU.add))
                    dve.tensor_scalar(ff[:, :], zz[:, :], 0.0001, None, ALU.add).then_inc(feat.sem, 1)
                dve.wait_ge(*feat(b, 2))
                link(dve.tensor_tensor_scan(z0[:, :], kf[:, :], kf[:, :], 0.0, ALU.add, ALU.bypass))
                dve.tensor_tensor(z2[:, :], z0[:, :], qf[:, :], ALU.mult).then_inc(feat.sem, 1)
                for j in range(GH):
                    ins = dve.tensor_scalar(qfm[:, :, j, :], qf[:, :].rearrange("p (n r) -> p n r", n=T),
                                            hmask[:, j:j + 1], None, ALU.mult)
                ins.then_inc(feat.sem, 1)
                full("den")
                link(dve.tensor_scalar(z1[:, :], jflat("den"), 1e-6, None, ALU.add))
                dve.reciprocal(rdenT[:, :], z1[:, :]).then_inc(by_v.sem, 1)
                full("kv")
                dve.tensor_tensor(tmp[:, 0:T - 1, :], jtiles("kv")[:, 0:T - 1, :],
                                  bcm(cst[:, C_BLK:C_BLK + P], T - 1), ALU.mult).then_inc(by_v.sem, 1)
                drained(dve, b, "kv")
                link(dve.tensor_copy(state[:, 1, :], tmp[:, 0, :]))
                for n in range(2, T):
                    ins = dve.tensor_tensor(state[:, n, :], state[:, n - 1, :], tmp[:, n - 1, :], ALU.add)
                    if n < T - 1:
                        link(ins)
                ins.then_inc(states.sem, 1)

                def scores_there(s):
                    dve.wait_ge(*win_scores(b, s + 1))

                def win_front(s):
                    n = s // 4
                    S = pair[s % 2][:, :, :].rearrange("p a n -> p (a n)").rearrange("p (j k) -> p j k", j=GH)
                    if s < 2:
                        scores_there(s)
                        own[0] += 1
                        dve.memset(poke[:, s:s + 1], 0.0).then_inc(v_own, 1)
                    before = S[:, :, 0:P] if n else bcm(neg[:, :], GH)
                    link(dve.copy_predicated(S[:, :, P:2 * P], bcm(cst[:, C_JGT:C_JGT + P].bitcast(I32), GH), before))
                    dve.tensor_reduce(nmx[:, s % 3, :], S[:, :, P:2 * P], X, ALU.max, negate=True)\
                       .then_inc(win_max.sem, 1)

                def win_recip(s):
                    dve.wait_ge(*win_exp(b, s + 1))
                    dve.reciprocal(rdn[:, s % 3, :], den[:, s % 3, :]).then_inc(win_rden.sem, 1)

                def win_evac(s):
                    dve.wait_ge(*win_tr(b, s + 1))
                    if s >= 2:
                        dve.wait_ge(*win_pv(b, s - 1))
                    t = bank(4 + s % 2).rearrange("p (j r) -> p j r", j=GH)
                    dve.tensor_tensor(ptp[s % 2][:, :, :], t, bcm(cst[:, C_KGT:C_KGT + P], GH), ALU.mult)
                    if s + 2 < 4 * T:
                        scores_there(s + 2)
                    dve.tensor_tensor(ptc[s % 2][:, :, :], t, bcm(cst[:, C_KLE:C_KLE + P], GH), ALU.mult)\
                       .then_inc(win_pt.sem, 1)

                def pick(n):
                    link(dve.tensor_tensor(ext[:, :, :], bank(6 + n % 2).rearrange("p (j r) -> p j r", j=GH),
                                           bc(hmask, P), ALU.mult))
                    return ext[:, :, :].rearrange("p j r -> p r j")

                def win_extract(n):
                    dve.wait_ge(*win_pv(b, 4 * n + 4))
                    dve.tensor_reduce(winT[:, n * P:(n + 1) * P], pick(n), X, ALU.add).then_inc(win_out.sem, 1)

                for s in range(4 * T + 4):
                    if 1 <= s <= 4 * T:
                        win_recip(s - 1)
                    if 2 <= s < 4 * T + 2:
                        win_evac(s - 2)
                    if s < 4 * T:
                        win_front(s)
                    if s >= 4 and s % 4 == 3 and s < 4 * T + 4 and s // 4 - 1 < T:
                        win_extract(s // 4 - 1)

                def lin_evac(s):
                    dve.wait_ge(*lin_a(b, s + 1))
                    if s >= 3:
                        dve.wait_ge(*lin_pv(b, s - 2))
                    dve.tensor_tensor(am[s % 3][:, :, :], bank(s % 4).rearrange("p (j r) -> p j r", j=GH),
                                      bcm(cst[:, C_KLE:C_KLE + P], GH), ALU.mult).then_inc(lin_am.sem, 1)

                def lin_extract(n):
                    at = slice(n * P, (n + 1) * P)
                    dve.wait_ge(*lin_pv(b, 4 * n + 4))
                    link(dve.tensor_reduce(red[:, :], pick(n), X, ALU.add))
                    src = red
                    if n:
                        link(dve.tensor_tensor(red2[:, :], red[:, :], interT[:, at], ALU.add))
                        src = red2
                    dve.tensor_tensor(linT[:, at], src[:, :], rdenT[:, at], ALU.mult).then_inc(lin_out.sem, 1)

                drained(dve, b, "inter")
                for s in range(4 * T + 3):
                    if s < 4 * T:
                        lin_evac(s)
                    if s >= 6 and s % 4 == 2 and s // 4 - 1 < T:
                        lin_extract(s // 4 - 1)
                    if s == 13:
                        dve.wait_ge(*fc_gelu(b, T))
                        dve.tensor_scalar(hst[:, 1, :], hst[:, 0, :], -1.0 / FF, None, ALU.mult)\
                           .then_inc(hid_mean.sem, 1)
                    if s == 19:
                        dve.wait_ge(*hid_sq(b, 1))
                        dve.tensor_scalar(hst[:, 3, :], hst[:, 2, :], 1.0 / FF, LN_EPS, ALU.mult, ALU.add)\
                           .then_inc(stat_in.sem, 1)
                    if s == 21:
                        dve.wait_ge(*rstd_out(b, 3))
                    if 21 <= s < 21 + T:
                        t = s - 21
                        dve.tensor_scalar(hid[:, t, :], hid[:, t, :], hst[:, 1, t:t + 1], hst[:, 4, t:t + 1],
                                          ALU.add, ALU.mult).then_inc(hid_norm.sem, 1)

                full("mixed")
                dve.tensor_tensor(tmp[:, :, :], jtiles("mixed"), xn[:, :, :], ALU.add).then_inc(by_v.sem, 1)
                drained(dve, b, "mixed")
                link(dve.tensor_tensor(s0[:, :, :], tmp[:, :, :], bcm(row[:, R_BO:R_BO + C], T), ALU.add))
                center(3, s0[:, :, :])
                dve.tensor_tensor(xa[:, :, :], xc[:, :, :], bc(st[:, 3, :], C), ALU.mult).then_inc(xn_ready.sem, 1)
                link(dve.tensor_tensor(s0[:, :, :], s0[:, :, :], bcm(row[:, R_B2:R_B2 + C], T), ALU.add))
                full("mlp")
                dve.tensor_tensor(s0[:, :, :], jtiles("mlp"), s0[:, :, :], ALU.add).then_inc(by_v.sem, 1)
                drained(dve, b, "ffn")
                drained(dve, b, "mlp")
                link(dve.tensor_tensor(tmp[:, :, :], s0[:, :, :], gate[:, :, :], ALU.mult))
                link(dve.tensor_tensor(x1[:, :, :], tmp[:, :, :], xs[:, :, :], ALU.add))

                center(4, x1[:, :, :])
                dve.tensor_tensor(xn[:, :, :], xc[:, :, :], bc(st[:, 3, :], C), ALU.mult).then_inc(xn_ready.sem, 1)
                dve.wait_ge(*xn_ready(b, 4))
                full("x1T")
                dve.tensor_copy(xnT[:, :], jflat("x1T")).then_inc(by_v.sem, 1)

                dve.wait_ge(*fsign(b, 1))
                fp4(link, xn[:, :, :].rearrange("p t c -> p (t c)"), xa[:, :, :].rearrange("p t c -> p (t c)"),
                    qs_[:, 0:L], L // QB).then_inc(xn_ready.sem, 1)

                def gate_and_up():
                    full("xqT")
                    dve.tensor_copy(xaT[:, :], jflat("xqT")).then_inc(by_v.sem, 1)
                    for t in range(T):
                        dve.wait_ge(*up_done(b, t + 1))
                        dve.tensor_tensor(hh[:, t, :], jflat(f"gu_{t}")[:, 512:512 + FI], sg[:, t % 2, :],
                                          ALU.mult).then_inc(by_v.sem, 1)
                    drained(dve, b, f"gu_{T - 1}")

                def l_front(i, k):
                    q = ORDER[k]
                    dve.wait_ge(u_full, i * NU + USE[q] + 1)
                    dve.tensor_reduce(nm1[:, q:q + 1], used(q)[:, 0:(q + 1) * P], X, ALU.max, negate=True)\
                       .then_inc(l_max, 1)

                def l_normalize(i, k):
                    q, w = ORDER[k], (ORDER[k] + 1) * P
                    dve.wait_ge(u_free, i * NU + (NU + USE[q] + 1))
                    dve.reciprocal(rd1[:, q:q + 1], dn1[:, q:q + 1]).then_inc(l_own, 1)
                    dve.wait_ge(l_own, i * T + k + 1)
                    dve.tensor_scalar(pb[k % 4][:, 0:w], pb[k % 4][:, 0:w], rd1[:, q:q + 1], None, ALU.mult)\
                       .then_inc(l_norm, 1)

                def l_evac(i, k, first):
                    q = ORDER[k]
                    for g, js in enumerate(groups_of(q)):
                        ti = T_IDX[q, g] + 2
                        pi = PV_IDX[q, g]
                        dve.wait_ge(t_full, i * NT + ti + 1)
                        if pi >= NPT or not first:
                            dve.wait_ge(l_pv, i * NPV + pi - NPT + 1)
                        dve.tensor_copy(pt[pi % NPT][:, 0:len(js), :],
                                        bank(4 + ti % 2).rearrange("p (j r) -> p j r", j=4)[:, 0:len(js), :])\
                           .then_inc(t_free, 1)

                def l1_head(i, first):
                    if not first:
                        l_evac(i - 1, 5, False)
                        l_evac(i - 1, 6, False)
                    for k in range(T):
                        l_front(i, k)
                        if first and k == 1:
                            gate_and_up()
                        if k == FOLD_AT:
                            for n, dst in ((T_IDX["G"] + 2, G), (T_IDX["B"] + 2, Bv)):
                                dve.wait_ge(t_full, i * NT + n + 1)
                                dve.tensor_copy(dst[:, :], bank(4 + n % 2)[:, 0:P]).then_inc(t_free, 1)
                        if k >= T_LAG:
                            l_evac(i, k - T_LAG, first)
                        if k:
                            l_normalize(i, k - 1)
                        elif not first:
                            l_normalize(i - 1, 7)
                            l_evac(i - 1, 7, False)
                    if first:
                        sc, rs = qsc[:, 0, :], qsc[:, 1, :]
                        link(dve.tensor_reduce(sc, hh.rearrange("p t (n q) -> p (t n) q", q=QB), X, ALU.max,
                                               apply_absolute_value=True))
                        link(dve.tensor_scalar(sc, sc, 1.0 / 6.0, 1e-12, ALU.mult, ALU.max))
                        link(dve.reciprocal(rs, sc))
                        dve.tensor_scalar(sc, sc, 0.5, None, ALU.mult).then_inc(fscale.sem, 1)

                l1_head(b * H1, True)
                with dve.Fori(1, H1) as h:
                    l1_head(b * H1 + h, False)
                tail = (b + 1) * H1 - 1
                l_evac(tail, 5, False)
                l_evac(tail, 6, False)
                l_normalize(tail, 7)
                l_evac(tail, 7, False)
                dve.wait_ge(l_pv, (b + 1) * (H1 * NPV))
                dve.tensor_copy(s0[:, :, :], tiles(3)).then_inc(acc_out.sem, 1)

                drained(dve, b, "down")
                dve.wait_ge(*acc_out(b, 1))
                link(dve.tensor_tensor(tmp[:, :, :], s0[:, :, :], gate[:, :, :], ALU.mult))
                dve.wait_ge(*stored(b, 0))
                dve.tensor_tensor(ost[:, :, :], tmp[:, :, :], x1[:, :, :], ALU.add).then_inc(ready, 1)
                assert own[0] == V_STEPS, own[0]

        @block.tensor
        def _(pe):
            def mm(o, lhsT, rhs, start=True, stop=True, **kw):
                return pe.matmul(o, lhsT, rhs, start=start, stop=stop, **kw)

            pe.wait_ge(loaded, 16 * 9)
            pe.wait_ge(pool_const, 4)
            pe.wait_ge(set_v, 2)
            mm(bank(0)[:, 0:2], ones[:, :], rsum[:, :]).then_inc(set_pe, 1)
            pe.wait_ge(set_v, 13)
            for k in range(3):
                n = min(P, FI - k * P)
                pe.transpose(bank(2 + k)[:, 0:P], wnat[:, 0, k, :], ident)
                pe.transpose(bank(2 + k)[:, P:2 * P], wnat[:, 1, k, :], ident)
                pe.transpose(bank(2 + k)[0:n, 2 * P:3 * P], wdn[:, k * P:k * P + n], ident).then_inc(set_pe, 1)
            pe.wait_ge(set_a, 5)

            def fold(index, i_wait):
                for k, name in enumerate(("G", "B")):
                    slot = 4 + k % 2 if index is None else 4 + (T_IDX[name] + 2) % 2
                    if index is not None:
                        pe.wait_ge(t_free, index * NT + T_IDX[name] + 2 - 1)
                    if k == 0:
                        pe.wait_ge(hw_in, i_wait)
                    mm(bank(slot)[:, 0:P], hw[:, 2 * k, :], hw[:, 2 * k + 1, :]).then_inc(t_full, 1)

            pe.wait_ge(set_v, 22)
            fold(None, 16)

            with pe.Fori(0, NB) as b:
                def begin(name):
                    k = before_on_pair(JOB[name])
                    if k is not None:
                        drained(pe, b, JOBS[k][0])

                def end(ins):
                    ins.then_inc(filled.sem, 1)

                def transpose_tiles(name, src):
                    begin(name)
                    for t in range(T):
                        ins = pe.transpose(jtiles(name)[:, t, :], src[:, t, :], ident)
                    end(ins)

                def wide(name, lhsT, rhs):
                    begin(name)
                    for a in range(2):
                        ins = mm(jflat(name)[:, a * 512:(a + 1) * 512], lhsT, rhs[:, a * 512:(a + 1) * 512])
                    end(ins)

                pe.wait_ge(*xn_ready(b, 1))
                transpose_tiles("xnT", xn)
                pe.wait_ge(*xn_ready(b, 2))
                transpose_tiles("xaT", xa)
                drained(pe, b, "xaT")
                wide("qa", wts[:, W_QKVA:W_QKVA + C], xaT)
                wide("ka", wts[:, W_QKVA + C:W_QKVA + 2 * C], xaT)
                wide("qs", wts[:, W_QKVS:W_QKVS + C], xaT)
                wide("ks", wts[:, W_QKVS + C:W_QKVS + 2 * C], xaT)
                for k in range(2):
                    begin(f"v{k}")
                    for t in range(4 * k, 4 * k + 4):
                        for a, w in enumerate((W_QKVA, W_QKVS)):
                            at = (t % 4) * 2 * C + a * C
                            ins = mm(jflat(f"v{k}")[:, at:at + C], xaT[:, t * P:(t + 1) * P],
                                     wts[:, w + 2 * C:w + 3 * C])
                    end(ins)
                begin("ktok")
                pe.wait_ge(*feat(b, 2))
                for t in range(T):
                    ins = pe.transpose(jtiles("ktok")[:, t, :], kf[:, t * P:(t + 1) * P], ident)
                end(ins)
                pe.wait_ge(*feat(b, 3))
                wide("den", cst[:, C_BLK:C_BLK + P], z2)
                begin("kv")
                drained(pe, b, "ktok")
                drained(pe, b, "v1")
                for n in range(T - 1):
                    ins = mm(jtiles("kv")[:, n, :], ktok[:, n, :], val[:, n, C:2 * C])
                end(ins)
                begin("inter")
                pe.wait_ge(*states(b, 1))
                for n in range(1, T):
                    ins = mm(jtiles("inter")[:, n, :], state[:, n, :], qf[:, n * P:(n + 1) * P])
                end(ins)

                drained(pe, b, "kv")
                drained(pe, b, "inter")
                for s in range(4 * T + 3):
                    if s < 4 * T:
                        n, g = s // 4, s % 4
                        rows = slice(32 * g, 32 * g + 32)
                        if s >= 2:
                            pe.wait_ge(*win_exp(b, s - 1))
                        S = pair[s % 2][:, :, :].rearrange("p a n -> p (a n)").rearrange("p (j k) -> p j k", j=GH)
                        lo = (n - 1) * P if n else 0
                        for j in range(GH):
                            ins = mm(S[:, j, (0 if n else P):2 * P], qam[rows, n, j, :], kaT[rows, lo:(n + 1) * P])
                        ins.then_inc(win_scores.sem, 1)
                    t = s - 2
                    if 0 <= t < 4 * T:
                        pe.wait_ge(*win_norm(b, t + 1))
                        if t >= 2:
                            pe.wait_ge(*win_pt(b, t - 1))
                        for j in range(GH):
                            ins = pe.transpose(bank(4 + t % 2)[:, j * P:(j + 1) * P], pr[t % 3][:, j, :], ident)
                        ins.then_inc(win_tr.sem, 1)
                    u = s - 3
                    if 0 <= u < 4 * T:
                        n, g = u // 4, u % 4
                        pe.wait_ge(*win_pt(b, u + 1))
                        if g == 0 and n >= 2:
                            pe.wait_ge(*win_out(b, n - 1))
                        o = bank(6 + n % 2)[32 * g:32 * g + 32, :]
                        ch = slice(32 * g, 32 * g + 32)
                        ins = mm(o, val[:, n, ch], ptc[u % 2][:, :, :].rearrange("p j r -> p (j r)"), stop=(n == 0))
                        if n:
                            ins = mm(o, val[:, n - 1, ch], ptp[u % 2][:, :, :].rearrange("p j r -> p (j r)"), start=False)
                        ins.then_inc(win_pv.sem, 1)

                pe.wait_ge(*feat(b, 4))
                pe.wait_ge(*win_exp(b, 4 * T))
                for s in range(4 * T + 2):
                    if s < 4 * T:
                        n, g = s // 4, s % 4
                        rows = slice(32 * g, 32 * g + 32)
                        if s >= 4:
                            pe.wait_ge(*lin_am(b, s - 3))
                        mm(bank(s % 4), kf[rows, n * P:(n + 1) * P], qfm[rows, n, :, :].rearrange("p j r -> p (j r)"))\
                            .then_inc(lin_a.sem, 1)
                    if s < T:
                        if s >= 2:
                            pe.wait_ge(*fc_gelu(b, s - 1))
                        mm(bank(4 + s % 2), xnT[:, s * P:(s + 1) * P], wfc).then_inc(fc_full.sem, 1)
                    u = s - 2
                    if 0 <= u:
                        n, g = u // 4, u % 4
                        pe.wait_ge(*lin_am(b, u + 1))
                        if g == 0:
                            pe.wait_ge(*(lin_out(b, n - 1) if n >= 2 else win_out(b, T - 1 + n)))
                        mm(bank(6 + n % 2)[32 * g:32 * g + 32, :], val[:, n, C + 32 * g:C + 32 * g + 32],
                           am[u % 3][:, :, :].rearrange("p j r -> p (j r)")).then_inc(lin_pv.sem, 1)

                pe.wait_ge(*lin_out(b, T))
                begin("sumT")
                for a in range(2):
                    at = slice(a * 512, (a + 1) * 512)
                    o = jflat("sumT")[:, at]
                    mm(o, wts[:, W_PA:W_PA + C], winT[:, at], stop=False)
                    ins = mm(o, wts[:, W_OS:W_OS + C], linT[:, at], start=False)
                end(ins)

                def transpose_hidden(f):
                    begin(f"fT_{f}")
                    for t in range(T):
                        ins = pe.transpose(jtiles(f"fT_{f}")[:, t, :], hid[:, t, f * P:(f + 1) * P], ident)
                    end(ins)

                pe.wait_ge(*hid_norm(b, T))
                transpose_hidden(0)
                begin("mixed")
                drained(pe, b, "sumT")
                for t in range(T):
                    ins = mm(jtiles("mixed")[:, t, :], sumT[:, t * P:(t + 1) * P], wts[:, W_O:W_O + C])
                end(ins)
                for f in range(1, FB):
                    transpose_hidden(f)
                begin("ffn")
                drained(pe, b, "fT_3")
                for t in range(T):
                    for f in range(FB):
                        ins = mm(jtiles("ffn")[:, t, :], hidT[:, f, t * P:(t + 1) * P], wproj[:, f, :],
                                 start=(f == 0), stop=(f == FB - 1))
                end(ins)
                pe.wait_ge(*xn_ready(b, 3))
                transpose_tiles("hT", xa)
                drained(pe, b, "hT")
                for f in range(FB):
                    wide(f"w1_{f}", wts[:, W_1 + f * P:W_1 + (f + 1) * P], xaT)
                begin("mlp")
                drained(pe, b, "w1_3")
                for t in range(T):
                    for f in range(FB):
                        ins = mm(jtiles("mlp")[:, t, :], h1T[:, f, t * P:(t + 1) * P],
                                 wts[:, W_2 + f * P:W_2 + (f + 1) * P], start=(f == 0), stop=(f == FB - 1))
                end(ins)
                pe.wait_ge(*xn_ready(b, 4))
                transpose_tiles("x1T", xn)
                drained(pe, b, "x1T")
                drained(pe, b, "mlp")
                drained(pe, b, "w1_1")

                def gate_and_up():
                    pe.wait_ge(*xn_ready(b, 5))
                    transpose_tiles("xqT", xa)
                    drained(pe, b, "xqT")
                    for t in range(T):
                        begin(f"gu_{t}")
                        for k in range(2):
                            ins = mm(jflat(f"gu_{t}")[:, k * 512:k * 512 + FI], xaT[:, t * P:(t + 1) * P],
                                     wgT[:, k, :])
                        end(ins)
                    drained(pe, b, f"gu_{T - 1}")

                def free(i, name):
                    pe.wait_ge(u_free, i * NU + (NU + USE_BEFORE[USE[name]] + 1))

                def proj_y(i, first):
                    free(i, "Y")
                    pe.wait_ge(t_free, i * NT + (2 if first else T_IDX["G"] + 3 - NT))
                    for a in range(2):
                        at = slice(a * 512, (a + 1) * 512)
                        ins = mm(used("Y")[:, at], G[:, :], xnT[:, at])
                    ins.then_inc(u_full, 1)

                def proj_z(i, first):
                    free(i, "Z")
                    pe.wait_ge(t_free, i * NT + (2 if first else T_IDX["B"] + 3 - NT))
                    for t in range(T):
                        at = slice(t * P, (t + 1) * P)
                        ins = mm(used("Z")[:, at], xnT[:, at], Bv[:, :])
                    ins.then_inc(u_full, 1)

                def scores(i, k):
                    q = ORDER[k]
                    free(i, q)
                    if k == 0:
                        pe.wait_ge(u_free, i * NU + (NU + USE["Y"] + 1))
                    w = (q + 1) * P
                    S = used(q)
                    for at in range(0, w, 512):
                        to = min(w, at + 512)
                        mm(S[:, at:to], yT[:, q * P:(q + 1) * P], xnT[:, at:to])
                    mm(S[:, q * P:w], ident_b[:, :], causal_b[:, :], start=False, skip_group_check=True)\
                        .then_inc(u_full, 1)

                def transposes(i, k):
                    q = ORDER[k]
                    pe.wait_ge(l_norm, i * T + k + 1)
                    for g, js in enumerate(groups_of(q)):
                        ti = T_IDX[q, g] + 2
                        pe.wait_ge(t_free, i * NT + ti - 1)
                        for n, j in enumerate(js):
                            ins = pe.transpose(bank(4 + ti % 2)[:, n * P:(n + 1) * P],
                                               pb[k % 4][:, j * P:(j + 1) * P], ident)
                        ins.then_inc(t_full, 1)

                def pv(i, k, first):
                    q = ORDER[k]
                    if k == 0:
                        pe.wait_ge(u_free, i * NU + (NU + USE["Z"] + 1))
                    clears = first and q == next(x for x in ORDER if x // 4 == q // 4)
                    for g, js in enumerate(groups_of(q)):
                        pi = PV_IDX[q, g]
                        pe.wait_ge(t_free, i * NT + T_IDX[q, g] + 2 + 1)
                        for n, j in enumerate(js):
                            ins = mm(tiles(3)[:, q, :], pt[pi % NPT][:, n, :], Z[:, j, :],
                                     start=(clears and j == 0), skip_group_check=True)
                        ins.then_inc(l_pv, 1)

                def l1_head(i, first):
                    proj_y(i, first)
                    if not first:
                        transposes(i - 1, 5)
                        pv(i - 1, 4, False)
                        transposes(i - 1, 6)
                    scores(i, 0)
                    if not first:
                        pv(i - 1, 5, False)
                        transposes(i - 1, 7)
                    scores(i, 1)
                    if not first:
                        pv(i - 1, 6, False)
                        pv(i - 1, 7, False)
                    else:
                        gate_and_up()
                    proj_z(i, first)
                    for k in range(2, T):
                        scores(i, k)
                        if k == FOLD_AT:
                            fold(i, i * 16 + 32)
                        if k >= T_LAG:
                            transposes(i, k - T_LAG)
                        if k >= PV_LAG:
                            pv(i, k - PV_LAG, first)

                l1_head(b * H1, True)
                with pe.Fori(1, H1) as h:
                    l1_head(b * H1 + h, False)
                tail = (b + 1) * H1 - 1
                transposes(tail, 5)
                pv(tail, 4, False)
                transposes(tail, 6)
                pv(tail, 5, False)
                transposes(tail, 7)
                pv(tail, 6, False)
                pv(tail, 7, False)

                pe.wait_ge(t_free, (b + 1) * (H1 * NT) + 2)
                pe.wait_ge(*hq_ready(b, 1))
                for k in range(3):
                    n = min(P, FI - k * P)
                    begin(f"hqT_{k}")
                    for t in range(T):
                        ins = pe.transpose(jtiles(f"hqT_{k}")[0:n, t, :], hq[:, t, k * P:k * P + n], ident)
                    end(ins)
                begin("down")
                drained(pe, b, "hqT_2")
                pe.wait_ge(*acc_out(b, 1))
                for t in range(T):
                    for k in range(3):
                        n = min(P, FI - k * P)
                        ins = mm(jtiles("down")[:, t, :], hqT[0:n, k, t * P:(t + 1) * P], wdT[0:n, k, :],
                                 start=(k == 0), stop=(k == 2))
                end(ins)
                drained(pe, b, "down")


def kernel(**inputs):
    import concourse.bacc as bacc
    from concourse.bass_utils import run_bass_kernel_spmd

    a = {k.removeprefix("L"): np.asarray(v) for k, v in inputs.items()}
    heads = lambda w: w.reshape(H1, E1, C)
    hw = np.stack([heads(a["1_attn_wq"]), heads(a["1_attn_wk"]), heads(a["1_attn_wv"]),
                   heads(a["1_attn_wo"].T)], axis=2)
    hw = np.concatenate([hw, hw[0:1]])
    blocks = lambda w: w.reshape(FB, P, C).transpose(1, 0, 2).reshape(P, FB * C)
    wtab = np.concatenate([
        a["0_attn_Wqkv_a"], a["0_attn_Wqkv_s"], a["0_attn_Wp_a"], a["0_attn_Wo_s"], a["0_attn_Wo"],
        a["0_attn_W1"], blocks(a["0_attn_W2"]), a["0_ffn_W_fc"].T, blocks(a["0_ffn_W_proj"].T)], axis=1)
    ba, bs = a["0_attn_bqkv_a"], a["0_attn_bqkv_s"]
    vtab = np.stack([a["0_attn_g1"], a["0_attn_b1"], ba[0:C], ba[C:2 * C], bs[0:C], bs[C:2 * C],
                     a["0_attn_bp_a"], a["0_attn_bo_s"], a["0_attn_gm"], a["0_attn_bm"],
                     *a["0_attn_b1m"].reshape(FB, P), *a["0_ffn_ln_w"].reshape(FB, P),
                     *a["0_ffn_ln_b"].reshape(FB, P)], axis=1)
    rtab = np.concatenate([ba[2 * C:], bs[2 * C:], a["0_attn_bo"], a["0_attn_b2m"]])

    p, f = np.arange(P)[:, None], np.arange(P)[None, :]
    one = np.float32(1)
    ctab = np.concatenate([
        (p == f) * one, (p <= f) * one, (p > f) * one, (f > p) * one, (p // E0 == f // E0) * one,
        (f > p) * np.float32(NEG),
        (p % 32 // E0 == f[:, 0:GH]) * one, (p % 32 // E0 == f[:, 0:GH]) * np.float32(WIN_SCALE)],
        axis=1).astype(np.float32)
    arrays = {"x": a["0_attn_x"], "head_w": hw, "wtab": wtab, "vtab": vtab, "rtab": rtab, "ctab": ctab,
              "w_gate": a["1_ffn_w_gate"], "w_up": a["1_ffn_w_up"], "w_down": a["1_ffn_w_down"]}
    arrays = {k: np.ascontiguousarray(v) for k, v in arrays.items()}
    nc = bacc.Bacc("TRN2", target_bir_lowering=False, num_devices=1)
    args = [nc.dram_tensor(k, v.shape, mybir.dt.from_np(v.dtype), kind="ExternalInput").ap()
            for k, v in arrays.items()]
    args.append(nc.dram_tensor("out", (NB, L, C), F32, kind="ExternalOutput").ap())
    program(nc, *args)
    r = run_bass_kernel_spmd(nc, [arrays], core_ids=[0])
    return r.results[0]["out"]
```

```python
from contextlib import ExitStack

import numpy as np

import concourse.bass as bass
from concourse import mybir

F32 = mybir.dt.float32
F32R = mybir.dt.float32r
BF16 = mybir.dt.bfloat16
I32 = mybir.dt.int32
ALU = mybir.AluOpType
ACT = mybir.ActivationFunctionType
X = mybir.AxisListType.X

NB, L, C = 4, 1024, 128
P = 128
T = L // P
H0, E0 = 16, 8
GH = 4
HH = 2 * GH
H1, E1 = 16, 64
FF, FB = 512, 4
FI = 352
QB = 16
WIN_SCALE = float(np.float32(1) / np.sqrt(np.float32(E0)))
L1_SCALE = float(E1) ** -0.5
NEG = -1e30
LN_EPS = 1e-5

C_ID, C_KLE, C_JGT, C_BLK, C_CAUS, C_HM, C_HMS, C_H4 = 0, 128, 256, 384, 512, 640, 648, 656
C_N = 660
W_QKVA, W_QKVS, W_PA, W_OS, W_O, W_1, W_2, W_FC, W_PROJ = 0, 384, 768, 896, 1024, 1152, 1664, 2176, 2688
W_N = 3200
V_G1, V_B1, V_BQA, V_BKA, V_BQS, V_BKS, V_BPA, V_BOS, V_GM, V_BM, V_B1M, V_LNW, V_LNB = (
    0, 1, 2, 3, 4, 5, 6, 7, 8, 9, 10, 14, 18)
V_N = 22
R_BV, R_BO, R_B2 = 0, 256, 384
R_N = 512

JOBS = (
    [("xaT", "a", 0), ("ks", "a", 1), ("qa", "a", 2), ("ka", "v", 3), ("qs", "a", 1), ("xnT", "v", 0),
     ("v0", "v", 2), ("v1", "v", 3),
     ("ktok", "a", 2), ("kv", "v", 3),
     ("den", "v", 2), ("inter", "a", 3),
     ("sumT", "a", 0), ("fT_0", "a", 1), ("mixed", "v", 2), ("fT_1", "a", 3), ("fT_2", "a", 0), ("fT_3", "a", 1),
     ("ffn", "a", 3), ("hT", "a", 2)]
    + [(f"w1_{f}", "a", (0, 1, 3, 2)[f]) for f in range(FB)] + [("mlp", "v", 0)]
    + [("x1T", "v", 2), ("xqT", "v", 3)] + [(f"gu_{t}", "v", 2 + t % 2) for t in range(T)]
    + [(f"hqT_{k}", "a", k) for k in range(3)] + [("down", "a", 0)]
)
JOB = {name: k for k, (name, _, _) in enumerate(JOBS)}


def drained_count(k):
    return sum(1 for _, e, _ in JOBS[:k + 1] if e == JOBS[k][1])


def before_on_pair(k):
    return max((i for i in range(k) if JOBS[i][2] == JOBS[k][2]), default=None)


class Signal:

    def __init__(self, sem, per_seq, before=0):
        self.sem, self.per_seq, self.before = sem, per_seq, before

    def __call__(self, b, count):
        return self.sem, b * self.per_seq + (self.before + count)


def groups_of(i):
    return [range(0, min(4, i + 1))] + ([range(4, i + 1)] if i >= 4 else [])


ORDER = (4, 6, 1, 3, 7, 5, 2, 0)
T_LAG, PV_LAG = 3, 4
FOLD_AT = {"G": 6, "B": 6}
T_IDX, PV_IDX = {}, {}
for _k, _q in enumerate(ORDER):
    for _name in ("G", "B"):
        if _k == FOLD_AT[_name] - T_LAG:
            T_IDX[_name] = len(T_IDX)
    for _g in range(len(groups_of(_q))):
        PV_IDX[_q, _g] = len(PV_IDX)
        T_IDX[_q, _g] = len(T_IDX)
NT, NPV = len(T_IDX), len(PV_IDX)
BY_SCALAR = (4, 6, 7)
T_BY = ["a" if name[0] in BY_SCALAR else "v" for name in T_IDX]
NTV, NTA = T_BY.count("v"), T_BY.count("a")
NPT = 4
USES = ("Y",) + ORDER[:2] + ("Z",) + ORDER[2:]
USE = {name: u for u, name in enumerate(USES)}
NU = len(USES)


def place_uses():
    size = [1 if name in range(4) else 2 for name in USES]
    last, first_bank = [-4, -3, -2, -1], []
    for u, n in enumerate(size):
        _, at = min((max(last[at:at + n]), at) for at in range(0, 4, n))
        first_bank.append(at)
        last[at:at + n] = [u] * n
    before = []
    last = [u - NU for u in last]
    for u, n in enumerate(size):
        at = first_bank[u]
        before.append(max(last[at:at + n]))
        last[at:at + n] = [u] * n
    return first_bank, before


USE_BANK, USE_BEFORE = place_uses()
HEADS_PEELED = 4
HEADS_UNROLLED = 3
V_STEPS = 119


def program(nc, x, head_w, wtab, vtab, rtab, ctab, w_gate, w_up, w_down, out):
    with ExitStack() as ctx:
        def sb(name, shape, dt=F32):
            return ctx.enter_context(nc.sbuf_tensor(name, shape, dt))

        def sem(name):
            return ctx.enter_context(nc.semaphore(name))

        def sig(name, per_seq, before=0):
            return Signal(sem(name), per_seq, before)

        cst = sb("cst", [P, C_N])
        wts = sb("wts", [P, W_N])
        vec = sb("vec", [P, V_N])
        row = sb("row", [P, R_N])
        ident = cst[:, C_ID:C_ID + P]
        hmask = cst[:, C_HM:C_HM + HH]
        hmask_s = cst[:, C_HMS:C_HMS + HH]
        gmask = cst[:, C_H4:C_H4 + GH]
        ident_b = sb("ident_b", [P, P], BF16)
        causal_b = sb("causal_b", [P, P], BF16)
        neg = sb("neg", [P, P])
        mhalf = sb("mhalf", [P, T])
        bqa_m = sb("bqa_m", [P, HH])
        bqs_s = sb("bqs_s", [P, 1])
        bqs_neg = sb("bqs_neg", [P, 1])
        bks_neg = sb("bks_neg", [P, 1])
        bsum = sb("bsum", [P, 1])
        ones = sb("ones", [P, P])
        wfc = wts[:, W_FC:W_FC + FF]
        wproj = wts[:, W_PROJ:W_PROJ + FF].rearrange("p (f n) -> p f n", f=FB)
        rsum = sb("rsum", [P, 2])
        half = sb("half", [P, 4])
        wgT = sb("wgT", [P, 2, FI])
        wdT = sb("wdT", [P, 3, P])

        xs = sb("xs", [P, T, C])
        xn = sb("xn", [P, T, C])
        xa = sb("xa", [P, T, C])
        tmp = sb("tmp", [P, T, C])
        st = sb("st", [P, 8, T])
        hst = sb("hst", [P, 5, T])
        xnT = sb("xnT", [P, L])
        xaT = sb("xaT", [P, L])
        big = sb("big", [P, 8 * L])
        big0, big1 = big[:, 0:4 * L], big[:, 4 * L:8 * L]
        qam = big[:, :].rearrange("p (n j r) -> p n j r", n=T, j=HH)
        h1T = big0[:, :].rearrange("p (f r) -> p f r", f=FB)
        hid = big0[:, :].rearrange("p (t n) -> p t n", t=T)
        hidT = big1[:, :].rearrange("p (f r) -> p f r", f=FB)
        NQ = T * FI
        work = sb("work", [P, 4 * NQ])
        kaT, qf, kf, z0, z1, z2, z3, interT, ktok_, state_ = (work[:, k * L:(k + 1) * L] for k in range(10))
        ktok, state = (w.rearrange("p (t c) -> p t c", t=T) for w in (ktok_, state_))
        qa_, qz_, qy_, qs_ = (work[:, k * NQ:(k + 1) * NQ] for k in range(4))
        val = sb("val", [P, T, 2 * C])
        rdenT = kaT
        winT = sb("winT", [P, L])
        linT = sb("linT", [P, L])
        sumT = sb("sumT", [P, L])
        x1 = sb("x1", [P, T, C])
        s0 = sb("s0", [P, T, C])
        gate = sb("gate", [P, T, C])
        xc = sumT[:, :].rearrange("p (t c) -> p t c", t=T)
        wnat = x1[:, 0:2 * 3, :].rearrange("p (k t) c -> p k t c", k=2)
        wdn = s0[:, :, :].rearrange("p t c -> p (t c)")[:, 0:FI]

        probs = sb("probs", [P, 12 * 512])
        quarter = [probs[:, k * 512:(k + 1) * 512].rearrange("p (j r) -> p j r", j=GH) for k in range(12)]
        pr, am, ext = quarter[0:3] + quarter[11:12], quarter[7:10], quarter[10]
        ptc, ptp = quarter[3:5] + quarter[7:8], quarter[5:7] + quarter[8:9]
        h_sq = quarter[0:7] + quarter[11:12]
        nmx = sb("nmx", [P, 4, GH])
        den = sb("den", [P, 4, GH])
        rdn = sb("rdn", [P, 4, GH])
        red = sb("red", [P, P])
        poke = sb("poke", [P, 4])
        red2 = sb("red2", [P, P])

        hw = sb("hw", [E1, 4, C])
        G_hi = sb("G_hi", [P, P], F32R)
        G_lo = sb("G_lo", [P, P], F32R)
        Bv = sb("Bv", [P, P])
        y_hi, y_lo, x_hi, x_lo = (sb(name, [P, L], F32R)[:, :] for name in ("y_hi", "y_lo", "x_hi", "x_lo"))
        Z = linT[:, :].rearrange("p (t c) -> p t c", t=T)
        pb = [probs[:, k * L:(k + 1) * L] for k in range(4)]
        pt = quarter[8:8 + NPT]
        nm1 = sb("nm1", [P, T])
        dn1 = sb("dn1", [P, T])
        rd1 = sb("rd1", [P, T])

        qfm = [w[:, :, :] for w in (x1, s0, gate)]
        vdiff = interT.rearrange("p (t c) -> p t c", t=T)

        qsc = sb("qsc", [P, 2, NQ // QB])
        hh = big0[:, 0:NQ].rearrange("p (t n) -> p t n", t=T)
        hq = big1[:, 0:NQ].rearrange("p (t n) -> p t n", t=T)
        sg = sb("sg", [P, 2, FI])
        hqT = big0[:, 0:3 * L].rearrange("p (k r) -> p k r", k=3)

        pair = [ctx.enter_context(nc.psum_tensor(f"pair{i}", [P, 2, 512], F32)) for i in range(4)]

        def flat(k):
            return pair[k][:, :, :].rearrange("p a n -> p (a n)")

        def tiles(k):
            return flat(k).rearrange("p (t n) -> p t n", n=P)

        def jflat(name):
            return flat(JOBS[JOB[name]][2])

        def jtiles(name):
            return tiles(JOBS[JOB[name]][2])

        def bank(n):
            return pair[n // 2][:, n % 2, :]

        def used(name):
            n = USE_BANK[USE[name]]
            return bank(n) if name in range(4) else flat(n // 2)

        loaded = sem("loaded")
        x_in = sig("x_in", 16)
        hw_in = sem("hw_in")
        stored = sig("stored", 16, 16)
        pool_const = sem("pool_const")
        filled = sig("filled", len(JOBS))
        by_v = sig("drained_by_vector", sum(e == "v" for _, e, _ in JOBS))
        by_a = sig("drained_by_scalar", sum(e == "a" for _, e, _ in JOBS))
        v_own = sem("v_own")
        stat_in = sig("stat_in", 5)
        rstd_out = sig("rstd_out", 5)
        xn_ready = sig("xn_ready", 5)
        feat_neg = sig("feat_neg", 2)
        feat_exp = sig("feat_exp", 2)
        feat = sig("features", 3)
        state_step = sig("state_step", T - 2)
        win_scores = sig("win_scores", 32)
        win_max = sig("win_max", 32)
        win_exp = sig("win_exp", 32)
        win_rden = sig("win_rden", 32)
        win_norm = sig("win_norm", 32)
        win_tr = sig("win_tr", 32)
        win_pt = sig("win_pt", 32)
        win_pc = sig("win_pc", 32)
        masked_q = sig("masked_q", 1)
        xb_ready = sig("xb_ready", 1)
        vdiff_ready = sig("vdiff_ready", 1)
        qfm_ready = sig("qfm_ready", T)
        win_pv = sig("win_pv", 32)
        win_out = sig("win_out", T)
        lin_a = sig("lin_a", 32)
        lin_am = sig("lin_am", 32)
        lin_pv = sig("lin_pv", 32)
        lin_out = sig("lin_out", T)
        fc_full = sig("fc_filled", T)
        fc_gelu = sig("fc_gelu", T)
        hid_mean = sig("hid_mean", 1)
        hid_sq = sig("hid_squares", 1)
        hid_norm = sig("hid_norm", T)
        up_done = sig("up_silu", T)
        x_hi_ready = sig("x_hi_ready", 1)
        x_lo_ready = sig("x_lo_ready", 1)
        g_hi_ready = sem("l1_g_hi")
        y_lo_ready = sem("l1_y_lo")
        u_full = sem("l1_use_filled")
        u_free = sem("l1_use_drained")
        l_max = sem("l1_max")
        l_norm = sem("l1_norm")
        t_full = sem("l1_tr_filled")
        t_free_v = sem("l1_tr_drained_by_vector")
        t_free_a = sem("l1_tr_drained_by_scalar")
        l_pv = sem("l1_pv")
        acc_out = sig("l1_out", 1)
        l_own = sem("l1_v_own")
        hq_ready = sig("hq_ready", 1)
        fsign = sig("fp4_sign", 2)
        fscale = sig("fp4_scale", 1)
        p_own = sig("pool_own", 15)
        set_pe = sem("setup_pe")
        set_v = sem("setup_v")
        set_a = sem("setup_a")
        ready = sem("result_ready")

        block = ctx.enter_context(nc.Block())

        def drained(eng, b, name):
            k = JOB[name]
            eng.wait_ge(*(by_v if JOBS[k][1] == "v" else by_a)(b, drained_count(k)))

        def evacuate(eng, i, k, first):
            q = ORDER[k]
            scalar = eng is nc.scalar
            if (q in BY_SCALAR) != scalar:
                return
            for g, js in enumerate(groups_of(q)):
                ti = T_IDX[q, g] + 2
                pi = PV_IDX[q, g]
                eng.wait_ge(t_full, i * NT + ti + 1)
                if pi >= NPT or not first:
                    eng.wait_ge(l_pv, i * NPV + pi - NPT + 1)
                dst = pt[pi % NPT][:, 0:len(js), :]
                src = bank(4 + ti % 2).rearrange("p (j r) -> p j r", j=4)[:, 0:len(js), :]
                if scalar:
                    eng.activation(dst, src, ACT.Copy).then_inc(t_free_a, 1)
                else:
                    eng.tensor_copy(dst, src).then_inc(t_free_v, 1)

        def tr_drained(eng, i, idx, first):
            if idx < 0:
                if first:
                    return
                i, idx = i - 1, idx + NT
            n = T_BY[:idx + 1].count(T_BY[idx])
            if T_BY[idx] == "v":
                eng.wait_ge(t_free_v, i * NTV + (2 + n))
            else:
                eng.wait_ge(t_free_a, i * NTA + n)

        @block.sync
        def _(sp):
            sp.sem_inc(stored.sem, 16)
            sp.dma_start(cst[:, :], ctab).then_inc(loaded, 16)
            sp.dma_start(wts[:, :], wtab).then_inc(loaded, 16)
            sp.dma_start(vec[:, :], vtab).then_inc(loaded, 16)
            sp.dma_start(row[:, :], rtab.partition_broadcast(P)).then_inc(loaded, 16)
            sp.wait_ge(pool_const, 1)
            for k, w in enumerate((w_gate, w_up)):
                sp.dma_start(wnat[:, k, 0:2, :], w[0:2 * P, :].rearrange("(t p) c -> p t c", p=P)).then_inc(loaded, 16)
                sp.dma_start(wnat[0:FI - 2 * P, k, 2, :], w[2 * P:FI, :]).then_inc(loaded, 16)
            sp.dma_start(wdn[:, :], w_down).then_inc(loaded, 16)
            sp.dma_start(hw[:, :, :], head_w[0]).then_inc(hw_in, 16)

            def load_x(b):
                sp.dma_start(xs[:, :, :], x[b].rearrange("(t p) c -> p t c", p=P)).then_inc(x_in.sem, 16)

            def sequence(b, last):
                sp.wait_ge(*xn_ready(b, 4))
                load_x(b if last else b + 1)
                with sp.Fori(0, H1) as h:
                    sp.wait_ge(t_full, b * (H1 * NT) + h * NT + (2 + T_IDX["B"] + 1))
                    sp.dma_start(hw[:, :, :], head_w[h + 2]).then_inc(hw_in, 16)
                sp.wait_ge(ready, b + 1)
                sp.dma_start(out[b].rearrange("(t p) c -> p t c", p=P), x1[:, :, :]).then_inc(stored.sem, 16)

            load_x(0)
            sp.wait_ge(t_full, 2)
            sp.dma_start(hw[:, :, :], head_w[1]).then_inc(hw_in, 16)
            with sp.Fori(0, NB - 1) as b:
                sequence(b, False)
            sequence(NB - 1, True)
            sp.wait_ge(*stored(NB - 1, 16))
            sp.wait_ge(*x_in(NB, 16))
            sp.wait_ge(hw_in, 16 * (NB * H1 + 2))

        @block.gpsimd
        def _(pool):
            pool.memset(wnat[:, :, 2, :], 0.0).then_inc(pool_const, 1)
            pool.memset(mhalf[:, :], -0.5).then_inc(pool_const, 1)
            pool.memset(ones[:, :], 1.0).then_inc(pool_const, 1)
            pool.memset(neg[:, :], NEG).then_inc(pool_const, 1)
            pool.wait_ge(pool_const, 4)

            def rstd(b, k, dst, src):
                pool.wait_ge(*stat_in(b, k + 1))
                pool.tensor_tensor(dst, src, mhalf[:, :], ALU.pow).then_inc(rstd_out.sem, 1)

            def first_norms(b):
                rstd(b, 0, st[:, 3, :], st[:, 2, :])
                rstd(b, 1, st[:, 5, :], st[:, 4, :])

            first_norms(0)
            with pool.Fori(0, NB) as b:
                steps = [0]

                def step(ins):
                    steps[0] += 1
                    ins.then_inc(p_own.sem, 1)

                def link(ins):
                    step(ins)
                    pool.wait_ge(*p_own(b, steps[0]))

                drained(pool, b, "v1")
                pool.tensor_tensor(vdiff[:, 1:T, :], val[:, 1:T, 0:C], val[:, 0:T - 1, 0:C], ALU.subtract)\
                    .then_inc(vdiff_ready.sem, 1)

                pool.tensor_tensor(xa[:, :, :], xn[:, :, :], row[:, R_BO:R_BO + C].unsqueeze(1)
                                   .broadcast_to([P, T, C]), ALU.add).then_inc(xb_ready.sem, 1)

                def mask_queries(n):
                    if n == 0:
                        pool.wait_ge(*feat(b, 2))
                        pool.wait_ge(*stored(b, 0))
                    if n >= 3:
                        pool.wait_ge(*lin_a(b, 4 * (n - 2)))
                    pool.tensor_tensor(qfm[n % 3], qf[:, n * P:(n + 1) * P].unsqueeze(1).broadcast_to([P, HH, P]),
                                       hmask.unsqueeze(2).broadcast_to([P, HH, P]), ALU.mult)\
                        .then_inc(qfm_ready.sem, 1)

                for s in range(4 * T):
                    if s in (12, 18, 24):
                        mask_queries((s - 12) // 6)
                    pool.wait_ge(*win_rden(b, s + 1))
                    p = pr[s % 4]
                    pool.tensor_tensor(p[:, :, :], p[:, :, :],
                                       rdn[:, s % 4, :].unsqueeze(2).broadcast_to([P, GH, P]),
                                       ALU.mult).then_inc(win_norm.sem, 1)
                for n in range(3, T):
                    mask_queries(n)
                rstd(b, 2, hst[:, 4, :], hst[:, 3, :])
                for k in range(3, 5):
                    rstd(b, k, st[:, 3, :], st[:, 2, :])
                first_norms(b + 1)

                b3 = lambda ap: ap.rearrange("p (n q) -> p n q", q=QB)
                scale = lambda k: qsc[:, k, :].unsqueeze(2).broadcast_to([P, NQ // QB, QB])
                pool.wait_ge(*fsign(b, 2))
                pool.wait_ge(*fscale(b, 1))
                hq_ = hq.rearrange("p t n -> p (t n)")
                z = (qz_, hq_)
                midpoints = ((0.75, 1.0), (1.25, 1.0), (1.75, 1.0), (2.5, 2.0), (3.5, 2.0), (5.0, 4.0))

                def over(k):
                    mid, half_steps = midpoints[k]
                    step(pool.tensor_scalar(z[k % 2], qa_, mid, half_steps, ALU.is_gt, ALU.mult))

                link(pool.tensor_tensor(b3(qa_), b3(qa_), scale(1), ALU.mult))
                step(pool.tensor_tensor(b3(qs_), b3(qs_), scale(0), ALU.mult))
                step(pool.tensor_scalar(qy_, qa_, 0.25, None, ALU.is_gt))
                over(0)
                for k in range(len(midpoints)):
                    pool.wait_ge(*p_own(b, steps[0]))
                    step(pool.tensor_tensor(qy_, qy_, z[k % 2], ALU.add))
                    if k + 1 < len(midpoints):
                        over(k + 1)
                pool.wait_ge(*p_own(b, steps[0]))
                pool.tensor_tensor(hq_, qy_, qs_, ALU.mult).then_inc(hq_ready.sem, 1)
                assert steps[0] == p_own.per_seq, steps

        @block.scalar
        def _(act):
            act.wait_ge(loaded, 16 * 9)
            for dst, src in ((ident_b, C_ID), (causal_b, C_CAUS)):
                act.activation(dst[:, :], cst[:, src:src + P], ACT.Copy).then_inc(set_a, 1)
            for k in range(2):
                act.activation(qs_[:, k * 3 * P:(k + 1) * 3 * P], wnat[:, k, :, :].rearrange("p t c -> p (t c)"),
                               ACT.Sign).then_inc(set_a, 1)
            act.activation(qs_[:, 6 * P:6 * P + FI], wdn[:, :], ACT.Sign).then_inc(set_a, 1)
            act.wait_ge(set_v, 16)
            act.sem_inc(u_free, NU)

            with act.Fori(0, NB) as b:
                def full(name):
                    act.wait_ge(*filled(b, JOB[name] + 1))

                full("xaT")
                act.activation(xaT[:, :], jflat("xaT"), ACT.Identity, bias=vec[:, V_B1:V_B1 + 1],
                               scale=vec[:, V_G1:V_G1 + 1]).then_inc(by_a.sem, 1)

                def features(job, neg_part, pos_part, bias, minus_bias, scale):
                    full(job)
                    act.activation(neg_part[:, :], jflat(job), ACT.Relu, bias=minus_bias, scale=-scale)\
                       .then_inc(feat_neg.sem, 1)
                    act.activation(pos_part[:, :], jflat(job), ACT.Relu, bias=bias, scale=scale).then_inc(by_a.sem, 1)
                    act.wait_ge(*feat_neg(b, 1 if job == "ks" else 2))
                    act.activation(neg_part[:, :], neg_part[:, :], ACT.Exp, scale=-1.0).then_inc(feat_exp.sem, 1)

                features("ks", z2, z3, vec[:, V_BKS:V_BKS + 1], bks_neg[:, 0:1], 1.0)
                full("qa")
                for j in range(HH):
                    ins = act.activation(qam[:, 0:T // 2, j, :], jtiles("qa")[:, 0:T // 2, :], ACT.Identity,
                                         bias=bqa_m[:, j:j + 1], scale=hmask_s[:, j:j + 1])
                ins.then_inc(by_a.sem, 1)
                features("qs", z0, z1, bqs_s[:, 0:1], bqs_neg[:, 0:1], WIN_SCALE)
                full("ktok")
                act.activation(ktok[:, :, :], jtiles("ktok"), ACT.Copy).then_inc(by_a.sem, 1)
                def copy_transposed(s):
                    act.wait_ge(*win_tr(b, s + 1))
                    if s >= 3:
                        act.wait_ge(*win_pv(b, s - 2))
                    act.activation(ptp[s % 3][:, :, :].rearrange("p j r -> p (j r)"), bank(4 + s % 2), ACT.Copy)\
                       .then_inc(win_pc.sem, 1)

                for s in range(4 * T):
                    if s >= 3:
                        copy_transposed(s - 3)
                    act.wait_ge(*win_max(b, s + 1))
                    if s >= 4:
                        act.wait_ge(*win_tr(b, s - 3))
                    S = pair[s % 2][:, :, :].rearrange("p a n -> p (a n)").rearrange("p (j k) -> p j k", j=GH)
                    for j in range(GH):
                        ins = act.activation(pr[s % 4][:, j, :], S[:, j, P:2 * P], ACT.Exp,
                                             bias=nmx[:, s % 4, j:j + 1], accum_out=den[:, s % 4, j:j + 1])
                    ins.then_inc(win_exp.sem, 1)

                for s in range(4 * T - 3, 4 * T):
                    copy_transposed(s)
                full("inter")
                act.activation(interT[:, P:L], jflat("inter")[:, P:L], ACT.Copy).then_inc(by_a.sem, 1)
                for t in range(T):
                    act.wait_ge(*fc_full(b, t + 1))
                    act.activation(hid[:, t, :], bank(4 + t % 2), ACT.Gelu, accum_out=hst[:, 0, t:t + 1])\
                       .then_inc(fc_gelu.sem, 1)
                act.wait_ge(*hid_mean(b, 1))
                for t in range(T):
                    ins = act.activation(h_sq[t].rearrange("p j r -> p (j r)"), hid[:, t, :], ACT.Square, bias=hst[:, 1, t:t + 1],
                                         accum_out=hst[:, 2, t:t + 1])
                ins.then_inc(hid_sq.sem, 1)

                def drain_fT(f):
                    full(f"fT_{f}")
                    act.activation(hidT[:, f, :], jflat(f"fT_{f}"), ACT.Identity,
                                   bias=vec[:, V_LNB + f:V_LNB + f + 1],
                                   scale=vec[:, V_LNW + f:V_LNW + f + 1]).then_inc(by_a.sem, 1)

                full("sumT")
                act.activation(sumT[:, :], jflat("sumT"), ACT.Identity, bias=bsum[:, 0:1]).then_inc(by_a.sem, 1)
                for f in range(FB):
                    drain_fT(f)
                full("ffn")
                act.activation(gate[:, :, :], jtiles("ffn"), ACT.Silu).then_inc(by_a.sem, 1)
                full("hT")
                act.activation(xaT[:, :], jflat("hT"), ACT.Identity, bias=vec[:, V_BM:V_BM + 1],
                               scale=vec[:, V_GM:V_GM + 1]).then_inc(by_a.sem, 1)
                for f in range(FB):
                    full(f"w1_{f}")
                    act.activation(h1T[:, f, :], jflat(f"w1_{f}"), ACT.Gelu,
                                   bias=vec[:, V_B1M + f:V_B1M + f + 1]).then_inc(by_a.sem, 1)
                def gate_and_up():
                    for t in range(T):
                        full(f"gu_{t}")
                        if t >= 2:
                            act.wait_ge(*by_v(b, drained_count(JOB[f"gu_{t - 2}"])))
                        act.activation(sg[:, t % 2, :], jflat(f"gu_{t}")[:, 0:FI], ACT.Silu).then_inc(up_done.sem, 1)

                def beside_heads(s):
                    if T <= s < 2 * T:
                        n = (s - T) % 4
                        at = slice(2 * n * FI, 2 * (n + 1) * FI)
                        src = hh.rearrange("p t n -> p (t n)")[:, at]
                        if s == T:
                            drained(act, b, f"gu_{T - 1}")
                        if s < T + 4:
                            act.activation(qa_[:, at], src, ACT.Abs)
                        else:
                            ins = act.activation(qs_[:, at], src, ACT.Sign)
                            if n == 3:
                                ins.then_inc(fsign.sem, 1)

                act.wait_ge(*xn_ready(b, 4))
                act.activation(qs_[:, 0:L], xn[:, :, :].rearrange("p t c -> p (t c)"), ACT.Sign)\
                   .then_inc(fsign.sem, 1)

                drained(act, b, "x1T")
                act.activation(x_hi, xnT[:, :], ACT.Copy).then_inc(x_hi_ready.sem, 1)

                def l1_head(i, first, number=HEADS_PEELED):
                    for u, use in enumerate(USES):
                        if use == "Y":
                            act.wait_ge(u_full, i * NU + u + 1)
                            act.activation(y_hi, used("Y"), ACT.Copy, scale=L1_SCALE).then_inc(u_free, 1)
                        elif use == "Z":
                            act.wait_ge(u_full, i * NU + u + 1)
                            if not first:
                                act.wait_ge(l_pv, i * NPV)
                            act.activation(Z[:, :, :].rearrange("p t c -> p (t c)"), used("Z"), ACT.Copy)\
                               .then_inc(u_free, 1)
                            if first:
                                gate_and_up()
                        else:
                            k, w = ORDER.index(use), (use + 1) * P
                            if k >= T_LAG:
                                evacuate(act, i, k - T_LAG, first)
                            act.wait_ge(l_max, i * T + k + 1)
                            act.activation(pb[k % 4][:, 0:w], used(use)[:, 0:w], ACT.Exp,
                                           bias=nm1[:, use:use + 1], accum_out=dn1[:, use:use + 1])\
                               .then_inc(u_free, 1)
                            beside_heads(number * T + k)

                for k in range(HEADS_PEELED):
                    l1_head(b * H1 + k, k == 0, k)
                with act.Fori(0, (H1 - HEADS_PEELED) // HEADS_UNROLLED) as h:
                    for k in range(HEADS_UNROLLED):
                        l1_head(b * H1 + h * HEADS_UNROLLED + (HEADS_PEELED + k), False)

                for k in range(3):
                    n = min(P, FI - k * P)
                    full(f"hqT_{k}")
                    act.activation(hqT[0:n, k, :], jflat(f"hqT_{k}")[0:n, :], ACT.Copy).then_inc(by_a.sem, 1)
                full("down")
                act.activation(gate[:, :, :], jtiles("down"), ACT.Silu).then_inc(by_a.sem, 1)

        @block.vector
        def _(dve):
            own = [0]

            def bc(ap, n):
                return ap.unsqueeze(2).broadcast_to([P, ap.shape[1], n])

            def bcm(ap, n):
                return ap.unsqueeze(1).broadcast_to([P, n, ap.shape[1]])

            def fp4(link, src, dst, sgn, nblk):
                a = qa_[:, 0:nblk * QB]
                z = qz_[:, 0:nblk * QB]
                y = qy_[:, 0:nblk * QB]
                sc, rs = qsc[:, 0, 0:nblk], qsc[:, 1, 0:nblk]
                b3 = lambda ap: ap.rearrange("p (n q) -> p n q", q=QB)
                link(dve.tensor_reduce(sc, b3(src), X, ALU.max, apply_absolute_value=True))
                link(dve.tensor_scalar(sc, sc, 1.0 / 6.0, 1e-12, ALU.mult, ALU.max))
                link(dve.reciprocal(rs, sc))
                link(dve.tensor_tensor(b3(y), b3(src), bc(rs, QB), ALU.mult))
                link(dve.scalar_tensor_tensor(a, y, -1.0, y, ALU.mult, ALU.max))
                link(dve.tensor_scalar(z, a, 5.0, 2.0, ALU.is_gt, ALU.mult))
                link(dve.scalar_tensor_tensor(y, a, 3.5, z, ALU.is_gt, ALU.add))
                link(dve.scalar_tensor_tensor(z, a, 2.5, y, ALU.is_gt, ALU.add))
                link(dve.tensor_scalar(y, z, 2.0, None, ALU.mult))
                link(dve.scalar_tensor_tensor(z, a, 1.75, y, ALU.is_gt, ALU.add))
                link(dve.scalar_tensor_tensor(y, a, 1.25, z, ALU.is_gt, ALU.add))
                link(dve.scalar_tensor_tensor(z, a, 0.75, y, ALU.is_gt, ALU.add))
                link(dve.scalar_tensor_tensor(y, a, 0.25, z, ALU.is_gt, ALU.add))
                link(dve.scalar_tensor_tensor(b3(z), b3(sgn), 0.5, bc(sc, QB), ALU.mult, ALU.mult))
                return dve.tensor_tensor(dst, y, z, ALU.mult)

            def slink(ins):
                own[0] += 1
                ins.then_inc(v_own, 1)
                dve.wait_ge(v_own, own[0])

            dve.wait_ge(loaded, 16 * 9)
            dve.wait_ge(pool_const, 4)
            for k, w in enumerate((W_FC, W_PROJ)):
                dve.tensor_reduce(rsum[:, k:k + 1], wts[:, w:w + FF], X, ALU.add, apply_absolute_value=True)\
                   .then_inc(set_v, 1)
            dve.wait_ge(set_pe, 1)
            slink(dve.tensor_scalar(half[:, 0:2], bank(0)[:, 0:2], 1.0 / (FF * C), 1e-6, ALU.mult, ALU.add))
            slink(dve.tensor_scalar(half[:, 2:4], half[:, 0:2], -0.5, None, ALU.mult))
            slink(dve.tensor_scalar(half[:, 0:2], half[:, 0:2], 0.5, None, ALU.mult))
            for k, w in enumerate((W_FC, W_PROJ)):
                m = wts[:, w:w + FF]
                slink(dve.tensor_scalar(qa_[:, 0:FF], m, half[:, 2 + k:3 + k], None, ALU.is_lt))
                slink(dve.scalar_tensor_tensor(qz_[:, 0:FF], m, half[:, k:k + 1], qa_[:, 0:FF], ALU.is_gt, ALU.subtract))
                dve.tensor_copy(m, qz_[:, 0:FF]).then_inc(set_v, 1)
                dve.wait_ge(set_v, 3 + k)
            for j in range(HH):
                dve.tensor_tensor(bqa_m[:, j:j + 1], hmask_s[:, j:j + 1], vec[:, V_BQA:V_BQA + 1], ALU.mult)\
                   .then_inc(set_v, 1)
            dve.tensor_scalar(bqs_s[:, :], vec[:, V_BQS:V_BQS + 1], WIN_SCALE, None, ALU.mult).then_inc(set_v, 1)
            dve.tensor_scalar(bqs_neg[:, :], vec[:, V_BQS:V_BQS + 1], -WIN_SCALE, None, ALU.mult).then_inc(set_v, 1)
            dve.tensor_scalar(bks_neg[:, :], vec[:, V_BKS:V_BKS + 1], -1.0, None, ALU.mult).then_inc(set_v, 1)
            dve.tensor_tensor(bsum[:, :], vec[:, V_BPA:V_BPA + 1], vec[:, V_BOS:V_BOS + 1], ALU.add).then_inc(set_v, 1)
            dve.wait_ge(set_a, 5)
            for k in range(2):
                src = wnat[:, k, :, :].rearrange("p t c -> p (t c)")
                fp4(slink, src, src, qs_[:, k * 3 * P:(k + 1) * 3 * P], 3 * P // QB).then_inc(set_v, 1)
                dve.wait_ge(set_v, 17 + k)
            fp4(slink, wdn[:, :], wdn[:, :], qs_[:, 6 * P:6 * P + FI], FI // QB).then_inc(set_v, 1)
            for k in range(3):
                dve.wait_ge(set_pe, 2 + k)
                n = min(P, FI - k * P)
                dve.tensor_copy(wgT[:, 0, k * P:k * P + n], bank(2 + k)[:, 0:n]).then_inc(set_v, 1)
                dve.tensor_copy(wgT[:, 1, k * P:k * P + n], bank(2 + k)[:, P:P + n]).then_inc(set_v, 1)
                dve.tensor_copy(wdT[0:n, k, :], bank(2 + k)[0:n, 2 * P:3 * P]).then_inc(set_v, 1)
            dve.wait_ge(t_full, 1)
            dve.tensor_copy(G_hi[:, :], bank(4)[:, 0:P]).then_inc(g_hi_ready, 1)
            dve.wait_ge(g_hi_ready, 1)
            dve.tensor_tensor(G_lo[:, :], bank(4)[:, 0:P], G_hi[:, :], ALU.subtract).then_inc(t_free_v, 1)
            dve.wait_ge(t_full, 2)
            dve.tensor_copy(Bv[:, :], bank(5)[:, 0:P]).then_inc(t_free_v, 1)
            setup_steps = own[0]

            def center_step(link, src, step):
                if step == 0:
                    link(dve.tensor_reduce(st[:, 0, :], src, X, ALU.add))
                    link(dve.tensor_scalar(st[:, 1, :], st[:, 0, :], -1.0 / C, None, ALU.mult))
                if step == 1:
                    link(dve.tensor_tensor(xc[:, :, :], src, bc(st[:, 1, :], C), ALU.add))
                if step == 2:
                    link(dve.tensor_tensor(tmp[:, :, :], xc[:, :, :], xc[:, :, :], ALU.mult))
                if step == 3:
                    link(dve.tensor_reduce(st[:, 6, :], tmp[:, :, :], X, ALU.add))
                if step == 4:
                    dve.tensor_scalar(st[:, 2, :], st[:, 6, :], 1.0 / C, LN_EPS, ALU.mult, ALU.add)\
                       .then_inc(stat_in.sem, 1)

            def center(link, b, k, src):
                for step in range(5):
                    center_step(link, src, step)
                dve.wait_ge(*rstd_out(b, k + 1))

            def scale_xn(link, b):
                dve.wait_ge(*rstd_out(b, 1))
                dve.tensor_tensor(xn[:, :, :], xc[:, :, :], bc(st[:, 3, :], C), ALU.mult).then_inc(xn_ready.sem, 1)
                link(dve.tensor_tensor(st[:, 1, :], st[:, 3, :], st[:, 3, :], ALU.mult))
                link(dve.scalar_tensor_tensor(st[:, 7, :], st[:, 6, :], 1.0 / C, st[:, 1, :], ALU.mult, ALU.mult))
                dve.tensor_scalar(st[:, 4, :], st[:, 7, :], LN_EPS, None, ALU.add).then_inc(stat_in.sem, 1)

            def scale_xa(b):
                dve.wait_ge(*rstd_out(b, 2))
                dve.wait_ge(*xn_ready(b, 1))
                dve.tensor_tensor(xa[:, :, :], xn[:, :, :], bc(st[:, 5, :], C), ALU.mult).then_inc(xn_ready.sem, 1)

            dve.wait_ge(*x_in(0, 16))
            center(slink, 0, 0, xs[:, :, :])
            scale_xn(slink, 0)
            scale_xa(0)
            setup_steps = own[0]

            with dve.Fori(0, NB) as b:
                own[0] = 0

                def link(ins):
                    own[0] += 1
                    ins.then_inc(v_own, 1)
                    dve.wait_ge(v_own, b * V_STEPS + (setup_steps + own[0]))

                def full(name):
                    dve.wait_ge(*filled(b, JOB[name] + 1))

                full("qa")
                for j in range(HH):
                    ins = dve.tensor_scalar(qam[:, T // 2:T, j, :], jtiles("qa")[:, T // 2:T, :],
                                            hmask_s[:, j:j + 1], bqa_m[:, j:j + 1], ALU.mult, ALU.add)
                ins.then_inc(masked_q.sem, 1)
                full("ka")
                dve.tensor_scalar(kaT[:, :], jflat("ka"), vec[:, V_BKA:V_BKA + 1], None, ALU.add)\
                   .then_inc(by_v.sem, 1)
                for k, (pos_part, ee, ff) in enumerate(((z3, z2, kf), (z1, z0, qf))):
                    if k:
                        full("xnT")
                        dve.tensor_copy(xnT[:, :], jflat("xnT")).then_inc(by_v.sem, 1)
                    dve.wait_ge(*feat_exp(b, k + 1))
                    dve.scalar_tensor_tensor(ff[:, :], ee[:, :], 0.0001, pos_part[:, :], ALU.add, ALU.add)\
                       .then_inc(feat.sem, 1)
                for k in range(2):
                    full(f"v{k}")
                    dve.tensor_tensor(val[:, 4 * k:4 * k + 4, :],
                                      jflat(f"v{k}").rearrange("p (t n) -> p t n", n=2 * C),
                                      bcm(row[:, R_BV:R_BV + 2 * C], 4), ALU.add).then_inc(by_v.sem, 1)
                def beside_window(s):
                    if s == 4:
                        full("kv")
                        dve.tensor_tensor(tmp[:, 0:T - 1, :], jtiles("kv")[:, 0:T - 1, :],
                                          bcm(cst[:, C_BLK:C_BLK + P], T - 1), ALU.mult).then_inc(by_v.sem, 1)
                    if s == 5:
                        drained(dve, b, "kv")
                        link(dve.tensor_copy(state[:, 1, :], tmp[:, 0, :]))
                    n = s - 4
                    if 2 <= n < T:
                        if n > 2:
                            dve.wait_ge(*state_step(b, n - 2))
                        dve.tensor_tensor(state[:, n, :], state[:, n - 1, :], tmp[:, n - 1, :], ALU.add)\
                           .then_inc(state_step.sem, 1)
                    if s == T + 4:
                        dve.wait_ge(*feat(b, 2))
                        link(dve.tensor_tensor_scan(z0[:, :], kf[:, :], kf[:, :], 0.0, ALU.add, ALU.bypass))
                    if s == T + 5:
                        dve.tensor_tensor(z2[:, :], z0[:, :], qf[:, :], ALU.mult).then_inc(feat.sem, 1)

                def scores_there(s):
                    dve.wait_ge(*win_scores(b, s + 1))

                def win_front(s):
                    n = s // 4
                    S = pair[s % 2][:, :, :].rearrange("p a n -> p (a n)").rearrange("p (j k) -> p j k", j=GH)
                    if s < 4:
                        scores_there(s)
                        own[0] += 1
                        dve.memset(poke[:, s:s + 1], 0.0).then_inc(v_own, 1)
                    before = S[:, :, 0:P] if n else bcm(neg[:, :], GH)
                    link(dve.copy_predicated(S[:, :, P:2 * P], bcm(cst[:, C_JGT:C_JGT + P].bitcast(I32), GH), before))
                    dve.tensor_reduce(nmx[:, s % 4, :], S[:, :, P:2 * P], X, ALU.max, negate=True)\
                       .then_inc(win_max.sem, 1)

                def win_recip(s):
                    dve.wait_ge(*win_exp(b, s + 1))
                    dve.reciprocal(rdn[:, s % 4, :], den[:, s % 4, :]).then_inc(win_rden.sem, 1)

                def win_mask(s):
                    dve.wait_ge(*win_pc(b, s + 1))
                    if s >= 3:
                        dve.wait_ge(*win_pv(b, s - 2))
                    if s + 4 < 4 * T:
                        scores_there(s + 4)
                    dve.tensor_tensor(ptc[s % 3][:, :, :], ptp[s % 3][:, :, :], bcm(cst[:, C_KLE:C_KLE + P], GH),
                                      ALU.mult).then_inc(win_pt.sem, 1)

                def pick(n):
                    link(dve.tensor_tensor(ext[:, :, :], bank(6 + n % 2).rearrange("p (j r) -> p j r", j=GH),
                                           bc(gmask, P), ALU.mult))
                    return ext[:, :, :].rearrange("p j r -> p r j")

                def win_extract(n):
                    dve.wait_ge(*win_pv(b, 4 * n + 4))
                    dve.tensor_reduce(winT[:, n * P:(n + 1) * P], pick(n), X, ALU.add).then_inc(win_out.sem, 1)

                for s in range(4 * T + 6):
                    if 4 <= s < 4 * T + 4:
                        win_mask(s - 4)
                    if s < 4 * T:
                        win_front(s)
                    if 1 <= s <= 4 * T:
                        win_recip(s - 1)
                    if s >= 9 and s % 4 == 1:
                        win_extract(s // 4 - 2)
                    beside_window(s)

                def lin_evac(s):
                    dve.wait_ge(*lin_a(b, s + 1))
                    if s >= 3:
                        dve.wait_ge(*lin_pv(b, s - 2))
                    dve.tensor_tensor(am[s % 3][:, :, :], bank(s % 4).rearrange("p (j r) -> p j r", j=GH),
                                      bcm(cst[:, C_KLE:C_KLE + P], GH), ALU.mult).then_inc(lin_am.sem, 1)

                def lin_extract(n):
                    at = slice(n * P, (n + 1) * P)
                    dve.wait_ge(*lin_pv(b, 4 * n + 4))
                    link(dve.tensor_reduce(red[:, :], pick(n), X, ALU.add))
                    src = red
                    if n:
                        link(dve.tensor_tensor(red2[:, :], red[:, :], interT[:, at], ALU.add))
                        src = red2
                    dve.tensor_tensor(linT[:, at], src[:, :], rdenT[:, at], ALU.mult).then_inc(lin_out.sem, 1)

                full("den")
                dve.tensor_scalar(z1[:, :], jflat("den"), 1e-6, None, ALU.add).then_inc(by_v.sem, 1)
                for s in range(4 * T + 3):
                    if s < 4 * T:
                        lin_evac(s)
                    if s == 9:
                        drained(dve, b, "inter")
                    if s % 4 == 1 and s // 4 < T:
                        at = slice(s // 4 * P, (s // 4 + 1) * P)
                        if s == 1:
                            drained(dve, b, "den")
                        own[0] += 1
                        dve.reciprocal(rdenT[:, at], z1[:, at]).then_inc(v_own, 1)
                    if s >= 6 and s % 4 == 2 and s // 4 - 1 < T:
                        lin_extract(s // 4 - 1)
                    if s == 10:
                        dve.wait_ge(*fc_gelu(b, T))
                        dve.tensor_scalar(hst[:, 1, :], hst[:, 0, :], -1.0 / FF, None, ALU.mult)\
                           .then_inc(hid_mean.sem, 1)
                    if s == 24:
                        dve.wait_ge(*hid_sq(b, 1))
                        dve.tensor_scalar(hst[:, 3, :], hst[:, 2, :], 1.0 / FF, LN_EPS, ALU.mult, ALU.add)\
                           .then_inc(stat_in.sem, 1)
                    if s == 27:
                        dve.wait_ge(*rstd_out(b, 3))
                    if 27 <= s < 27 + T:
                        t = s - 27
                        dve.tensor_scalar(hid[:, t, :], hid[:, t, :], hst[:, 1, t:t + 1], hst[:, 4, t:t + 1],
                                          ALU.add, ALU.mult).then_inc(hid_norm.sem, 1)

                full("mixed")
                dve.wait_ge(*xb_ready(b, 1))
                dve.tensor_tensor(s0[:, :, :], jtiles("mixed"), xa[:, :, :], ALU.add).then_inc(by_v.sem, 1)
                drained(dve, b, "mixed")
                center(link, b, 3, s0[:, :, :])
                dve.tensor_tensor(xa[:, :, :], xc[:, :, :], bc(st[:, 3, :], C), ALU.mult).then_inc(xn_ready.sem, 1)
                link(dve.tensor_tensor(s0[:, :, :], s0[:, :, :], bcm(row[:, R_B2:R_B2 + C], T), ALU.add))
                drained(dve, b, "ffn")
                link(dve.tensor_tensor(tmp[:, :, :], s0[:, :, :], gate[:, :, :], ALU.mult))
                link(dve.tensor_tensor(s0[:, :, :], tmp[:, :, :], xs[:, :, :], ALU.add))
                full("mlp")
                dve.tensor_tensor(tmp[:, :, :], jtiles("mlp"), gate[:, :, :], ALU.mult).then_inc(by_v.sem, 1)
                drained(dve, b, "mlp")
                link(dve.tensor_tensor(x1[:, :, :], tmp[:, :, :], s0[:, :, :], ALU.add))

                center(link, b, 4, x1[:, :, :])
                dve.tensor_tensor(xn[:, :, :], xc[:, :, :], bc(st[:, 3, :], C), ALU.mult).then_inc(xn_ready.sem, 1)
                dve.wait_ge(*xn_ready(b, 4))
                full("x1T")
                dve.tensor_copy(xnT[:, :], jflat("x1T")).then_inc(by_v.sem, 1)

                drained(dve, b, "x1T")
                dve.wait_ge(*x_hi_ready(b, 1))
                dve.tensor_tensor(x_lo, xnT[:, :], x_hi, ALU.subtract).then_inc(x_lo_ready.sem, 1)

                def gate_and_up():
                    full("xqT")
                    dve.tensor_copy(xaT[:, :], jflat("xqT")).then_inc(by_v.sem, 1)
                    for t in range(T):
                        dve.wait_ge(*up_done(b, t + 1))
                        dve.tensor_tensor(hh[:, t, :], jflat(f"gu_{t}")[:, 512:512 + FI], sg[:, t % 2, :],
                                          ALU.mult).then_inc(by_v.sem, 1)
                    drained(dve, b, f"gu_{T - 1}")

                def l_front(i, k):
                    q = ORDER[k]
                    dve.wait_ge(u_full, i * NU + USE[q] + 1)
                    dve.tensor_reduce(nm1[:, q:q + 1], used(q)[:, 0:(q + 1) * P], X, ALU.max, negate=True)\
                       .then_inc(l_max, 1)

                def l_normalize(i, k):
                    q, w = ORDER[k], (ORDER[k] + 1) * P
                    dve.wait_ge(u_free, i * NU + (NU + USE[q] + 1))
                    dve.reciprocal(rd1[:, q:q + 1], dn1[:, q:q + 1]).then_inc(l_own, 1)
                    dve.wait_ge(l_own, i * T + k + 1)
                    dve.tensor_scalar(pb[k % 4][:, 0:w], pb[k % 4][:, 0:w], rd1[:, q:q + 1], None, ALU.mult)\
                       .then_inc(l_norm, 1)

                def l_evac(i, k, first):
                    evacuate(dve, i, k, first)

                def y_rest(i):
                    dve.wait_ge(u_free, i * NU + (NU + USE["Y"] + 1))
                    dve.scalar_tensor_tensor(y_lo, used("Y"), L1_SCALE, y_hi, ALU.mult, ALU.subtract)\
                       .then_inc(y_lo_ready, 1)

                def beside_heads(s):
                    sc, rs = qsc[:, 0, :], qsc[:, 1, :]
                    for n, step in enumerate((2, 3, 8, 9)):
                        if s == step:
                            part = slice(2 * n * (FI // QB), 2 * (n + 1) * (FI // QB))
                            link(dve.tensor_reduce(sc[:, part], hh[:, 2 * n:2 * n + 2, :]
                                                   .rearrange("p t (n q) -> p (t n) q", q=QB), X, ALU.max,
                                                   apply_absolute_value=True))
                    if s == 10:
                        link(dve.tensor_scalar(sc, sc, 1.0 / 6.0, 1e-12, ALU.mult, ALU.max))
                        link(dve.reciprocal(rs, sc))
                        dve.tensor_scalar(sc, sc, 0.5, None, ALU.mult).then_inc(fscale.sem, 1)
                    if s == 11:
                        dve.wait_ge(*x_in(b + 1, 16))
                    for n, step in enumerate((11, 16, 17, 18, 19)):
                        if s == step:
                            center_step(link, xs[:, :, :], n)
                    if s == 24:
                        scale_xn(link, b + 1)
                    if s == 26:
                        scale_xa(b + 1)

                def l1_head(i, first, number=HEADS_PEELED):
                    if not first:
                        l_evac(i - 1, 5, False)
                    y_rest(i)
                    if not first:
                        l_evac(i - 1, 6, False)
                    for k in range(T):
                        l_front(i, k)
                        if first and k == 0:
                            dve.wait_ge(*fsign(b, 1))
                            fp4(link, xn[:, :, :].rearrange("p t c -> p (t c)"),
                                xa[:, :, :].rearrange("p t c -> p (t c)"), qs_[:, 0:L], L // QB)\
                                .then_inc(xn_ready.sem, 1)
                        if first and k == 1:
                            gate_and_up()
                        if k == FOLD_AT["G"]:
                            n = T_IDX["G"] + 2
                            dve.wait_ge(t_full, i * NT + n + 1)
                            dve.tensor_copy(G_hi[:, :], bank(4 + n % 2)[:, 0:P]).then_inc(g_hi_ready, 1)
                            dve.wait_ge(g_hi_ready, i + 2)
                            dve.tensor_tensor(G_lo[:, :], bank(4 + n % 2)[:, 0:P], G_hi[:, :], ALU.subtract)\
                               .then_inc(t_free_v, 1)
                        if k == FOLD_AT["B"]:
                            n = T_IDX["B"] + 2
                            dve.wait_ge(t_full, i * NT + n + 1)
                            dve.tensor_copy(Bv[:, :], bank(4 + n % 2)[:, 0:P]).then_inc(t_free_v, 1)
                        if k >= T_LAG:
                            l_evac(i, k - T_LAG, first)
                        if k:
                            l_normalize(i, k - 1)
                        elif not first:
                            l_normalize(i - 1, 7)
                            l_evac(i - 1, 7, False)
                        beside_heads(number * T + k)

                for k in range(HEADS_PEELED):
                    l1_head(b * H1 + k, k == 0, k)
                with dve.Fori(0, (H1 - HEADS_PEELED) // HEADS_UNROLLED) as h:
                    for k in range(HEADS_UNROLLED):
                        l1_head(b * H1 + h * HEADS_UNROLLED + (HEADS_PEELED + k), False)
                tail = (b + 1) * H1 - 1
                l_evac(tail, 5, False)
                l_evac(tail, 6, False)
                l_normalize(tail, 7)
                l_evac(tail, 7, False)
                dve.wait_ge(l_pv, (b + 1) * (H1 * NPV))
                dve.tensor_copy(s0[:, :, :], tiles(3)).then_inc(acc_out.sem, 1)

                drained(dve, b, "down")
                dve.wait_ge(*acc_out(b, 1))
                link(dve.tensor_tensor(tmp[:, :, :], s0[:, :, :], gate[:, :, :], ALU.mult))
                dve.tensor_tensor(x1[:, :, :], tmp[:, :, :], x1[:, :, :], ALU.add).then_inc(ready, 1)
                assert own[0] == V_STEPS, own[0]

        @block.tensor
        def _(pe):
            def mm(o, lhsT, rhs, start=True, stop=True, **kw):
                return pe.matmul(o, lhsT, rhs, start=start, stop=stop, **kw)

            pe.wait_ge(loaded, 16 * 9)
            pe.wait_ge(pool_const, 4)
            pe.wait_ge(set_v, 2)
            mm(bank(0)[:, 0:2], ones[:, :], rsum[:, :]).then_inc(set_pe, 1)
            pe.wait_ge(set_v, 19)
            for k in range(3):
                n = min(P, FI - k * P)
                pe.transpose(bank(2 + k)[:, 0:P], wnat[:, 0, k, :], ident)
                pe.transpose(bank(2 + k)[:, P:2 * P], wnat[:, 1, k, :], ident)
                pe.transpose(bank(2 + k)[0:n, 2 * P:3 * P], wdn[:, k * P:k * P + n], ident).then_inc(set_pe, 1)
            pe.wait_ge(set_a, 5)

            def fold(i, name):
                k = ("G", "B").index(name)
                if i is None:
                    pe.wait_ge(hw_in, 16)
                    slot = k
                else:
                    slot = T_IDX[name] % 2
                    tr_drained(pe, i, T_IDX[name] - 2, False)
                    pe.wait_ge(hw_in, i * 16 + 32)
                mm(bank(4 + slot)[:, 0:P], hw[:, 2 * k, :], hw[:, 2 * k + 1, :]).then_inc(t_full, 1)

            pe.wait_ge(set_v, 28)
            fold(None, "G")
            fold(None, "B")

            with pe.Fori(0, NB) as b:
                def begin(name):
                    k = before_on_pair(JOB[name])
                    if k is not None:
                        drained(pe, b, JOBS[k][0])

                def end(ins):
                    ins.then_inc(filled.sem, 1)

                def transpose_tiles(name, src):
                    begin(name)
                    for t in range(T):
                        ins = pe.transpose(jtiles(name)[:, t, :], src[:, t, :], ident)
                    end(ins)

                def wide(name, lhsT, rhs):
                    begin(name)
                    for a in range(2):
                        ins = mm(jflat(name)[:, a * 512:(a + 1) * 512], lhsT, rhs[:, a * 512:(a + 1) * 512])
                    end(ins)

                pe.wait_ge(*xn_ready(b, 2))
                transpose_tiles("xaT", xa)
                drained(pe, b, "xaT")
                wide("ks", wts[:, W_QKVS + C:W_QKVS + 2 * C], xaT)
                wide("qa", wts[:, W_QKVA:W_QKVA + C], xaT)
                wide("ka", wts[:, W_QKVA + C:W_QKVA + 2 * C], xaT)
                wide("qs", wts[:, W_QKVS:W_QKVS + C], xaT)
                transpose_tiles("xnT", xn)
                pe.wait_ge(*masked_q(b, 1))
                for k in range(2):
                    begin(f"v{k}")
                    for t in range(4 * k, 4 * k + 4):
                        for a, w in enumerate((W_QKVA, W_QKVS)):
                            at = (t % 4) * 2 * C + a * C
                            ins = mm(jflat(f"v{k}")[:, at:at + C], xaT[:, t * P:(t + 1) * P],
                                     wts[:, w + 2 * C:w + 3 * C])
                    end(ins)

                def chunk_products(s):
                    if s == 0:
                        begin("ktok")
                        pe.wait_ge(*feat(b, 1))
                        for t in range(T):
                            ins = pe.transpose(jtiles("ktok")[:, t, :], kf[:, t * P:(t + 1) * P], ident)
                        end(ins)
                    if s == 2:
                        begin("kv")
                        drained(pe, b, "ktok")
                        for n in range(T - 1):
                            ins = mm(jtiles("kv")[:, n, :], ktok[:, n, :], val[:, n, C:2 * C])
                        end(ins)

                for s in range(4 * T + 5):
                    if s < 2:
                        drained(pe, b, ("xnT", "qs")[s])
                    if s == 5:
                        drained(pe, b, "kv")
                    if s < 4 * T:
                        n, g = s // 4, s % 4
                        rows, j0 = slice(64 * (g // 2), 64 * (g // 2) + 64), GH * (g % 2)
                        if s >= 2:
                            pe.wait_ge(*win_exp(b, s - 1))
                        S = pair[s % 2][:, :, :].rearrange("p a n -> p (a n)").rearrange("p (j k) -> p j k", j=GH)
                        lo = (n - 1) * P if n else 0
                        for j in range(GH):
                            ins = mm(S[:, j, (0 if n else P):2 * P], qam[rows, n, j0 + j, :], kaT[rows, lo:(n + 1) * P])
                        ins.then_inc(win_scores.sem, 1)
                    chunk_products(s)
                    t = s - 3
                    if 0 <= t < 4 * T:
                        pe.wait_ge(*win_norm(b, t + 1))
                        if t >= 2:
                            pe.wait_ge(*win_pc(b, t - 1))
                        for j in range(GH):
                            ins = pe.transpose(bank(4 + t % 2)[:, j * P:(j + 1) * P], pr[t % 4][:, j, :], ident)
                        ins.then_inc(win_tr.sem, 1)
                    u = s - 5
                    if 0 <= u < 4 * T:
                        n, g = u // 4, u % 4
                        pe.wait_ge(*win_pt(b, u + 1))
                        if u == 4:
                            pe.wait_ge(*vdiff_ready(b, 1))
                        if g == 0 and n >= 2:
                            pe.wait_ge(*win_out(b, n - 1))
                        o = bank(6 + n % 2)[32 * g:32 * g + 32, :]
                        ch = slice(32 * g, 32 * g + 32)
                        own_part = ptc[u % 3][:, :, :].rearrange("p j r -> p (j r)")
                        whole = ptp[u % 3][:, :, :].rearrange("p j r -> p (j r)")
                        if n:
                            mm(o, vdiff[:, n, ch], own_part, stop=False)
                            ins = mm(o, val[:, n - 1, ch], whole, start=False)
                        else:
                            ins = mm(o, val[:, n, ch], own_part)
                        ins.then_inc(win_pv.sem, 1)

                pe.wait_ge(*feat(b, 3))
                pe.wait_ge(*win_exp(b, 4 * T))
                wide("den", cst[:, C_BLK:C_BLK + P], z2)
                pe.wait_ge(*win_out(b, T))
                begin("inter")
                pe.wait_ge(*state_step(b, T - 2))
                for n in range(1, T):
                    ins = mm(jtiles("inter")[:, n, :], state[:, n, :], qf[:, n * P:(n + 1) * P])
                end(ins)
                for s in range(4 * T + 2):
                    if s < 4 * T:
                        n, g = s // 4, s % 4
                        rows, j0 = slice(64 * (g // 2), 64 * (g // 2) + 64), GH * (g % 2)
                        if s >= 4:
                            pe.wait_ge(*lin_am(b, s - 3))
                        if g == 0:
                            pe.wait_ge(*qfm_ready(b, n + 1))
                        mm(bank(s % 4), kf[rows, n * P:(n + 1) * P],
                           qfm[n % 3][rows, j0:j0 + GH, :].rearrange("p j r -> p (j r)"))\
                            .then_inc(lin_a.sem, 1)
                    if s < T:
                        if s >= 2:
                            pe.wait_ge(*fc_gelu(b, s - 1))
                        elif s == 0:
                            drained(pe, b, "den")
                            drained(pe, b, "xnT")
                        mm(bank(4 + s % 2), xnT[:, s * P:(s + 1) * P], wfc).then_inc(fc_full.sem, 1)
                    u = s - 2
                    if 0 <= u:
                        n, g = u // 4, u % 4
                        pe.wait_ge(*lin_am(b, u + 1))
                        if g == 0 and n >= 2:
                            pe.wait_ge(*lin_out(b, n - 1))
                        elif u == 0:
                            drained(pe, b, "inter")
                        mm(bank(6 + n % 2)[32 * g:32 * g + 32, :], val[:, n, C + 32 * g:C + 32 * g + 32],
                           am[u % 3][:, :, :].rearrange("p j r -> p (j r)")).then_inc(lin_pv.sem, 1)

                pe.wait_ge(*lin_out(b, T))
                begin("sumT")
                for a in range(2):
                    at = slice(a * 512, (a + 1) * 512)
                    o = jflat("sumT")[:, at]
                    mm(o, wts[:, W_PA:W_PA + C], winT[:, at], stop=False)
                    ins = mm(o, wts[:, W_OS:W_OS + C], linT[:, at], start=False)
                end(ins)

                def transpose_hidden(f):
                    begin(f"fT_{f}")
                    for t in range(T):
                        ins = pe.transpose(jtiles(f"fT_{f}")[:, t, :], hid[:, t, f * P:(f + 1) * P], ident)
                    end(ins)

                pe.wait_ge(*hid_norm(b, T))
                transpose_hidden(0)
                begin("mixed")
                drained(pe, b, "sumT")
                for t in range(T):
                    ins = mm(jtiles("mixed")[:, t, :], sumT[:, t * P:(t + 1) * P], wts[:, W_O:W_O + C])
                end(ins)
                for f in range(1, FB):
                    transpose_hidden(f)
                begin("ffn")
                drained(pe, b, "fT_3")
                for t in range(T):
                    for f in range(FB):
                        ins = mm(jtiles("ffn")[:, t, :], hidT[:, f, t * P:(t + 1) * P], wproj[:, f, :],
                                 start=(f == 0), stop=(f == FB - 1))
                end(ins)
                pe.wait_ge(*xn_ready(b, 3))
                transpose_tiles("hT", xa)
                drained(pe, b, "hT")
                for f in range(FB):
                    wide(f"w1_{f}", wts[:, W_1 + f * P:W_1 + (f + 1) * P], xaT)
                begin("mlp")
                drained(pe, b, "w1_3")
                for t in range(T):
                    for f in range(FB):
                        ins = mm(jtiles("mlp")[:, t, :], h1T[:, f, t * P:(t + 1) * P],
                                 wts[:, W_2 + f * P:W_2 + (f + 1) * P], start=(f == 0), stop=(f == FB - 1))
                end(ins)
                pe.wait_ge(*xn_ready(b, 4))
                transpose_tiles("x1T", xn)
                pe.wait_ge(*x_lo_ready(b, 1))
                drained(pe, b, "mlp")
                drained(pe, b, "w1_1")

                def gate_and_up():
                    pe.wait_ge(*xn_ready(b, 5))
                    transpose_tiles("xqT", xa)
                    drained(pe, b, "xqT")
                    for t in range(T):
                        begin(f"gu_{t}")
                        for k in range(2):
                            ins = mm(jflat(f"gu_{t}")[:, k * 512:k * 512 + FI], xaT[:, t * P:(t + 1) * P],
                                     wgT[:, k, :])
                        end(ins)
                    drained(pe, b, f"gu_{T - 1}")

                def free(i, name):
                    pe.wait_ge(u_free, i * NU + (NU + USE_BEFORE[USE[name]] + 1))

                def three_passes(o, hi, lo, at):
                    mm(o, hi, x_hi[:, at], stop=False)
                    mm(o, hi, x_lo[:, at], start=False, stop=False)
                    return mm(o, lo, x_hi[:, at], start=False)

                def proj_y(i, first):
                    free(i, "Y")
                    if first:
                        pe.wait_ge(t_free_v, i * NTV + 2)
                    else:
                        tr_drained(pe, i - 1, T_IDX["G"], False)
                    for a in range(2):
                        at = slice(a * 512, (a + 1) * 512)
                        ins = three_passes(used("Y")[:, at], G_hi[:, :], G_lo[:, :], at)
                    ins.then_inc(u_full, 1)

                def proj_z(i, first):
                    free(i, "Z")
                    if not first:
                        tr_drained(pe, i - 1, T_IDX["B"], False)
                    for t in range(T):
                        at = slice(t * P, (t + 1) * P)
                        ins = mm(used("Z")[:, at], xnT[:, at], Bv[:, :])
                    ins.then_inc(u_full, 1)

                def scores(i, k):
                    q = ORDER[k]
                    free(i, q)
                    if k == 0:
                        pe.wait_ge(y_lo_ready, i + 1)
                    w = (q + 1) * P
                    S = used(q)
                    y = slice(q * P, w)
                    for at in range(0, w, 512):
                        to = max(min(w, at + 512), at + 256)
                        three_passes(S[:, at:to], y_hi[:, y], y_lo[:, y], slice(at, to))
                    mm(S[:, q * P:w], ident_b[:, :], causal_b[:, :], start=False, skip_group_check=True)\
                        .then_inc(u_full, 1)

                def transposes(i, k, first=False):
                    q = ORDER[k]
                    pe.wait_ge(l_norm, i * T + k + 1)
                    for g, js in enumerate(groups_of(q)):
                        ti = T_IDX[q, g] + 2
                        tr_drained(pe, i, T_IDX[q, g] - 2, first)
                        for n, j in enumerate(js):
                            ins = pe.transpose(bank(4 + ti % 2)[:, n * P:(n + 1) * P],
                                               pb[k % 4][:, j * P:(j + 1) * P], ident)
                        ins.then_inc(t_full, 1)

                def pv(i, k, first):
                    q = ORDER[k]
                    if k == 0:
                        pe.wait_ge(u_free, i * NU + (NU + USE["Z"] + 1))
                    clears = first and q == next(x for x in ORDER if x // 4 == q // 4)
                    for g, js in enumerate(groups_of(q)):
                        pi = PV_IDX[q, g]
                        tr_drained(pe, i, T_IDX[q, g], first)
                        for n, j in enumerate(js):
                            ins = mm(tiles(3)[:, q, :], pt[pi % NPT][:, n, :], Z[:, j, :],
                                     start=(clears and j == 0), skip_group_check=True)
                        ins.then_inc(l_pv, 1)

                def l1_head(i, first):
                    proj_y(i, first)
                    if not first:
                        transposes(i - 1, 5)
                        pv(i - 1, 4, False)
                        transposes(i - 1, 6)
                    scores(i, 0)
                    if not first:
                        pv(i - 1, 5, False)
                        transposes(i - 1, 7)
                    scores(i, 1)
                    if not first:
                        pv(i - 1, 6, False)
                        pv(i - 1, 7, False)
                    proj_z(i, first)
                    if first:
                        gate_and_up()
                    for k in range(2, T):
                        scores(i, k)
                        for name in ("G", "B"):
                            if k == FOLD_AT[name]:
                                fold(i, name)
                        if k >= T_LAG:
                            transposes(i, k - T_LAG, first)
                        if k >= PV_LAG:
                            pv(i, k - PV_LAG, first)

                for k in range(HEADS_PEELED):
                    l1_head(b * H1 + k, k == 0)
                with pe.Fori(0, (H1 - HEADS_PEELED) // HEADS_UNROLLED) as h:
                    for k in range(HEADS_UNROLLED):
                        l1_head(b * H1 + h * HEADS_UNROLLED + (HEADS_PEELED + k), False)
                tail = (b + 1) * H1 - 1
                transposes(tail, 5)
                pv(tail, 4, False)
                transposes(tail, 6)
                pv(tail, 5, False)
                transposes(tail, 7)
                pv(tail, 6, False)
                pv(tail, 7, False)

                pe.wait_ge(t_free_v, (b + 1) * (H1 * NTV) + 2)
                pe.wait_ge(*hq_ready(b, 1))
                for k in range(3):
                    n = min(P, FI - k * P)
                    begin(f"hqT_{k}")
                    for t in range(T):
                        ins = pe.transpose(jtiles(f"hqT_{k}")[0:n, t, :], hq[:, t, k * P:k * P + n], ident)
                    end(ins)
                begin("down")
                drained(pe, b, "hqT_2")
                pe.wait_ge(*acc_out(b, 1))
                for t in range(T):
                    for k in range(3):
                        n = min(P, FI - k * P)
                        ins = mm(jtiles("down")[:, t, :], hqT[0:n, k, t * P:(t + 1) * P], wdT[0:n, k, :],
                                 start=(k == 0), stop=(k == 2))
                end(ins)
                drained(pe, b, "down")


def kernel(**inputs):
    import concourse.bacc as bacc
    from concourse.bass_utils import run_bass_kernel_spmd

    a = {k.removeprefix("L"): np.asarray(v) for k, v in inputs.items()}
    heads = lambda w: w.reshape(H1, E1, C)
    hw = np.stack([heads(a["1_attn_wq"]), heads(a["1_attn_wk"]), heads(a["1_attn_wv"]),
                   heads(a["1_attn_wo"].T)], axis=2)
    hw = np.concatenate([hw, hw[0:2]])
    blocks = lambda w: w.reshape(FB, P, C).transpose(1, 0, 2).reshape(P, FB * C)
    wtab = np.concatenate([
        a["0_attn_Wqkv_a"], a["0_attn_Wqkv_s"], a["0_attn_Wp_a"], a["0_attn_Wo_s"], a["0_attn_Wo"],
        a["0_attn_W1"], blocks(a["0_attn_W2"]), a["0_ffn_W_fc"].T, blocks(a["0_ffn_W_proj"].T)], axis=1)
    ba, bs = a["0_attn_bqkv_a"], a["0_attn_bqkv_s"]
    vtab = np.stack([a["0_attn_g1"], a["0_attn_b1"], ba[0:C], ba[C:2 * C], bs[0:C], bs[C:2 * C],
                     a["0_attn_bp_a"], a["0_attn_bo_s"], a["0_attn_gm"], a["0_attn_bm"],
                     *a["0_attn_b1m"].reshape(FB, P), *a["0_ffn_ln_w"].reshape(FB, P),
                     *a["0_ffn_ln_b"].reshape(FB, P)], axis=1)
    rtab = np.concatenate([ba[2 * C:], bs[2 * C:], a["0_attn_bo"], a["0_attn_b2m"]])

    p, f = np.arange(P)[:, None], np.arange(P)[None, :]
    one = np.float32(1)
    ctab = np.concatenate([
        (p == f) * one, (p <= f) * one, (f > p) * one, (p // E0 == f // E0) * one,
        (f > p) * np.float32(NEG),
        (p % 64 // E0 == f[:, 0:HH]) * one, (p % 64 // E0 == f[:, 0:HH]) * np.float32(WIN_SCALE),
        (p % 32 // E0 == f[:, 0:GH]) * one],
        axis=1).astype(np.float32)
    arrays = {"x": a["0_attn_x"], "head_w": hw, "wtab": wtab, "vtab": vtab, "rtab": rtab, "ctab": ctab,
              "w_gate": a["1_ffn_w_gate"], "w_up": a["1_ffn_w_up"], "w_down": a["1_ffn_w_down"]}
    arrays = {k: np.ascontiguousarray(v) for k, v in arrays.items()}
    nc = bacc.Bacc("TRN2", target_bir_lowering=False, num_devices=1)
    args = [nc.dram_tensor(k, v.shape, mybir.dt.from_np(v.dtype), kind="ExternalInput").ap()
            for k, v in arrays.items()]
    args.append(nc.dram_tensor("out", (NB, L, C), F32, kind="ExternalOutput").ap())
    program(nc, *args)
    r = run_bass_kernel_spmd(nc, [arrays], core_ids=[0])
    return r.results[0]["out"]
```
